# Optimizing a Trainium2 kernel written in Bass

```python
import numpy as np
import jax
import jax.numpy as jnp

def _softmax(x, axis=-1):
    return jax.nn.softmax(x, axis=axis)

def _gelu(x):
    return jax.nn.gelu(x, approximate=True)

def _silu(x):
    return jax.nn.silu(x)

def _sigmoid(x):
    return jax.nn.sigmoid(x)

def _layernorm(x, axis=-1, eps=1e-05):
    m = jnp.mean(x, axis=axis, keepdims=True)
    v = jnp.var(x, axis=axis, keepdims=True)
    return (x - m) / jnp.sqrt(v + eps)

def _scatter_add(tgt, idx, src, axis=0):
    return tgt.at[idx].add(src)

def _segment_sum(src, seg, n):
    return jax.ops.segment_sum(src, seg, n)
kernel_name = 'mk_gnn_resnorm_d2_gnn_r8_7242fd'

def setup_inputs(seed: int=0):
    np.random.seed(seed)
    _w = jnp.asarray

    def _rec_inputs():
        import jax
        import jax.numpy as jnp
        _gk = jax.random.key(seed)
        x = -0.000202 + 1 * jax.random.normal(jax.random.fold_in(_gk, 1), (6250, 128), jnp.float32)
        _s = jax.random.randint(jax.random.fold_in(_gk, 2), (100000,), 0, 6250, jnp.int32)
        _d = jax.random.randint(jax.random.fold_in(_gk, 3), (100000,), 0, 6250, jnp.int32)
        _loop = jnp.arange(6250, dtype=jnp.int32)
        src = jnp.concatenate([_s, _d, _loop])
        dst = jnp.concatenate([_d, _s, _loop])
        _o = jnp.argsort(dst, stable=True)
        src = src[_o]
        dst = dst[_o]
        edge_attr_96 = 5.93493e-05 + 1.00006 * jax.random.normal(jax.random.fold_in(_gk, 12), (206250, 96), jnp.float32)
        return (x, src, dst, edge_attr_96)
    x, src, dst, edge_attr_96 = _rec_inputs()

    def _L0_gnn_setup():
        import jax, jax.numpy as jnp
        import numpy as np
        N = 6250
        E = 100000
        F = 128
        HID = 128
        LN_EPS = 1e-05
        NEG_SLOPE = 0.2

        def _gatv2(x, Wl, bl, Wr, br, att, bias, src, dst, heads, outc, concat):
            n = x.shape[0]
            xl = (x @ Wl + bl).reshape(n, heads, outc)
            e_feat = jax.nn.leaky_relu(xl[src] + (x @ Wr + br).reshape(n, heads, outc)[dst], NEG_SLOPE)
            logits = jnp.einsum('ehc,hc->eh', e_feat, att)
            m = jax.ops.segment_max(logits, dst, num_segments=n)
            a = jnp.exp(logits - m[dst])
            denom = jax.ops.segment_sum(a, dst, num_segments=n)
            a = a / denom[dst]
            out = jax.ops.segment_sum(xl[src] * a[:, :, None], dst, num_segments=n)
            out = out.reshape(n, heads * outc) if concat else out.mean(axis=1)
            return out + bias

        def _ln(h, g, b):
            mu = h.mean(-1, keepdims=True)
            var = ((h - mu) ** 2).mean(-1, keepdims=True)
            return (h - mu) * jax.lax.rsqrt(var + LN_EPS) * g + b
        key = jax.random.key(seed)
        ks = jax.random.split(key, 32)
        g = lambda k, shape, s=0.05: jax.random.normal(k, shape, dtype=jnp.float32) * s
        inp = {}
        inp['x'] = jax.random.normal(ks[0], (N, F), dtype=jnp.float32)
        inp['edge_index'] = jax.random.randint(ks[1], (2, E), 0, N)
        i = 2
        inp['W1l'] = g(ks[i], (F, HID))
        inp['b1l'] = jnp.zeros((HID,), jnp.float32)
        inp['W1r'] = g(ks[i + 1], (F, HID))
        inp['b1r'] = jnp.zeros((HID,), jnp.float32)
        inp['a1'] = g(ks[i + 2], (4, HID // 4))
        inp['c1'] = jnp.zeros((HID,), jnp.float32)
        inp['g1'] = jnp.ones((HID,), jnp.float32)
        inp['be1'] = jnp.zeros((HID,), jnp.float32)
        inp['W2l'] = g(ks[i + 3], (HID, HID))
        inp['b2l'] = jnp.zeros((HID,), jnp.float32)
        inp['W2r'] = g(ks[i + 4], (HID, HID))
        inp['b2r'] = jnp.zeros((HID,), jnp.float32)
        inp['a2'] = g(ks[i + 5], (4, HID // 4))
        inp['c2'] = jnp.zeros((HID,), jnp.float32)
        inp['g2'] = jnp.ones((HID,), jnp.float32)
        inp['be2'] = jnp.zeros((HID,), jnp.float32)
        inp['W3l'] = g(ks[i + 6], (HID, HID))
        inp['b3l'] = jnp.zeros((HID,), jnp.float32)
        inp['W3r'] = g(ks[i + 7], (HID, HID))
        inp['b3r'] = jnp.zeros((HID,), jnp.float32)
        inp['a3'] = g(ks[i + 8], (1, HID))
        inp['c3'] = jnp.zeros((HID,), jnp.float32)
        inp['g3'] = jnp.ones((HID,), jnp.float32)
        inp['be3'] = jnp.zeros((HID,), jnp.float32)
        return inp
    _L0_gnn_all = _L0_gnn_setup()
    _L0_gnn_in = {k: v for k, v in _L0_gnn_all.items() if k in ('W1l', 'b1l', 'W1r', 'b1r', 'a1', 'c1', 'g1', 'be1', 'W2l', 'b2l', 'W2r', 'b2r', 'a2', 'c2', 'g2', 'be2', 'W3l', 'b3l', 'W3r', 'b3r', 'a3', 'c3', 'g3', 'be3')}
    del _L0_gnn_all

    def _L1_gnn_setup():
        import jax, jax.numpy as jnp
        import numpy as np
        N_NODES = 6250
        N_EDGES = 100000
        D_NODE_IN, D_EDGE, D_GRAPH = (128, 96, 64)
        HIDDEN, D_NODE_OUT = (256, 128)
        NUM_GRAPHS = 64
        BN_EPS = 1e-05
        key = jax.random.key(seed)
        ks = jax.random.split(key, 10)
        d_in = D_NODE_IN + D_EDGE + D_GRAPH
        return {'x': jax.random.normal(ks[0], (N_NODES, D_NODE_IN), jnp.float32), 'edge_index': jax.random.randint(ks[1], (2, N_EDGES), 0, N_NODES, jnp.int64), 'edge_attr': jax.random.normal(ks[2], (N_EDGES, D_EDGE), jnp.float32), 'u': jax.random.normal(ks[3], (NUM_GRAPHS, D_GRAPH), jnp.float32), 'batch': jnp.sort(jax.random.randint(ks[4], (N_NODES,), 0, NUM_GRAPHS, jnp.int64)), 'W1': jax.random.normal(ks[5], (d_in, HIDDEN), jnp.float32) / np.sqrt(d_in), 'b1': jnp.zeros((HIDDEN,), jnp.float32), 'gamma': jnp.ones((HIDDEN,), jnp.float32), 'beta': jnp.zeros((HIDDEN,), jnp.float32), 'W2': jax.random.normal(ks[6], (HIDDEN, D_NODE_OUT), jnp.float32) / np.sqrt(HIDDEN), 'b2': jnp.zeros((D_NODE_OUT,), jnp.float32)}
    _L1_gnn_all = _L1_gnn_setup()
    _L1_gnn_in = {k: v for k, v in _L1_gnn_all.items() if k in ('u', 'W1', 'b1', 'gamma', 'beta', 'W2', 'b2')}
    del _L1_gnn_all
    return {'x': x, 'src': src, 'dst': dst, 'edge_attr_96': edge_attr_96, 'L0_gnn_W1l': _L0_gnn_in['W1l'], 'L0_gnn_b1l': _L0_gnn_in['b1l'], 'L0_gnn_W1r': _L0_gnn_in['W1r'], 'L0_gnn_b1r': _L0_gnn_in['b1r'], 'L0_gnn_a1': _L0_gnn_in['a1'], 'L0_gnn_c1': _L0_gnn_in['c1'], 'L0_gnn_g1': _L0_gnn_in['g1'], 'L0_gnn_be1': _L0_gnn_in['be1'], 'L0_gnn_W2l': _L0_gnn_in['W2l'], 'L0_gnn_b2l': _L0_gnn_in['b2l'], 'L0_gnn_W2r': _L0_gnn_in['W2r'], 'L0_gnn_b2r': _L0_gnn_in['b2r'], 'L0_gnn_a2': _L0_gnn_in['a2'], 'L0_gnn_c2': _L0_gnn_in['c2'], 'L0_gnn_g2': _L0_gnn_in['g2'], 'L0_gnn_be2': _L0_gnn_in['be2'], 'L0_gnn_W3l': _L0_gnn_in['W3l'], 'L0_gnn_b3l': _L0_gnn_in['b3l'], 'L0_gnn_W3r': _L0_gnn_in['W3r'], 'L0_gnn_b3r': _L0_gnn_in['b3r'], 'L0_gnn_a3': _L0_gnn_in['a3'], 'L0_gnn_c3': _L0_gnn_in['c3'], 'L0_gnn_g3': _L0_gnn_in['g3'], 'L0_gnn_be3': _L0_gnn_in['be3'], 'L1_gnn_u': _L1_gnn_in['u'], 'L1_gnn_W1': _L1_gnn_in['W1'], 'L1_gnn_b1': _L1_gnn_in['b1'], 'L1_gnn_gamma': _L1_gnn_in['gamma'], 'L1_gnn_beta': _L1_gnn_in['beta'], 'L1_gnn_W2': _L1_gnn_in['W2'], 'L1_gnn_b2': _L1_gnn_in['b2']}

def reference(x, src, dst, edge_attr_96, L0_gnn_W1l, L0_gnn_b1l, L0_gnn_W1r, L0_gnn_b1r, L0_gnn_a1, L0_gnn_c1, L0_gnn_g1, L0_gnn_be1, L0_gnn_W2l, L0_gnn_b2l, L0_gnn_W2r, L0_gnn_b2r, L0_gnn_a2, L0_gnn_c2, L0_gnn_g2, L0_gnn_be2, L0_gnn_W3l, L0_gnn_b3l, L0_gnn_W3r, L0_gnn_b3r, L0_gnn_a3, L0_gnn_c3, L0_gnn_g3, L0_gnn_be3, L1_gnn_u, L1_gnn_W1, L1_gnn_b1, L1_gnn_gamma, L1_gnn_beta, L1_gnn_W2, L1_gnn_b2):
    import jax
    import jax.numpy as jnp

    def _L0_gnn_ref(x, edge_index, W1l, b1l, W1r, b1r, a1, c1, g1, be1, W2l, b2l, W2r, b2r, a2, c2, g2, be2, W3l, b3l, W3r, b3r, a3, c3, g3, be3):
        import jax, jax.numpy as jnp
        import numpy as np
        N = 6250
        E = 100000
        F = 128
        HID = 128
        LN_EPS = 1e-05
        NEG_SLOPE = 0.2

        def _gatv2(x, Wl, bl, Wr, br, att, bias, src, dst, heads, outc, concat):
            n = x.shape[0]
            xl = (x @ Wl + bl).reshape(n, heads, outc)
            e_feat = jax.nn.leaky_relu(xl[src] + (x @ Wr + br).reshape(n, heads, outc)[dst], NEG_SLOPE)
            logits = jnp.einsum('ehc,hc->eh', e_feat, att)
            m = jax.ops.segment_max(logits, dst, num_segments=n)
            a = jnp.exp(logits - m[dst])
            denom = jax.ops.segment_sum(a, dst, num_segments=n)
            a = a / denom[dst]
            out = jax.ops.segment_sum(xl[src] * a[:, :, None], dst, num_segments=n)
            out = out.reshape(n, heads * outc) if concat else out.mean(axis=1)
            return out + bias

        def _ln(h, g, b):
            mu = h.mean(-1, keepdims=True)
            var = ((h - mu) ** 2).mean(-1, keepdims=True)
            return (h - mu) * jax.lax.rsqrt(var + LN_EPS) * g + b
        n = x.shape[0]
        loops = jnp.arange(n, dtype=edge_index.dtype)
        src = jnp.concatenate([edge_index[0], loops])
        dst = jnp.concatenate([edge_index[1], loops])
        h = _gatv2(x, W1l, b1l, W1r, b1r, a1, c1, src, dst, 4, HID // 4, True)
        h = jax.nn.relu(_ln(h, g1, be1))
        h = _gatv2(h, W2l, b2l, W2r, b2r, a2, c2, src, dst, 4, HID // 4, True)
        h = jax.nn.relu(_ln(h, g2, be2))
        h = _gatv2(h, W3l, b3l, W3r, b3r, a3, c3, src, dst, 1, HID, False)
        h = jax.nn.relu(_ln(h, g3, be3))
        return h

    def _L1_gnn_ref(x, edge_index, edge_attr, u, batch, W1, b1, gamma, beta, W2, b2):
        import jax, jax.numpy as jnp
        import numpy as np
        N_NODES = 6250
        N_EDGES = 100000
        D_NODE_IN, D_EDGE, D_GRAPH = (128, 96, 64)
        HIDDEN, D_NODE_OUT = (256, 128)
        NUM_GRAPHS = 64
        BN_EPS = 1e-05
        col = edge_index[1]
        n = x.shape[0]
        sums = jax.ops.segment_sum(edge_attr, col, num_segments=n)
        cnt = jax.ops.segment_sum(jnp.ones((edge_attr.shape[0], 1), edge_attr.dtype), col, num_segments=n)
        e_aggr = sums / jnp.maximum(cnt, 1.0)
        h = jnp.concatenate([x, e_aggr, u[batch]], axis=1)
        h = h @ W1 + b1
        mu = jnp.mean(h, axis=0)
        var = jnp.mean((h - mu) ** 2, axis=0)
        h = (h - mu) * jax.lax.rsqrt(var + BN_EPS) * gamma + beta
        h = jax.nn.relu(h)
        return h @ W2 + b2
    edge_index = jnp.stack([src, dst])
    batch0 = jnp.zeros((6250,), jnp.int32)
    x = _layernorm(x + _L0_gnn_ref(x, edge_index, L0_gnn_W1l, L0_gnn_b1l, L0_gnn_W1r, L0_gnn_b1r, L0_gnn_a1, L0_gnn_c1, L0_gnn_g1, L0_gnn_be1, L0_gnn_W2l, L0_gnn_b2l, L0_gnn_W2r, L0_gnn_b2r, L0_gnn_a2, L0_gnn_c2, L0_gnn_g2, L0_gnn_be2, L0_gnn_W3l, L0_gnn_b3l, L0_gnn_W3r, L0_gnn_b3r, L0_gnn_a3, L0_gnn_c3, L0_gnn_g3, L0_gnn_be3), axis=-1)
    x = _layernorm(x + _L1_gnn_ref(x, edge_index, edge_attr_96, L1_gnn_u, batch0, L1_gnn_W1, L1_gnn_b1, L1_gnn_gamma, L1_gnn_beta, L1_gnn_W2, L1_gnn_b2), axis=-1)
    return x

_drawn_inputs = setup_inputs


def setup_inputs(seed=0):
    import zlib

    import numpy as np

    out = dict(_drawn_inputs(seed))
    spreads = {'L0_gnn_b1l': (0.0, 0.1),
     'L0_gnn_b1r': (0.0, 2.0),
     'L0_gnn_c1': (0.0, 0.1),
     'L0_gnn_g1': (1.0, 0.2),
     'L0_gnn_be1': (0.0, 0.1),
     'L0_gnn_b2l': (0.0, 0.1),
     'L0_gnn_b2r': (0.0, 2.0),
     'L0_gnn_c2': (0.0, 0.1),
     'L0_gnn_g2': (1.0, 0.2),
     'L0_gnn_be2': (0.0, 0.1),
     'L0_gnn_b3l': (0.0, 0.1),
     'L0_gnn_b3r': (0.0, 2.0),
     'L0_gnn_c3': (0.0, 0.1),
     'L0_gnn_g3': (1.0, 0.2),
     'L0_gnn_be3': (0.0, 0.1),
     'L1_gnn_b1': (0.0, 2.0),
     'L1_gnn_gamma': (1.0, 0.2),
     'L1_gnn_beta': (0.0, 0.1),
     'L1_gnn_b2': (0.0, 0.1)}
    factors = {'L0_gnn_W1r': 64.0,
     'L0_gnn_W2r': 41.587,
     'L0_gnn_a2': 23.118,
     'L0_gnn_W3r': 64.0,
     'L0_gnn_a3': 64.0,
     'L1_gnn_u': 64.0}
    for name, (base, spread) in spreads.items():
        noise = np.random.default_rng([zlib.crc32(name.encode()), seed]).standard_normal(out[name].shape)
        drawn = base * np.exp(spread * noise) if base else spread * noise
        out[name] = jnp.asarray(drawn.astype(out[name].dtype))
    for name, factor in factors.items():
        out[name] = (out[name] * factor).astype(out[name].dtype)
    return out
```

```python
import concourse.bass as bass
from concourse import mybir
from contextlib import ExitStack

F32 = mybir.dt.float32
I32 = mybir.dt.int32
ALU = mybir.AluOpType
ACT = mybir.ActivationFunctionType
AX = mybir.AxisListType

P = 128
N_NODES = 6250
N_EDGES = 206250
F = 128
HEADS = 4
D_EDGE = 96
D_GRAPH = 64
HIDDEN = 256
N_GRAPHS = 64
LAYERS = 3
EPS = 1e-5
SLOPE = 0.2
BIG = 1e30

TILES = 26
CHUNK = TILES * P
N_CHUNKS = -(-N_EDGES // CHUNK)
E_PAD = N_CHUNKS * CHUNK
NO_NODE = 100000
GROUPS = [range(a, min(a + 4, TILES)) for a in range(0, TILES, 4)]
NG = len(GROUPS)
LH = TILES * HEADS

NB = 5
NROWS = NB * P
ROUNDS = -(-(N_NODES + P) // NROWS)
N_PAD = ROUNDS * NROWS
EMPTY_BASE = N_PAD - P
LAST_P = (N_NODES - (ROUNDS - 1) * NROWS) // NB
assert LAST_P * NB == N_NODES - (ROUNDS - 1) * NROWS

MAX_ITEMS = N_CHUNKS + N_NODES // P
MAX_ITEMS += MAX_ITEMS % 2
MIN_PAIRS, MAX_PAIRS = N_CHUNKS // 2, MAX_ITEMS // 2
assert N_CHUNKS % 2 == 0

C_ACC, C_DEN, C_CNT, C_EA = HEADS, HEADS + F, 2 * HEADS + F, 2 * HEADS + F + 1
ROW_L = C_CNT
ROW = C_EA + D_EDGE
MSG = F + HEADS + 1

ITEM_DMAS = 6 + HEADS
SETUP_ROW_STEPS = 8
NODE_STEPS = [4, 16, 17, 22]
OUT_STEPS = 9


def gnn_program(nc, x, src, dst, dst_rows, edge_attr, node_id, Wl, bl, Wr, br, att, c, g, be,
                u, W1, b1, gamma, beta, W2, b2, out):
    ctx = ExitStack()
    with ctx:
        def sb(name, shape, dt=F32):
            return ctx.enter_context(nc.sbuf_tensor(name, shape, dt))

        def sem(name):
            return ctx.enter_context(nc.semaphore(name))

        def sems(name, n):
            return [sem(f"{name}{i}") for i in range(n)]

        def scratch(name, shape, dt=F32):
            return nc.dram_tensor(name, shape, dt, kind="Internal").ap()

        xl_tab = scratch("xl_tab", (N_PAD, F))
        xr_tab = scratch("xr_tab", (N_PAD, F))
        state = scratch("state", (N_PAD, ROW))
        item_tab = scratch("item_tab", (MAX_ITEMS, 2), I32)

        ident = sb("ident", [P, P])
        ones = sb("ones", [1, P])
        w_lr = sb("w_lr", [P, LAYERS, 2 * F])
        b_lr = sb("b_lr", [P, LAYERS, 2 * F])
        att_b = sb("att_b", [P, LAYERS, F])
        c_b = sb("c_b", [P, LAYERS, F])
        g_b = sb("g_b", [P, LAYERS, F])
        be_b = sb("be_b", [P, LAYERS, F])
        w1_x = sb("w1_x", [P, HIDDEN])
        w1_e = sb("w1_e", [D_EDGE, HIDDEN])
        w1_u = sb("w1_u", [D_GRAPH, HIDDEN])
        u_col = sb("u_col", [D_GRAPH, 1])
        w2_s = sb("w2_s", [P, 2, F])
        b2_b = sb("b2_b", [P, F])
        cols1 = sb("cols1", [P, 3, 2])

        lohi = sb("lohi", [1, 2, N_CHUNKS], I32)
        span = sb("span", [1, N_CHUNKS], I32)
        nwin = sb("nwin", [1, N_CHUNKS])
        zero_row = sb("zero_row", [1, N_CHUNKS])
        tab_row = sb("tab_row", [1, 2, N_CHUNKS])
        lo_f = sb("lo_f", [1, N_CHUNKS])
        pairs_f = sb("pairs_f", [1, 1])
        pairs_i = sb("pairs_i", [1, 3], I32)
        k_col = sb("k_col", [P, 1])
        past = sb("past", [P, N_CHUNKS + 1])
        own = sb("own", [P, N_CHUNKS])
        item_f = sb("item_f", [P, 4])
        item_i = sb("item_i", [P, 2], I32)
        tab = sb("tab", [1, MAX_ITEMS * 2], I32)

        idx = sb("idx", [P, 2, TILES], I32)
        dst_e = sb("dst_e", [P, 2, TILES], I32)
        dst_next = sb("dst_next", [P, 2, TILES], I32)
        dst_r = sb("dst_r", [LH, 2, P], I32)
        dst_b = sb("dst_b", [P, 2, CHUNK], I32)
        node_col = sb("node_col", [P, 2, 1])
        node_row = sb("node_row", [P, 2, P])
        xr_w = sb("xr_w", [P, 2, F])
        xl_g = sb("xl_g", [P, 2, TILES, F])
        ea = sb("ea", [P, 2, TILES, D_EDGE])
        st_old = sb("st_old", [P, 2, ROW])
        st_new = sb("st_new", [P, 2, ROW])
        onehot = sb("onehot", [P, 2, TILES, P])
        S = onehot[:, 0, :, :]
        ST = onehot[:, 1, :, :]
        z = sb("z", [P, 2, 4, F])
        lk = sb("lk", [P, 2, 4, F])
        am = sb("am", [P, 2, 4, F])
        logit = sb("logit", [P, LH])
        logit_s = sb("logit_s", [P, TILES])
        logit_m = sb("logit_m", [P, LH])
        in_lo = sb("in_lo", [P, TILES])
        in_win = sb("in_win", [P, TILES])
        out_pen = sb("out_pen", [P, TILES])
        not_last = sb("not_last", [P, TILES])
        row_eq = sb("row_eq", [LH, P])
        row_pen = sb("row_pen", [LH, P])
        run_max = sb("run_max", [LH, P])
        ends = sb("ends", [P, TILES, HEADS + 1])
        no_run = sb("no_run", [P, TILES])
        cand = sb("cand", [P, TILES, HEADS])
        chunk_max = sb("chunk_max", [P, HEADS])
        dmax = sb("dmax", [P, HEADS])
        rescale = sb("rescale", [P, HEADS])
        shifted = sb("shifted", [P, LH])
        msg = sb("msg", [P, TILES, MSG])

        n_st = sb("n_st", [P, NB, ROW])
        n_new = sb("n_new", [P, NB, ROW])
        n_x = sb("n_x", [P, NB, F])
        n_h = sb("n_h", [P, NB, F])
        n_d = sb("n_d", [P, NB, F])
        n_t = sb("n_t", [P, NB, F])
        n_lr = sb("n_lr", [P, NB, 2 * F])
        n_hT = sb("n_hT", [P, NROWS])
        n_eT = sb("n_eT", [D_EDGE, NROWS])
        n_rd = sb("n_rd", [P, NB, HEADS])
        n_c = sb("n_c", [P, 8, NB])
        n_e = sb("n_e", [P, NB, D_EDGE])
        x1 = onehot[:, :, :, :].rearrange("p a t n -> p (a t n)")[:, 0:ROUNDS * NB * F].rearrange("p (j f) -> p j f", f=F)
        hid = [xl_g[:, :, :, :].rearrange("p a t f -> p (a t f)")[:, 0:N_PAD],
               dst_b[:, :, :].rearrange("p a e -> p (a e)")[:, 0:N_PAD].bitcast(F32)]
        hid_relu = n_lr[:, :, :].rearrange("p j f -> p (j f)").rearrange("p (h e) -> p h e", h=2)
        squares = msg[:, :, :].rearrange("p t n -> p (t n)")
        bn = sb("bn", [P, 8, 2])
        bn_sum = sb("bn_sum", [P, 2, 4])

        PS = ctx.enter_context(nc.psum_tensor("PS", [P, 8, 512], F32))
        flat = PS[:, :, :].rearrange("p b n -> p (b n)")
        zp = [PS[:, 0, :], PS[:, 1, :]]
        lt_ps = PS[0:LH, 2, 0:P]
        rm_ps = PS[:, 2, 128:128 + LH]
        cm_ps = PS[:, 2, 232:232 + TILES * (HEADS + 1)]
        me_ps = PS[:, 2, 364:364 + LH]
        agg_ps = PS[:, 3, 0:MSG]
        ea_ps = PS[:, 4, 0:D_EDGE]
        hT_ps = flat[:, 0:NROWS]
        eT_ps = flat[0:D_EDGE, 1024:1024 + NROWS]
        lr_ps = flat[:, 5 * 512:5 * 512 + NB * 2 * F]
        out_ps = flat[:, 0:NROWS]

        consts_in = sem("consts_in")
        ident_zero = sem("ident_zero")
        ident_made = sem("ident_made")
        ones_made = sem("ones_made")
        lohi_in = sem("lohi_in")
        tab_bc = sem("tab_bc")
        table_made = sem("table_made")
        table_out = sem("table_out")
        table_in = sem("table_in")
        setup = sem("setup")
        rows_made = sem("rows_made")

        idx_loaded = sems("idx_loaded", 2)
        item_loaded = sems("item_loaded", 2)
        ea_loaded = sems("ea_loaded", 2)
        state_loaded = sems("state_loaded", 2)
        state_stored = sem("state_stored")
        gathered = [sems(f"gathered{q}_", NG) for q in range(2)]
        gather_go = sem("gather_go")
        flags_done = sems("flags_done", 6)
        onehot_done = sems("onehot_done", NG)
        expanded = sems("expanded", NG)
        z_done = sems("z_done", NG)
        leaky_done = sems("leaky_done", NG)
        mult_done = sems("mult_done", NG)
        logit_done = sem("logit_done")
        headsum_done = sem("headsum_done")
        headcopy_done = sem("headcopy_done")
        masked_done = sem("masked_done")
        logitT_done = sem("logitT_done")
        runmax_done = sem("runmax_done")
        runmaxT_done = sem("runmaxT_done")
        ends_done = sem("ends_done")
        cand_ps_done = sem("cand_ps_done")
        norun_done = sem("norun_done")
        cand_done = sem("cand_done")
        chunkmax_done = sem("chunkmax_done")
        newmax_done = sem("newmax_done")
        dmax_done = sem("dmax_done")
        rescale_done = sem("rescale_done")
        edgemax_done = sem("edgemax_done")
        shifted_done = sem("shifted_done")
        alpha_done = sem("alpha_done")
        msg_done = sems("msg_done", NG)
        agg_done = sem("agg_done")
        scaled_done = sem("scaled_done")
        item_done = sem("item_done")

        x_loaded = sem("x_loaded")
        st_loaded = sem("st_loaded")
        hid_in = sem("hid_in")
        x1_ready = sem("x1_ready")
        x1_var = sem("x1_var")
        x1_std = sem("x1_std")
        out_read = sem("out_read")
        n_stored = sem("n_stored")
        n_step = sems("n_step", LAYERS + 1)
        n_var = sem("n_var")
        n_std = sem("n_std")
        n_ready = sem("n_ready")
        n_T = sem("n_T")
        n_Tc = sem("n_Tc")
        n_prod = sem("n_prod")
        n_made = sem("n_made")
        o_step = sems("o_step", 3)
        e_ready = sem("e_ready")
        e_T = sem("e_T")
        e_Tc = sem("e_Tc")
        hid_ps = sem("hid_ps")
        hid_bias = sem("hid_bias")
        hid_done = sem("hid_done")
        hid_b = sem("hid_b")
        mu_done = sem("mu_done")
        sq_done = sem("sq_done")
        bn_var = sem("bn_var")
        bn_std = sem("bn_std")
        bn_done = sem("bn_done")
        act_done = sem("act_done")
        out_mm = sem("out_mm")
        out_var = sem("out_var")
        out_std = sem("out_std")
        out_made = sem("out_made")
        out_stored = sem("out_stored")
        end_mark = sem("end_mark")


        block = ctx.enter_context(nc.Block())

        NODE_STORES = 3
        CONST_DMAS = 8 * LAYERS + 9
        stored_value = 16 * NODE_STORES

        def rounds_of(ap, r):
            return ap[bass.ds(r * NROWS, NROWS), :].rearrange("(p j) f -> p j f", j=NB)

        def over_blocks(ap):
            return ap.unsqueeze(1).to_broadcast([P, NB, ap.shape[1]])

        def over_features(ap, n=F):
            return ap.unsqueeze(2).to_broadcast([P, NB, n])

        def by_tile(ap):
            return ap.rearrange("p (h t) -> p t h", h=HEADS)

        class Chain:

            def __init__(self, eng, step_sem, base=0):
                self.eng, self.sem, self.base, self.n = eng, step_sem, base, 0

            def did(self, instruction):
                instruction.then_inc(self.sem, 1)
                self.n += 1
                return self.n

            def link(self, instruction):
                n = self.did(instruction)
                self.eng.wait_ge(self.sem, self.base + n)

        @block.sync
        def _(sp):
            sp.sem_inc(n_stored, stored_value)
            sp.sem_inc(out_stored, 16)
            for l in range(LAYERS):
                for h, (w, b) in enumerate(((Wl, bl), (Wr, br))):
                    sp.dma_start(w_lr[:, l, h * F:(h + 1) * F], w[l]).then_inc(consts_in, 16)
                    sp.dma_start(b_lr[:, l, h * F:(h + 1) * F], b[l].partition_broadcast(P)).then_inc(consts_in, 16)
                sp.dma_start(att_b[:, l, :], att[l].rearrange("h f -> (h f)").partition_broadcast(P)).then_inc(consts_in, 16)
                for t, v in ((c_b, c), (g_b, g), (be_b, be)):
                    sp.dma_start(t[:, l, :], v[l].partition_broadcast(P)).then_inc(consts_in, 16)
            sp.dma_start(w1_x[:, :], W1[0:F, :]).then_inc(consts_in, 16)
            sp.dma_start(w1_e[:, :], W1[F:F + D_EDGE, :]).then_inc(consts_in, 16)
            sp.dma_start(w1_u[:, :], W1[F + D_EDGE:F + D_EDGE + D_GRAPH, :]).then_inc(consts_in, 16)
            with nc.allow_non_contiguous_dma(reason="a few columns"):
                sp.dma_start(u_col[:, :], u[0:1, :].rearrange("a d -> d a")).then_inc(consts_in, 16)
                for i, v in enumerate((b1, gamma, beta)):
                    sp.dma_start(cols1[:, i, :], v.rearrange("(h p) -> p h", p=P)).then_inc(consts_in, 16)
                sp.dma_start(lohi[:, 0, :], dst[0:E_PAD].rearrange("(a c e) -> a c e", a=1, e=CHUNK)[:, :, 0]).then_inc(lohi_in, 16)
                sp.dma_start(lohi[:, 1, 0:N_CHUNKS - 1], dst[0:E_PAD - CHUNK].rearrange("(a c e) -> a c e", a=1, e=CHUNK)[:, :, CHUNK - 1]).then_inc(lohi_in, 16)
            sp.dma_start(lohi[:, 1, N_CHUNKS - 1:N_CHUNKS], dst[N_EDGES - 1:N_EDGES].rearrange("(a b) -> a b", a=1)).then_inc(lohi_in, 16)
            sp.dma_start(w2_s[:, :, :], W2.rearrange("(h p) f -> p h f", p=P)).then_inc(consts_in, 16)
            sp.dma_start(b2_b[:, :], b2.partition_broadcast(P)).then_inc(consts_in, 16)

            sp.wait_ge(table_made, 1)
            sp.dma_start(item_tab, item_i[0:MAX_ITEMS, :]).then_inc(table_out, 16)
            sp.wait_ge(table_out, 16)
            sp.dma_start(tab[:, :], item_tab.rearrange("(a k) w -> a (k w)", a=1)).then_inc(table_in, 16)
            sp.wait_ge(table_in, 16)
            pairs = sp.value_load(pairs_i[0:1, 1:2], min_val=MIN_PAIRS, max_val=MAX_PAIRS)

            last_pair = sp.value_load(pairs_i[0:1, 2:3], min_val=MIN_PAIRS - 1, max_val=MAX_PAIRS - 1)

            def load_round(stage, r):
                if stage == 0 or stage == LAYERS:
                    sp.dma_start(n_x[:, :, :], rounds_of(x, r)).then_inc(x_loaded, 16)
                if stage == LAYERS:
                    sp.dma_start(n_st[:, :, :], rounds_of(state, r)).then_inc(st_loaded, 16)
                elif stage > 0:
                    sp.dma_start(n_st[:, :, 0:ROW_L], rounds_of(state, r)[:, :, 0:ROW_L]).then_inc(st_loaded, 16)

            def store_round(stage, r):
                width = ROW if stage == 0 else ROW_L
                sp.wait_ge(n_made, r + (1 + stage * ROUNDS))
                sp.dma_start(rounds_of(xl_tab, r), n_lr[:, :, 0:F]).then_inc(n_stored, 16)
                sp.dma_start(rounds_of(xr_tab, r), n_lr[:, :, F:2 * F]).then_inc(n_stored, 16)
                sp.dma_start(rounds_of(state, r)[:, :, 0:width], n_new[:, :, 0:width]).then_inc(n_stored, 16)

            def load_item(k, q, first_layer):
                ch = sp.value_load(tab[0:1, bass.ds(2 * k, 1)], min_val=0, max_val=N_CHUNKS - 1)
                base = sp.value_load(tab[0:1, bass.ds(2 * k + 1, 1)], min_val=0, max_val=EMPTY_BASE)

                def edges(a, shift=0):
                    return a[bass.ds(ch * CHUNK + shift, CHUNK)].rearrange("(p t) -> p t", t=TILES)

                sp.dma_start(idx[:, q, :], edges(src)).then_inc(idx_loaded[q], 16)
                sp.dma_start(dst_e[:, q, :], edges(dst)).then_inc(item_loaded[q], 16)
                sp.dma_start(dst_next[:, q, :], edges(dst, TILES)).then_inc(item_loaded[q], 16)
                rows = dst_rows[bass.ds(ch, 1), :, :]
                sp.dma_start(dst_b[:, q, :], rows.rearrange("a t e -> a (t e)").to_broadcast([P, CHUNK])).then_inc(item_loaded[q], 16)
                for h in range(HEADS):
                    sp.dma_start(dst_r[h * TILES:(h + 1) * TILES, q, :], rows.rearrange("a t e -> (a t) e")).then_inc(item_loaded[q], 16)
                nodes = node_id[bass.ds(base, P)]
                with nc.allow_non_contiguous_dma(reason="one column of node numbers"):
                    sp.dma_start(node_col[:, q, :], nodes.rearrange("(p a) -> p a", a=1)).then_inc(item_loaded[q], 16)
                sp.dma_start(node_row[:, q, :], nodes.rearrange("(a p) -> a p", a=1).to_broadcast([P, P])).then_inc(item_loaded[q], 16)
                sp.dma_start(xr_w[:, q, :], xr_tab[bass.ds(base, P), :]).then_inc(item_loaded[q], 16)
                if first_layer:
                    sp.dma_start(ea[:, q, :, :].rearrange("p t f -> p (t f)"),
                                 edge_attr[bass.ds(ch * CHUNK, CHUNK), :].rearrange("(p t) f -> p (t f)", t=TILES))\
                        .then_inc(ea_loaded[q], 16)

            def window(k, width):
                base = sp.value_load(tab[0:1, bass.ds(2 * k + 1, 1)], min_val=0, max_val=EMPTY_BASE)
                return state[bass.ds(base, P), 0:width]

            for stage in range(LAYERS):
                first = stage == 0
                width = ROW if first else ROW_L
                load_round(stage, 0)
                with sp.Fori(0, ROUNDS - 1) as r:
                    store_round(stage, r)
                    load_round(stage, r + 1)
                store_round(stage, ROUNDS - 1)
                sp.wait_ge(n_stored, stored_value * ((stage + 1) * ROUNDS + 1))

                before = pairs * (2 * stage)
                load_item(0, 0, first)
                load_item(1, 1, first)
                sp.dma_start(st_old[:, 0, 0:width], window(0, width)).then_inc(state_loaded[0], 16)
                with sp.Fori(0, last_pair) as i:
                    for q in range(2):
                        k = 2 * i + q
                        here, ahead = window(k, width), window(k + 1, width)
                        sp.wait_ge(item_done, before + k + 1)
                        sp.dma_start(here, st_new[:, q, 0:width]).then_inc(state_stored, 16)
                        load_item(k + 2, q, first)
                        sp.wait_ge(state_stored, (before + k + 1) * 16)
                        sp.dma_start(st_old[:, 1 - q, 0:width], ahead).then_inc(state_loaded[1 - q], 16)
                for q in range(2):
                    k = 2 * last_pair + q
                    here = window(k, width)
                    if q == 0:
                        ahead = window(k + 1, width)
                    sp.wait_ge(item_done, before + k + 1)
                    sp.dma_start(here, st_new[:, q, 0:width]).then_inc(state_stored, 16)
                    sp.wait_ge(state_stored, (before + k + 1) * 16)
                    if q == 0:
                        sp.dma_start(st_old[:, 1, 0:width], ahead).then_inc(state_loaded[1], 16)
                    else:
                        sp.sem_inc(end_mark, 1)

            load_round(LAYERS, 0)
            with sp.Fori(0, ROUNDS - 1) as r:
                sp.wait_ge(hid_in, r + 1)
                load_round(LAYERS, r + 1)
            with sp.Fori(0, ROUNDS - 1) as r:
                sp.wait_ge(out_made, r + 1)
                sp.dma_start(rounds_of(out, r), n_h[:, :, :]).then_inc(out_stored, 16)
            sp.wait_ge(out_made, ROUNDS)
            sp.dma_start(out[(ROUNDS - 1) * NROWS:N_NODES, :].rearrange("(p j) f -> p j f", j=NB),
                         n_h[0:LAST_P, :, :]).then_inc(out_stored, 16)
            sp.wait_ge(out_stored, 16 * (ROUNDS + 1))

        @block.gpsimd
        def _(pool):
            pool.memset(ident[:, :], 0.0).then_inc(ident_zero, 1)
            pool.iota(k_col[:, :], [[0, 1]], base=0, channel_multiplier=1,
                      allow_small_or_imprecise_dtypes=True).then_inc(rows_made, 1)
            pool.wait_ge(ident_zero, 1)
            pool.affine_select(out=ident[:, :], in_=ident[:, :], compare_op=ALU.not_equal, fill=1.0, base=0,
                               pattern=[[-1, P]], channel_multiplier=1).then_inc(ident_made, 1)
            pool.wait_ge(table_made, 1)
            pairs = pool.value_load(pairs_i[0:1, 1:2], min_val=MIN_PAIRS, max_val=MAX_PAIRS)
            for stage in range(LAYERS):
                with pool.Fori(0, pairs) as i:
                    for q in range(2):
                        pool.wait_ge(idx_loaded[q], (pairs * stage + i + 1) * 16)
                        pool.sem_inc(gather_go, 1)
                        for gi, tiles in enumerate(GROUPS):
                            for t in tiles:
                                pool.indirect_dma_start(xl_g[:, q, t, :], None, xl_tab[:, :],
                                                        bass.IndirectOffsetOnAxis(idx[:, q, t:t + 1], 0))\
                                    .then_inc(gathered[q][gi], 16)

        @block.tensor
        def _(pe):
            pe.wait_ge(ones_made, 1)
            pe.wait_ge(setup, SETUP_ROW_STEPS)
            pe.matmul(flat[:, 0:2 * N_CHUNKS], ones[0:1, :], tab_row[:, :, :].rearrange("a w c -> a (w c)"),
                      start=True, stop=True).then_inc(tab_bc, 1)
            pe.wait_ge(table_made, 1)
            pairs = pe.value_load(pairs_i[0:1, 1:2], min_val=MIN_PAIRS, max_val=MAX_PAIRS)
            pe.wait_ge(ident_made, 1)
            pe.wait_ge(consts_in, 16 * CONST_DMAS)
            for stage in range(LAYERS):
                with pe.Fori(0, ROUNDS) as r:
                    v = r + (1 + stage * ROUNDS)
                    pe.wait_ge(n_ready, v)
                    for j in range(NB):
                        last = pe.transpose(hT_ps[:, j * P:(j + 1) * P], (n_x if stage == 0 else n_h)[:, j, :], ident[:, :])
                    last.then_inc(n_T, 1)
                    pe.wait_ge(n_Tc, v)
                    for j in range(NB):
                        last = pe.matmul(lr_ps[:, j * 2 * F:(j + 1) * 2 * F], n_hT[:, j * P:(j + 1) * P], w_lr[:, stage, :],
                                         start=True, stop=True)
                    last.then_inc(n_prod, 1)

                with pe.Fori(0, pairs) as i:
                    for q in range(2):
                        v = pairs * (2 * stage) + 2 * i + (q + 1)
                        use = pairs * stage + i + 1
                        pe.wait_ge(item_loaded[q], use * (16 * ITEM_DMAS))
                        if stage == 0:
                            pe.wait_ge(ea_loaded[q], use * 16)
                        for gi, tiles in enumerate(GROUPS):
                            pe.wait_ge(onehot_done[gi], v)
                            if gi >= 2:
                                pe.wait_ge(z_done[gi - 2], v)
                            for n, t in enumerate(tiles):
                                last = pe.matmul(zp[gi % 2][:, n * F:(n + 1) * F], ST[:, t, :], xr_w[:, q, :],
                                                 start=True, stop=True)
                            last.then_inc(expanded[gi], 1)
                            if stage == 0:
                                for t in tiles:
                                    last = pe.matmul(ea_ps, S[:, t, :], ea[:, q, t, :], start=t == 0, stop=t == TILES - 1)
                        pe.wait_ge(masked_done, v)
                        pe.transpose(lt_ps, logit_m[:, :], ident[:, :]).then_inc(logitT_done, 1)
                        pe.wait_ge(runmax_done, v)
                        pe.transpose(rm_ps, run_max[:, :], ident[0:LH, 0:LH]).then_inc(runmaxT_done, 1)
                        pe.wait_ge(ends_done, v)
                        for t in range(TILES):
                            last = pe.matmul(cm_ps[:, t * (HEADS + 1):(t + 1) * (HEADS + 1)], S[:, t, :], ends[:, t, :],
                                             start=True, stop=True)
                        last.then_inc(cand_ps_done, 1)
                        pe.wait_ge(newmax_done, v)
                        for t in range(TILES):
                            last = pe.matmul(me_ps[:, t * HEADS:(t + 1) * HEADS], ST[:, t, :], st_new[:, q, 0:HEADS],
                                             start=True, stop=True)
                        last.then_inc(edgemax_done, 1)
                        for gi, tiles in enumerate(GROUPS):
                            pe.wait_ge(msg_done[gi], v)
                            for t in tiles:
                                last = pe.matmul(agg_ps, S[:, t, :], msg[:, t, :], start=t == 0, stop=t == TILES - 1)
                        last.then_inc(agg_done, 1)

            for h in range(2):
                last = pe.matmul(PS[:, 4, h:h + 1], w1_u[:, h * P:(h + 1) * P], u_col[:, :], start=True, stop=True)
            last.then_inc(hid_bias, 1)
            pe.wait_ge(hid_b, 1)
            with pe.Fori(0, ROUNDS) as r:
                v = r + 1
                pe.wait_ge(x1_ready, v)
                for j in range(NB):
                    pe.transpose(hT_ps[:, j * P:(j + 1) * P], n_d[:, j, :], ident[:, :])
                for j in range(NB):
                    last = pe.transpose(eT_ps[:, j * P:(j + 1) * P], n_e[:, j, :], ident[:, :])
                last.then_inc(e_T, 1)
                pe.wait_ge(e_Tc, v)
                for h in range(2):
                    for m in range(2):
                        cut = slice(m * (NROWS // 2), (m + 1) * (NROWS // 2))
                        pe.matmul(PS[:, 4 + 2 * h + m, 0:NROWS // 2], w1_x[:, h * P:(h + 1) * P], n_hT[:, cut], start=True, stop=False)
                        last = pe.matmul(PS[:, 4 + 2 * h + m, 0:NROWS // 2], w1_e[:, h * P:(h + 1) * P], n_eT[:, cut], start=False, stop=True)
                last.then_inc(hid_ps, 1)
                pe.wait_ge(hid_done, v)
            with pe.Fori(0, ROUNDS) as r:
                pe.wait_ge(act_done, r + 1)
                for j in range(NB):
                    for h in range(2):
                        last = pe.matmul(out_ps[:, j * F:(j + 1) * F], hid_relu[:, h, j * P:(j + 1) * P], w2_s[:, h, :],
                                         start=h == 0, stop=h == 1)
                last.then_inc(out_mm, 1)
                pe.wait_ge(out_read, r + 1)

        @block.scalar
        def _(act):
            act.wait_ge(table_made, 1)
            pairs = act.value_load(pairs_i[0:1, 1:2], min_val=MIN_PAIRS, max_val=MAX_PAIRS)
            for stage in range(LAYERS):
                with act.Fori(0, ROUNDS) as r:
                    v = r + (1 + stage * ROUNDS)
                    if stage > 0:
                        act.wait_ge(n_var, r + (1 + (stage - 1) * ROUNDS))
                        act.activation(n_c[:, 3, :], n_c[:, 2, :], ACT.Sqrt).then_inc(n_std, 1)
                    act.wait_ge(n_T, v)
                    act.copy(n_hT[:, :], hT_ps).then_inc(n_Tc, 1)
                with act.Fori(0, pairs) as i:
                    for q in range(2):
                        v = pairs * (2 * stage) + 2 * i + (q + 1)
                        act.wait_ge(dmax_done, v)
                        act.activation(rescale[:, :], dmax[:, :], ACT.Exp).then_inc(rescale_done, 1)
                        act.wait_ge(shifted_done, v)
                        act.activation(msg[:, :, F:F + HEADS], shifted[:, :].rearrange("p (t h) -> p t h", h=HEADS),
                                       ACT.Exp).then_inc(alpha_done, 1)
            with act.Fori(0, ROUNDS) as r:
                v = r + 1
                act.wait_ge(n_var, r + (1 + (LAYERS - 1) * ROUNDS))
                act.activation(n_c[:, 3, :], n_c[:, 2, :], ACT.Sqrt).then_inc(n_std, 1)
                act.wait_ge(x1_var, v)
                act.activation(n_c[:, 7, :], n_c[:, 6, :], ACT.Sqrt).then_inc(x1_std, 1)
                act.wait_ge(e_T, v)
                act.copy(n_hT[:, :], hT_ps)
                act.copy(n_eT[:, :], eT_ps).then_inc(e_Tc, 1)
                act.wait_ge(hid_ps, v)
                for h in range(2):
                    for m in range(2):
                        last = act.activation(hid[h][:, bass.ds(r * NROWS + m * (NROWS // 2), NROWS // 2)],
                                              PS[:, 4 + 2 * h + m, 0:NROWS // 2], ACT.Identity, bias=bn[:, 0, h:h + 1])
                last.then_inc(hid_done, 1)
            act.wait_ge(mu_done, 1)
            full = (ROUNDS - 1) * NROWS
            for h in range(2):
                for m in range(3):
                    if h or m:
                        act.wait_ge(sq_done, 3 * h + m)
                    if m < 2:
                        a = act.activation(squares[:, 0:full // 2], hid[h][:, m * (full // 2):(m + 1) * (full // 2)], ACT.Square,
                                           bias=bn[:, 1, h:h + 1], accum_out=bn_sum[:, h, m:m + 1])
                    else:
                        a = act.activation(squares[:, 0:NB * LAST_P].rearrange("p (j e) -> p j e", j=NB),
                                           hid[h][:, full:].rearrange("p (j e) -> p j e", j=NB)[:, :, 0:LAST_P], ACT.Square,
                                           bias=bn[:, 1, h:h + 1], accum_out=bn_sum[:, h, 2:3])
                    a.then_inc(sq_done, 1)
            act.wait_ge(bn_var, 1)
            act.activation(bn[:, 4, :], bn[:, 3, :], ACT.Sqrt).then_inc(bn_std, 1)
            act.wait_ge(bn_done, 1)
            with act.Fori(0, ROUNDS) as r:
                for h in range(2):
                    last = act.activation(hid_relu[:, h, :], hid[h][:, bass.ds(r * NROWS, NROWS)], ACT.Relu, bias=bn[:, 6, h:h + 1], scale=bn[:, 5, h:h + 1])
                last.then_inc(act_done, 1)
                act.wait_ge(out_var, r + 1)
                act.activation(n_c[:, 3, :], n_c[:, 2, :], ACT.Sqrt).then_inc(out_std, 1)

        @block.vector
        def _(dve):
            ch = Chain(dve, setup)
            dve.memset(ones[:, :], 1.0).then_inc(ones_made, 1)
            ch.link(dve.memset(zero_row[:, :], 0.0))
            dve.wait_ge(lohi_in, 48)
            ch.link(dve.tensor_tensor(out=span[:, :], in0=lohi[:, 1, :], in1=lohi[:, 0, :], op=ALU.subtract))
            ch.link(dve.tensor_scalar(span[:, :], span[:, :], 7, None, ALU.arith_shift_right))
            ch.link(dve.tensor_scalar(nwin[:, :], span[:, :], 1.0, None, ALU.add))
            ch.link(dve.tensor_tensor_scan(tab_row[:, 0, :], nwin[:, :], zero_row[:, :], 0.0, ALU.add, ALU.add))
            ch.link(dve.tensor_tensor(out=nwin[:, :], in0=nwin[:, :], in1=tab_row[:, 0, :], op=ALU.subtract))
            ch.link(dve.tensor_copy(lo_f[:, :], lohi[:, 0, :]))
            ch.link(dve.scalar_tensor_tensor(tab_row[:, 1, :], nwin[:, :], float(P), lo_f[:, :], ALU.mult, ALU.add))
            assert ch.n == SETUP_ROW_STEPS, ch.n
            ch.link(dve.tensor_scalar(pairs_i[:, 0:1], tab_row[:, 0, N_CHUNKS - 1:N_CHUNKS], 1.0, None, ALU.add))
            ch.link(dve.tensor_scalar(pairs_i[:, 1:2], pairs_i[:, 0:1], 1, None, ALU.arith_shift_right))
            ch.link(dve.tensor_scalar(pairs_i[:, 2:3], pairs_i[:, 1:2], -1.0, None, ALU.add))
            dve.wait_ge(tab_bc, 1)
            dve.wait_ge(rows_made, 1)
            ch.link(dve.memset(past[:, 0:1], 1.0))
            ch.link(dve.tensor_scalar(past[:, 1:N_CHUNKS + 1], flat[:, 0:N_CHUNKS], k_col[:, 0:1], None, ALU.is_le))
            ch.link(dve.reduce_sum(item_f[:, 0:1], past[:, 1:N_CHUNKS + 1], axis=AX.X))
            ch.link(dve.tensor_tensor(out=own[:, :], in0=past[:, 0:N_CHUNKS], in1=past[:, 1:N_CHUNKS + 1], op=ALU.subtract))
            ch.link(dve.tensor_tensor(out=own[:, :], in0=own[:, :], in1=flat[:, N_CHUNKS:2 * N_CHUNKS], op=ALU.mult))
            ch.link(dve.reduce_sum(item_f[:, 1:2], own[:, :], axis=AX.X))
            ch.link(dve.scalar_tensor_tensor(item_f[:, 1:2], k_col[:, 0:1], float(P), item_f[:, 1:2], ALU.mult, ALU.add))
            ch.link(dve.tensor_scalar(item_f[:, 2:3], past[:, N_CHUNKS:N_CHUNKS + 1], -1.0, 1.0, ALU.mult, ALU.add))
            ch.link(dve.tensor_tensor(out=item_i[:, 0:1], in0=item_f[:, 0:1], in1=item_f[:, 2:3], op=ALU.mult))
            ch.link(dve.tensor_scalar(item_f[:, 3:4], item_f[:, 1:2], -float(EMPTY_BASE), item_f[:, 2:3], ALU.add, ALU.mult))
            ch.link(dve.tensor_scalar(item_i[:, 1:2], item_f[:, 3:4], float(EMPTY_BASE), None, ALU.add))
            dve.memset(row_pen[:, :], 0.0)
            dve.memset(msg[:, :, MSG - 1:MSG], 1.0).then_inc(table_made, 1)
            dve.wait_ge(table_made, 1)
            pairs = dve.value_load(pairs_i[0:1, 1:2], min_val=MIN_PAIRS, max_val=MAX_PAIRS)
            dve.wait_ge(ident_made, 1)
            dve.wait_ge(consts_in, 16 * CONST_DMAS)

            def normalize(n, y, col, var_sem, std_sem, v):
                n.link(dve.reduce_sum(n_c[:, col, :], y, axis=AX.X))
                n.link(dve.tensor_scalar(n_c[:, col + 1, :], n_c[:, col, :], -1.0 / F, None, ALU.mult))
                n.link(dve.tensor_tensor(out=n_d[:, :, :], in0=y, in1=over_features(n_c[:, col + 1, :]), op=ALU.add))
                n.link(dve.tensor_tensor(out=n_t[:, :, :], in0=n_d[:, :, :], in1=n_d[:, :, :], op=ALU.mult))
                n.link(dve.reduce_sum(n_c[:, col, :], n_t[:, :, :], axis=AX.X))
                dve.tensor_scalar(n_c[:, col + 2, :], n_c[:, col, :], 1.0 / F, EPS, ALU.mult, ALU.add).then_inc(var_sem, 1)
                dve.wait_ge(std_sem, v)
                n.link(dve.reciprocal(n_c[:, col + 1, :], n_c[:, col + 3, :]))
                n.link(dve.tensor_tensor(out=n_d[:, :, :], in0=n_d[:, :, :], in1=over_features(n_c[:, col + 1, :]), op=ALU.mult))

            def finish_layer(n, l, v):
                n.link(dve.reciprocal(n_rd[:, :, :], n_st[:, :, C_DEN:C_DEN + HEADS]))
                n.link(dve.tensor_tensor(out=n_h[:, :, :].rearrange("p j (h f) -> p j h f", h=HEADS),
                                         in0=n_st[:, :, C_ACC:C_ACC + F].rearrange("p j (h f) -> p j h f", h=HEADS),
                                         in1=n_rd[:, :, :].unsqueeze(3).to_broadcast([P, NB, HEADS, F // HEADS]), op=ALU.mult))
                n.link(dve.tensor_tensor(out=n_h[:, :, :], in0=n_h[:, :, :], in1=over_blocks(c_b[:, l, :]), op=ALU.add))
                normalize(n, n_h[:, :, :], 0, n_var, n_std, v)
                n.link(dve.tensor_tensor(out=n_d[:, :, :], in0=n_d[:, :, :], in1=over_blocks(g_b[:, l, :]), op=ALU.mult))
                n.link(dve.tensor_tensor(out=n_d[:, :, :], in0=n_d[:, :, :], in1=over_blocks(be_b[:, l, :]), op=ALU.add))

            def transform(n, stage, r):
                v = r + (1 + stage * ROUNDS)
                dve.wait_ge(n_prod, v)
                dve.wait_ge(n_stored, v * stored_value)
                n.link(dve.tensor_tensor(out=n_lr[:, :, :], in0=lr_ps.rearrange("p (j f) -> p j f", j=NB),
                                         in1=over_blocks(b_lr[:, stage, :]), op=ALU.add))
                n.link(dve.tensor_tensor(out=n_t[:, :, :], in0=n_lr[:, :, 0:F], in1=n_lr[:, :, F:2 * F], op=ALU.add))
                n.link(dve.scalar_tensor_tensor(n_d[:, :, :], n_t[:, :, :], SLOPE, n_t[:, :, :], ALU.mult, ALU.max))
                dve.tensor_copy(n_new[:, :, C_ACC:C_ACC + F], n_lr[:, :, 0:F])
                dve.memset(n_new[:, :, C_DEN:C_DEN + HEADS], 1.0)
                if stage == 0:
                    dve.memset(n_new[:, :, C_CNT:ROW], 0.0)
                n.link(dve.tensor_tensor(out=n_t[:, :, :], in0=n_d[:, :, :], in1=over_blocks(att_b[:, stage, :]), op=ALU.mult))
                if stage < LAYERS - 1:
                    dve.reduce_sum(n_new[:, :, 0:HEADS], n_t[:, :, :].rearrange("p j (h f) -> p j h f", h=HEADS),
                                   axis=AX.X).then_inc(n_made, 1)
                else:
                    n.link(dve.reduce_sum(n_c[:, 0, :], n_t[:, :, :], axis=AX.X))
                    dve.tensor_copy(n_new[:, :, 0:HEADS], over_features(n_c[:, 0, :], HEADS)).then_inc(n_made, 1)

            def edge_item(stage, q, v, use):
                item_value, slot = v, use
                dve.wait_ge(item_loaded[q], use * (16 * ITEM_DMAS))
                lo, hi = node_row[:, q, 0:1], node_row[:, q, P - 1:P]
                dve.tensor_scalar(in_lo[:, :], dst_e[:, q, :], lo, None, ALU.is_ge).then_inc(flags_done[0], 1)
                dve.tensor_tensor(out=not_last[:, :], in0=dst_e[:, q, :], in1=dst_next[:, q, :], op=ALU.not_equal).then_inc(flags_done[1], 1)
                dve.tensor_tensor(out=row_eq[:, 1:P], in0=dst_r[:, q, 1:P], in1=dst_r[:, q, 0:P - 1], op=ALU.is_equal).then_inc(flags_done[2], 1)
                dve.wait_ge(flags_done[0], v)
                dve.scalar_tensor_tensor(in_win[:, :], dst_e[:, q, :], hi, in_lo[:, :], ALU.is_le, ALU.mult).then_inc(flags_done[3], 1)
                dve.wait_ge(flags_done[1], v)
                dve.tensor_scalar(ends[:, :, HEADS], not_last[:, :], ident[:, P - 1:P], None, ALU.max).then_inc(flags_done[4], 1)
                dve.wait_ge(flags_done[2], v)
                dve.tensor_scalar(row_pen[:, 1:P], row_eq[:, 1:P], -1.0, BIG, ALU.add, ALU.mult)
                dve.wait_ge(flags_done[3], v)
                dve.tensor_scalar(out_pen[:, :], in_win[:, :], -1.0, BIG, ALU.add, ALU.mult).then_inc(flags_done[5], 1)

                def onehot(gi):
                    a, n = GROUPS[gi][0], len(GROUPS[gi])
                    dve.tensor_tensor(out=S[:, a:a + n, :], in0=node_row[:, q, :].unsqueeze(1).to_broadcast([P, n, P]),
                                      in1=dst_e[:, q, a:a + n].unsqueeze(2).to_broadcast([P, n, P]), op=ALU.is_equal)
                    dve.tensor_scalar(ST[:, a:a + n, :].rearrange("p t e -> p (t e)"), dst_b[:, q, a * P:(a + n) * P],
                                      node_col[:, q, 0:1], None, ALU.is_equal).then_inc(onehot_done[gi], 1)

                def add_transforms(gi):
                    a, n = GROUPS[gi][0], len(GROUPS[gi])
                    dve.wait_ge(expanded[gi], v)
                    dve.wait_ge(gathered[q][gi], use * (16 * n))
                    dve.tensor_tensor(out=z[:, gi % 2, 0:n, :], in0=zp[gi % 2][:, 0:n * F].rearrange("p (t f) -> p t f", f=F),
                                      in1=xl_g[:, q, a:a + n, :], op=ALU.add).then_inc(z_done[gi], 1)

                def leaky(gi):
                    n = len(GROUPS[gi])
                    dve.wait_ge(z_done[gi], v)
                    dve.scalar_tensor_tensor(lk[:, gi % 2, 0:n, :], z[:, gi % 2, 0:n, :], SLOPE, z[:, gi % 2, 0:n, :],
                                             ALU.mult, ALU.max).then_inc(leaky_done[gi], 1)

                def times_att(gi):
                    n = len(GROUPS[gi])
                    dve.wait_ge(leaky_done[gi], v)
                    dve.tensor_tensor(out=am[:, gi % 2, 0:n, :], in0=lk[:, gi % 2, 0:n, :],
                                      in1=att_b[:, stage, :].unsqueeze(1).to_broadcast([P, n, F]), op=ALU.mult).then_inc(mult_done[gi], 1)

                def logits(gi):
                    a, n = GROUPS[gi][0], len(GROUPS[gi])
                    dve.wait_ge(mult_done[gi], v)
                    if stage < LAYERS - 1:
                        r = dve.reduce_sum(by_tile(logit[:, :])[:, a:a + n, :],
                                           am[:, gi % 2, 0:n, :].rearrange("p t (h f) -> p t h f", h=HEADS), axis=AX.X)
                    else:
                        r = dve.reduce_sum(logit_s[:, a:a + n], am[:, gi % 2, 0:n, :], axis=AX.X)
                    if gi == NG - 1:
                        r.then_inc(logit_done, 1)

                onehot(0)
                add_transforms(0)
                for gi in range(NG):
                    if gi + 1 < NG:
                        onehot(gi + 1)
                    leaky(gi)
                    if gi + 1 < NG:
                        add_transforms(gi + 1)
                    times_att(gi)
                    logits(gi)
                dve.wait_ge(logit_done, v)
                dve.wait_ge(flags_done[5], v)
                per_head = [P, TILES, HEADS]
                dve.tensor_tensor(out=by_tile(logit_m[:, :]),
                                  in0=(by_tile(logit[:, :]) if stage < LAYERS - 1
                                       else logit_s[:, :].unsqueeze(2).to_broadcast(per_head)),
                                  in1=out_pen[:, :].unsqueeze(2).to_broadcast(per_head), op=ALU.add).then_inc(masked_done, 1)
                dve.wait_ge(logitT_done, v)
                dve.tensor_tensor_scan(run_max[:, :], row_pen[:, :], lt_ps, -BIG, ALU.add, ALU.max).then_inc(runmax_done, 1)
                dve.wait_ge(runmaxT_done, v)
                dve.wait_ge(flags_done[4], v)
                dve.tensor_tensor(out=ends[:, :, 0:HEADS], in0=by_tile(rm_ps),
                                  in1=ends[:, :, HEADS:HEADS + 1].to_broadcast(per_head), op=ALU.mult).then_inc(ends_done, 1)
                dve.wait_ge(cand_ps_done, v)
                cm = cm_ps.rearrange("p (t h) -> p t h", h=HEADS + 1)
                dve.tensor_scalar(no_run[:, :], cm[:, :, HEADS], -1.0, BIG, ALU.add, ALU.mult).then_inc(norun_done, 1)
                dve.wait_ge(norun_done, v)
                dve.tensor_tensor(out=cand[:, :, :], in0=cm[:, :, 0:HEADS], in1=no_run[:, :].unsqueeze(2).to_broadcast(per_head),
                                  op=ALU.add).then_inc(cand_done, 1)
                dve.wait_ge(cand_done, v)
                dve.reduce_max(chunk_max[:, :], cand[:, :, :].rearrange("p t h -> p h t"), axis=AX.X).then_inc(chunkmax_done, 1)
                dve.wait_ge(chunkmax_done, v)
                dve.wait_ge(state_loaded[q], use * 16)
                dve.tensor_tensor(out=st_new[:, q, 0:HEADS], in0=chunk_max[:, :], in1=st_old[:, q, 0:HEADS], op=ALU.max).then_inc(newmax_done, 1)
                dve.wait_ge(newmax_done, v)
                dve.tensor_tensor(out=dmax[:, :], in0=st_old[:, q, 0:HEADS], in1=st_new[:, q, 0:HEADS], op=ALU.subtract).then_inc(dmax_done, 1)
                dve.wait_ge(edgemax_done, v)
                dve.tensor_tensor(out=shifted[:, :].rearrange("p (t h) -> p t h", h=HEADS), in0=by_tile(logit_m[:, :]),
                                  in1=me_ps.rearrange("p (t h) -> p t h", h=HEADS), op=ALU.subtract).then_inc(shifted_done, 1)
                dve.wait_ge(alpha_done, v)
                for gi in range(NG):
                    a, n = GROUPS[gi][0], len(GROUPS[gi])
                    dve.tensor_tensor(out=msg[:, a:a + n, 0:F].rearrange("p t (h f) -> p t h f", h=HEADS),
                                      in0=xl_g[:, q, a:a + n, :].rearrange("p t (h f) -> p t h f", h=HEADS),
                                      in1=msg[:, a:a + n, F:F + HEADS].unsqueeze(3).to_broadcast([P, n, HEADS, F // HEADS]),
                                      op=ALU.mult).then_inc(msg_done[gi], 1)
                dve.wait_ge(rescale_done, v)
                dve.tensor_tensor(out=st_new[:, q, C_ACC:C_ACC + F].rearrange("p (h f) -> p h f", h=HEADS),
                                  in0=st_old[:, q, C_ACC:C_ACC + F].rearrange("p (h f) -> p h f", h=HEADS),
                                  in1=rescale[:, :].unsqueeze(2).to_broadcast([P, HEADS, F // HEADS]), op=ALU.mult)
                dve.tensor_tensor(out=st_new[:, q, C_DEN:C_DEN + HEADS], in0=st_old[:, q, C_DEN:C_DEN + HEADS], in1=rescale[:, :],
                                  op=ALU.mult).then_inc(scaled_done, 1)
                dve.wait_ge(agg_done, v)
                dve.wait_ge(scaled_done, v)
                done = dve.tensor_tensor(out=st_new[:, q, C_ACC:C_CNT], in0=st_new[:, q, C_ACC:C_CNT], in1=agg_ps[:, 0:F + HEADS], op=ALU.add)
                if stage == 0:
                    dve.tensor_tensor(out=st_new[:, q, C_CNT:C_EA], in0=st_old[:, q, C_CNT:C_EA], in1=agg_ps[:, MSG - 1:MSG], op=ALU.add)
                    done = dve.tensor_tensor(out=st_new[:, q, C_EA:ROW], in0=st_old[:, q, C_EA:ROW], in1=ea_ps, op=ALU.add)
                done.then_inc(item_done, 1)

            for stage in range(LAYERS):
                with dve.Fori(0, ROUNDS) as r:
                    n = Chain(dve, n_step[stage], r * NODE_STEPS[stage])
                    if stage == 0:
                        dve.wait_ge(x_loaded, r * 16 + 16)
                        dve.memset(n_c[:, 7, :], 0.0).then_inc(n_ready, 1)
                    else:
                        dve.wait_ge(st_loaded, (r + (1 + (stage - 1) * ROUNDS)) * 16)
                        finish_layer(n, stage - 1, r + (1 + (stage - 1) * ROUNDS))
                        dve.tensor_scalar(n_h[:, :, :], n_d[:, :, :], 0.0, None, ALU.max).then_inc(n_ready, 1)
                    transform(n, stage, r)
                    assert n.n == NODE_STEPS[stage], (stage, n.n)
                with dve.Fori(0, pairs) as i:
                    for q in range(2):
                        edge_item(stage, q, pairs * (2 * stage) + 2 * i + (q + 1), pairs * stage + i + 1)

            dve.wait_ge(hid_bias, 1)
            dve.tensor_tensor(out=bn[:, 0, :], in0=PS[:, 4, 0:2], in1=cols1[:, 0, :], op=ALU.add).then_inc(hid_b, 1)
            with dve.Fori(0, ROUNDS) as r:
                v = r + 1
                n = Chain(dve, n_step[LAYERS], r * NODE_STEPS[LAYERS])
                dve.wait_ge(st_loaded, (r + (1 + (LAYERS - 1) * ROUNDS)) * 16)
                finish_layer(n, LAYERS - 1, r + (1 + (LAYERS - 1) * ROUNDS))
                dve.wait_ge(x_loaded, (r + (1 + ROUNDS)) * 16)
                n.link(dve.scalar_tensor_tensor(n_h[:, :, :], n_d[:, :, :], 0.0, n_x[:, :, :], ALU.max, ALU.add))
                normalize(n, n_h[:, :, :], 4, x1_var, x1_std, v)
                dve.tensor_copy(x1[:, bass.ds(r * NB, NB), :], n_d[:, :, :])
                n.link(dve.tensor_scalar(n_c[:, 0, :], n_st[:, :, C_CNT], 1.0, None, ALU.max))
                n.link(dve.reciprocal(n_c[:, 1, :], n_c[:, 0, :]))
                dve.tensor_tensor(out=n_e[:, :, :], in0=n_st[:, :, C_EA:ROW], in1=over_features(n_c[:, 1, :], D_EDGE), op=ALU.mult)\
                    .then_inc(x1_ready, 1)
                dve.wait_ge(x1_ready, v)
                dve.memset(n_c[:, 2, :], 0.0).then_inc(hid_in, 1)
                dve.wait_ge(hid_done, v)
                assert n.n == NODE_STEPS[LAYERS], n.n

            ch = Chain(dve, o_step[0])
            full = (ROUNDS - 1) * NROWS
            for h in range(2):
                dve.reduce_sum(bn_sum[:, h, 0:1], hid[h][:, 0:full], axis=AX.X)
                ch.link(dve.reduce_sum(bn_sum[:, h, 1:2], hid[h][:, full:].rearrange("p (j e) -> p j e", j=NB)[:, :, 0:LAST_P], axis=AX.XY))
            ch.link(dve.tensor_tensor(out=bn[:, 2, :], in0=bn_sum[:, :, 0], in1=bn_sum[:, :, 1], op=ALU.add))
            dve.tensor_scalar(bn[:, 1, :], bn[:, 2, :], -1.0 / N_NODES, None, ALU.mult).then_inc(mu_done, 1)
            dve.wait_ge(sq_done, 6)
            ch.link(dve.reduce_sum(bn[:, 2, :], bn_sum[:, :, 0:3], axis=AX.X))
            dve.tensor_scalar(bn[:, 3, :], bn[:, 2, :], 1.0 / N_NODES, EPS, ALU.mult, ALU.add).then_inc(bn_var, 1)
            dve.wait_ge(bn_std, 1)
            ch.link(dve.reciprocal(bn[:, 7, :], bn[:, 4, :]))
            ch.link(dve.tensor_tensor(out=bn[:, 5, :], in0=bn[:, 7, :], in1=cols1[:, 1, :], op=ALU.mult))
            ch.link(dve.tensor_tensor(out=bn[:, 2, :], in0=bn[:, 1, :], in1=bn[:, 5, :], op=ALU.mult))
            dve.tensor_tensor(out=bn[:, 6, :], in0=bn[:, 2, :], in1=cols1[:, 2, :], op=ALU.add).then_inc(bn_done, 1)

            with dve.Fori(0, ROUNDS) as r:
                v = r + 1
                n = Chain(dve, o_step[1], r * OUT_STEPS)
                dve.wait_ge(out_mm, v)
                n.link(dve.tensor_tensor(out=n_d[:, :, :], in0=out_ps.rearrange("p (j f) -> p j f", j=NB), in1=over_blocks(b2_b[:, :]), op=ALU.add))
                n.link(dve.tensor_tensor(out=n_x[:, :, :], in0=n_d[:, :, :], in1=x1[:, bass.ds(r * NB, NB), :], op=ALU.add))
                dve.memset(n_c[:, 7, :], 0.0).then_inc(out_read, 1)
                normalize(n, n_x[:, :, :], 0, out_var, out_std, v)
                dve.wait_ge(out_stored, r * 16 + 16)
                dve.tensor_copy(n_h[:, :, :], n_d[:, :, :]).then_inc(out_made, 1)
                dve.wait_ge(out_made, v)
                assert n.n == OUT_STEPS, n.n


_LAYER = {"Wl": "W{}l", "bl": "b{}l", "Wr": "W{}r", "br": "b{}r", "att": "a{}", "c": "c{}", "g": "g{}", "be": "be{}"}
_LAST = ("u", "W1", "b1", "gamma", "beta", "W2", "b2")


def kernel(**inputs):
    import numpy as np
    import concourse.bacc as bacc
    from concourse.bass_utils import run_bass_kernel_spmd

    nc = bacc.Bacc("TRN2", target_bir_lowering=False, num_devices=1)
    arrays = {}

    def given(name, a):
        arrays[name] = np.ascontiguousarray(a)
        return nc.dram_tensor(name, a.shape, mybir.dt.from_np(a.dtype), kind="ExternalInput").ap()

    def padded(a, rows, value):
        a = np.asarray(a)
        return np.concatenate([a, np.full((rows - a.shape[0],) + a.shape[1:], value, a.dtype)])

    dst = padded(inputs["dst"], E_PAD + TILES, NO_NODE)
    args = {
        "x": given("x", padded(inputs["x"], N_PAD, 0)),
        "src": given("src", padded(inputs["src"], E_PAD, 0)),
        "dst": given("dst", dst),
        "dst_rows": given("dst_rows", dst[0:E_PAD].reshape(N_CHUNKS, P, TILES).transpose(0, 2, 1)),
        "edge_attr": given("edge_attr", padded(inputs["edge_attr_96"], E_PAD, 0)),
        "node_id": given("node_id", np.arange(N_PAD, dtype=np.float32)),
    }
    for key, name in _LAYER.items():
        args[key] = [given(f"{key}{l}", np.asarray(inputs["L0_gnn_" + name.format(l + 1)])) for l in range(LAYERS)]
    for key in _LAST:
        args[key] = given("last_" + key, np.asarray(inputs["L1_gnn_" + key]))
    args["out"] = nc.dram_tensor("out", (N_NODES, F), F32, kind="ExternalOutput").ap()
    gnn_program(nc, **args)
    r = run_bass_kernel_spmd(nc, [arrays], core_ids=[0])
    return r.results[0]["out"]
```

```python
import concourse.bass as bass
from concourse import mybir
from contextlib import ExitStack

F32 = mybir.dt.float32
I32 = mybir.dt.int32
ALU = mybir.AluOpType
ACT = mybir.ActivationFunctionType
AX = mybir.AxisListType

P = 128
N_NODES = 6250
N_EDGES = 206250
F = 128
HEADS = 4
D_EDGE = 96
D_GRAPH = 64
HIDDEN = 256
N_GRAPHS = 64
LAYERS = 3
EPS = 1e-5
SLOPE = 0.2
BIG = 1e30

TILES = 26
CHUNK = TILES * P
N_CHUNKS = -(-N_EDGES // CHUNK)
E_PAD = N_CHUNKS * CHUNK
LAST_EDGE = N_EDGES - 1 - (N_CHUNKS - 1) * CHUNK
NO_NODE = 100000
GROUPS = [range(a, min(a + 4, TILES)) for a in range(0, TILES, 4)]
NG = len(GROUPS)
SUMS_AT = {2: (0,), 3: (1, 2), 4: (3, 4), 5: (5, 6)}
LH = TILES * HEADS

NB = 5
NROWS = NB * P
ROUNDS = -(-(N_NODES + P) // NROWS)
N_PAD = ROUNDS * NROWS
EMPTY_BASE = N_PAD - P
LAST_P = (N_NODES - (ROUNDS - 1) * NROWS) // NB
assert LAST_P * NB == N_NODES - (ROUNDS - 1) * NROWS

MAX_ITEMS = N_CHUNKS + N_NODES // P
MAX_ITEMS += MAX_ITEMS % 2
MIN_PAIRS, MAX_PAIRS = N_CHUNKS // 2, MAX_ITEMS // 2
assert N_CHUNKS % 2 == 0

XW = F + HEADS

M_ALPHA, M_ONE, M_MAX = F, F + HEADS, F + HEADS + 1
MSG = M_MAX + HEADS

C_ACC, C_DEN, C_CNT, C_EA = HEADS, HEADS + F, 2 * HEADS + F, 2 * HEADS + F + 1
ROW_L = C_CNT
ROW = C_EA + D_EDGE

ITEM_DMAS = 7 + HEADS
SETUP_ROW_STEPS = 8
NODE_STEPS = [5, 17, 18, 22]
OUT_STEPS = 9


def gnn_program(nc, x, src_t, dst_t, next_t, dst, edge_attr, node_id, Wl, bl, Wr, br, att, c, g, be,
                u, W1, b1, gamma, beta, W2, b2, out):
    ctx = ExitStack()
    with ctx:
        def sb(name, shape, dt=F32):
            return ctx.enter_context(nc.sbuf_tensor(name, shape, dt))

        def sem(name):
            return ctx.enter_context(nc.semaphore(name))

        def sems(name, n):
            return [sem(f"{name}{i}") for i in range(n)]

        def scratch(name, shape, dt=F32):
            return nc.dram_tensor(name, shape, dt, kind="Internal").ap()

        xl_tab = scratch("xl_tab", (N_PAD, XW))
        xr_tab = scratch("xr_tab", (N_PAD, XW))
        state = scratch("state", (N_PAD, ROW))
        item_tab = scratch("item_tab", (MAX_ITEMS, 2), I32)

        ident = sb("ident", [P, P])
        ones = sb("ones", [1, P])
        w_lr = sb("w_lr", [P, LAYERS, 2 * F])
        b_lr = sb("b_lr", [P, LAYERS, 2 * F])
        att_b = sb("att_b", [P, LAYERS, F])
        att_relu = sb("att_relu", [P, LAYERS, F])
        att_lin = sb("att_lin", [P, LAYERS, F])
        c_b = sb("c_b", [P, LAYERS, F])
        g_b = sb("g_b", [P, LAYERS, F])
        be_b = sb("be_b", [P, LAYERS, F])
        w1_x = sb("w1_x", [P, HIDDEN])
        w1_e = sb("w1_e", [D_EDGE, HIDDEN])
        w1_u = sb("w1_u", [D_GRAPH, HIDDEN])
        u_col = sb("u_col", [D_GRAPH, 1])
        w2_s = sb("w2_s", [P, 2, F])
        b2_b = sb("b2_b", [P, F])
        cols1 = sb("cols1", [P, 3, 2])

        lohi = sb("lohi", [1, 2, N_CHUNKS], I32)
        span = sb("span", [1, N_CHUNKS], I32)
        nwin = sb("nwin", [1, N_CHUNKS])
        zero_row = sb("zero_row", [1, N_CHUNKS])
        tab_row = sb("tab_row", [1, 2, N_CHUNKS])
        lo_f = sb("lo_f", [1, N_CHUNKS])
        pairs_f = sb("pairs_f", [1, 1])
        pairs_i = sb("pairs_i", [1, 3], I32)
        k_col = sb("k_col", [P, 1])
        past = sb("past", [P, N_CHUNKS + 1])
        own = sb("own", [P, N_CHUNKS])
        item_f = sb("item_f", [P, 4])
        item_i = sb("item_i", [P, 2], I32)
        tab = sb("tab", [1, MAX_ITEMS * 2], I32)

        idx = sb("idx", [P, 2, TILES], I32)
        dst_e = sb("dst_e", [P, 2, TILES], I32)
        dst_next = sb("dst_next", [P, 2, TILES], I32)
        dst_r = sb("dst_r", [LH, 2, P], I32)
        tile_ends = sb("tile_ends", [1, 2, TILES, 2], I32)
        dst_b = sb("dst_b", [P, 2, CHUNK], I32)
        node_col = sb("node_col", [P, 2, 1])
        node_row = sb("node_row", [P, 2, P])
        xr_w = sb("xr_w", [P, 2, XW])
        xl_g = sb("xl_g", [P, 2, TILES, XW])
        ea = sb("ea", [P, 2, TILES, D_EDGE])
        st_old = sb("st_old", [P, 2, ROW])
        st_new = sb("st_new", [P, 2, ROW])
        neg_dst = sb("neg_dst", [P, 2, TILES])
        dist = sb("dist", [P, 2, 4, P])
        S = sb("S", [P, 2, TILES, P])
        ST = sb("ST", [P, TILES, P])
        z = sb("z", [P, 2, 4, XW])
        am = sb("am", [P, 2, 4, F])
        relu_logit = sb("relu_logit", [P, LH])
        logit = sb("logit", [P, 2, LH])
        seg_last = sb("seg_last", [P, TILES])
        row_eq = sb("row_eq", [LH, P])
        row_pen = sb("row_pen", [LH, P + 1])
        tile_eq = sb("tile_eq", [1, TILES + 1])
        tile_one = sb("tile_one", [1, TILES])
        through = sb("through", [1, 2, TILES])
        through_pen = sb("through_pen", [1, 2, LH])
        enter_pen = sb("enter_pen", [1, 2, LH])
        run_up = sb("run_up", [LH, P])
        run_down = sb("run_down", [LH, P])
        open_max = sb("open_max", [1, 2, LH + 2])
        carry = sb("carry", [1, 2, LH])
        carry_col = sb("carry_col", [LH, 2])
        up = sb("up", [LH, P])
        seg_max = sb("seg_max", [LH, P])
        shifted = sb("shifted", [P, LH])
        msg = sb("msg", [P, TILES, MSG])
        some = sb("some", [P, 1])
        none_pen = sb("none_pen", [P, 1])
        chunk_max = sb("chunk_max", [P, HEADS])
        dmax = sb("dmax", [P, 2, HEADS])
        rescale = sb("rescale", [P, 2, HEADS])
        scaled = sb("scaled", [P, 2, F + HEADS])

        spare = ST[:, :, :].rearrange("p t e -> p (t e)")
        n_h, n_d, n_t = [spare[:, i * NROWS:(i + 1) * NROWS].rearrange("p (j f) -> p j f", f=F) for i in range(3)]
        n_q = spare[:, 3 * NROWS:5 * NROWS].rearrange("p (j s f) -> p j s f", s=2, f=F)
        n_st = sb("n_st", [P, NB, ROW])
        n_new = sb("n_new", [P, NB, ROW])
        n_x = sb("n_x", [P, NB, F])
        n_lr = sb("n_lr", [P, NB, 2, XW])
        n_hT = sb("n_hT", [P, NROWS])
        n_eT = sb("n_eT", [D_EDGE, NROWS])
        n_rd = sb("n_rd", [P, NB, HEADS])
        n_m = sb("n_m", [P, NB, HEADS])
        n_l1 = sb("n_l1", [P, 2 * NB])
        n_c = sb("n_c", [P, 8, NB])
        n_e = sb("n_e", [P, NB, D_EDGE])
        x1 = S[:, :, :, :].rearrange("p a t n -> p (a t n)")[:, 0:ROUNDS * NB * F].rearrange("p (j f) -> p j f", f=F)
        hid = [xl_g[:, :, :, :].rearrange("p a t f -> p (a t f)")[:, 0:N_PAD],
               dst_b[:, :, :].rearrange("p a e -> p (a e)")[:, 0:N_PAD].bitcast(F32)]
        hid_relu = n_q[:, :, :, :].rearrange("p j s f -> p (j s f)").rearrange("p (h e) -> p h e", h=2)
        squares = msg[:, :, :].rearrange("p t n -> p (t n)")
        bn = sb("bn", [P, 8, 2])
        bn_sum = sb("bn_sum", [P, 2, 4])

        PS = ctx.enter_context(nc.psum_tensor("PS", [P, 8, 512], F32))
        flat = PS[:, :, :].rearrange("p b n -> p (b n)")
        zp = [flat[:, b * 1024:(b + 1) * 1024].rearrange("p (t f) -> p t f", t=4)[:, :, 0:XW] for b in range(2)]
        lt_ps = PS[0:LH, 4, 0:P]
        mb_ps = PS[:, 4, 128:128 + LH]
        open_ps = [PS[0:1, 4, 232 + d * LH:232 + (d + 1) * LH] for d in range(2)]
        carry_ps = PS[0:LH, 4, 440:442]
        agg_ps = PS[:, 5, 0:MSG]
        ea_ps = PS[:, 6, 0:D_EDGE]
        hT_ps = flat[:, 0:NROWS]
        eT_ps = flat[0:D_EDGE, 1024:1024 + NROWS]
        lr_ps = flat[:, 5 * 512:5 * 512 + NB * 2 * F]
        out_ps = flat[:, 0:NROWS]

        consts_in = sem("consts_in")
        ident_zero = sem("ident_zero")
        ident_made = sem("ident_made")
        ones_made = sem("ones_made")
        lohi_in = sem("lohi_in")
        tab_bc = sem("tab_bc")
        table_made = sem("table_made")
        table_out = sem("table_out")
        table_in = sem("table_in")
        setup = sem("setup")
        rows_made = sem("rows_made")

        idx_loaded = sems("idx_loaded", 2)
        item_loaded = sems("item_loaded", 2)
        ea_loaded = sems("ea_loaded", 2)
        state_loaded = sems("state_loaded", 2)
        state_stored = sem("state_stored")
        gathered = [sems(f"gathered{q}_", NG) for q in range(2)]
        gather_go = sem("gather_go")
        load_go = sem("load_go")
        negdst_done = sem("negdst_done")
        flag_done = sems("flag_done", 7)
        onehotT_done = sems("onehotT_done", NG)
        onehot_done = sems("onehot_done", NG)
        expanded = sems("expanded", NG)
        z_done = sems("z_done", NG)
        logit_done = sems("logit_done", NG)
        logitT_done = sem("logitT_done")
        runs_done = sem("runs_done")
        open_done = sem("open_done")
        openmax_done = sem("openmax_done")
        carry_done = sem("carry_done")
        carryT_done = sem("carryT_done")
        carrycol_done = sem("carrycol_done")
        up_done = sem("up_done")
        segmax_done = sem("segmax_done")
        segmaxT_done = sem("segmaxT_done")
        shifted_done = sem("shifted_done")
        alpha_done = sem("alpha_done")
        msg_done = sems("msg_done", NG)
        agg_done = sem("agg_done")
        some_done = sem("some_done")
        none_done = sem("none_done")
        chunkmax_done = sem("chunkmax_done")
        newmax_done = sem("newmax_done")
        dmax_done = sem("dmax_done")
        rescale_done = sem("rescale_done")
        scaled_done = sem("scaled_done")
        item_done = sem("item_done")

        x_loaded = sem("x_loaded")
        st_loaded = sem("st_loaded")
        hid_in = sem("hid_in")
        x1_ready = sem("x1_ready")
        x1_var = sem("x1_var")
        x1_std = sem("x1_std")
        out_read = sem("out_read")
        n_stored = sem("n_stored")
        n_step = sems("n_step", LAYERS + 1)
        n_var = sem("n_var")
        n_std = sem("n_std")
        n_ready = sem("n_ready")
        n_T = sem("n_T")
        n_Tc = sem("n_Tc")
        n_prod = sem("n_prod")
        n_made = sem("n_made")
        o_step = sems("o_step", 3)
        e_ready = sem("e_ready")
        e_T = sem("e_T")
        e_Tc = sem("e_Tc")
        hid_ps = sem("hid_ps")
        hid_bias = sem("hid_bias")
        hid_done = sem("hid_done")
        hid_b = sem("hid_b")
        mu_done = sem("mu_done")
        sq_done = sem("sq_done")
        bn_var = sem("bn_var")
        bn_std = sem("bn_std")
        bn_done = sem("bn_done")
        act_done = sem("act_done")
        out_mm = sem("out_mm")
        out_var = sem("out_var")
        out_std = sem("out_std")
        out_made = sem("out_made")
        out_stored = sem("out_stored")
        end_mark = sem("end_mark")


        block = ctx.enter_context(nc.Block())

        NODE_STORES = 3
        CONST_DMAS = 8 * LAYERS + 9
        stored_value = 16 * NODE_STORES

        def rounds_of(ap, r):
            return ap[bass.ds(r * NROWS, NROWS), :].rearrange("(p j) f -> p j f", j=NB)

        def over_blocks(ap):
            return ap.unsqueeze(1).to_broadcast([P, NB, ap.shape[1]])

        def over_features(ap, n=F):
            return ap.unsqueeze(2).to_broadcast([P, NB, n])

        def by_tile(ap):
            return ap.rearrange("p (h t) -> p t h", h=HEADS)

        class Chain:

            def __init__(self, eng, step_sem, base=0):
                self.eng, self.sem, self.base, self.n = eng, step_sem, base, 0

            def did(self, instruction):
                instruction.then_inc(self.sem, 1)
                self.n += 1
                return self.n

            def link(self, instruction):
                n = self.did(instruction)
                self.eng.wait_ge(self.sem, self.base + n)

        def pipeline(eng, stage, pairs, last_pair, step):
            def item(i, q):
                return q, pairs * (2 * stage) + 2 * i + (q + 1), pairs * stage + i + 1

            step(item(0, 0), None)
            with eng.Fori(0, last_pair) as i:
                step(item(i, 1), item(i, 0))
                step(item(i + 1, 0), item(i, 1))
            step(item(last_pair, 1), item(last_pair, 0))
            step(None, item(last_pair, 1))

        @block.sync
        def _(sp):
            sp.sem_inc(n_stored, stored_value)
            sp.sem_inc(out_stored, 16)
            for l in range(LAYERS):
                for h, (w, b) in enumerate(((Wl, bl), (Wr, br))):
                    sp.dma_start(w_lr[:, l, h * F:(h + 1) * F], w[l]).then_inc(consts_in, 16)
                    sp.dma_start(b_lr[:, l, h * F:(h + 1) * F], b[l].partition_broadcast(P)).then_inc(consts_in, 16)
                sp.dma_start(att_b[:, l, :], att[l].rearrange("h f -> (h f)").partition_broadcast(P)).then_inc(consts_in, 16)
                for t, v in ((c_b, c), (g_b, g), (be_b, be)):
                    sp.dma_start(t[:, l, :], v[l].partition_broadcast(P)).then_inc(consts_in, 16)
            sp.dma_start(w1_x[:, :], W1[0:F, :]).then_inc(consts_in, 16)
            sp.dma_start(w1_e[:, :], W1[F:F + D_EDGE, :]).then_inc(consts_in, 16)
            sp.dma_start(w1_u[:, :], W1[F + D_EDGE:F + D_EDGE + D_GRAPH, :]).then_inc(consts_in, 16)
            with nc.allow_non_contiguous_dma(reason="a few columns"):
                sp.dma_start(u_col[:, :], u[0:1, :].rearrange("a d -> d a")).then_inc(consts_in, 16)
                for i, v in enumerate((b1, gamma, beta)):
                    sp.dma_start(cols1[:, i, :], v.rearrange("(h p) -> p h", p=P)).then_inc(consts_in, 16)
                sp.dma_start(lohi[:, 0, :], dst.rearrange("(a c) t e -> a c (t e)", a=1)[:, :, 0]).then_inc(lohi_in, 16)
                sp.dma_start(lohi[:, 1, 0:N_CHUNKS - 1], dst[0:N_CHUNKS - 1].rearrange("(a c) t e -> a c (t e)", a=1)[:, :, CHUNK - 1]).then_inc(lohi_in, 16)
            sp.dma_start(lohi[:, 1, N_CHUNKS - 1:N_CHUNKS], dst[N_CHUNKS - 1].rearrange("(a t) e -> a (t e)", a=1)[:, LAST_EDGE:LAST_EDGE + 1]).then_inc(lohi_in, 16)
            sp.dma_start(w2_s[:, :, :], W2.rearrange("(h p) f -> p h f", p=P)).then_inc(consts_in, 16)
            sp.dma_start(b2_b[:, :], b2.partition_broadcast(P)).then_inc(consts_in, 16)

            sp.wait_ge(table_made, 1)
            sp.dma_start(item_tab, item_i[0:MAX_ITEMS, :]).then_inc(table_out, 16)
            sp.wait_ge(table_out, 16)
            sp.dma_start(tab[:, :], item_tab.rearrange("(a k) w -> a (k w)", a=1)).then_inc(table_in, 16)
            sp.wait_ge(table_in, 16)
            pairs = sp.value_load(pairs_i[0:1, 1:2], min_val=MIN_PAIRS, max_val=MAX_PAIRS)

            last_pair = sp.value_load(pairs_i[0:1, 2:3], min_val=MIN_PAIRS - 1, max_val=MAX_PAIRS - 1)

            def load_round(stage, r):
                if stage == 0 or stage == LAYERS:
                    sp.dma_start(n_x[:, :, :], rounds_of(x, r)).then_inc(x_loaded, 16)
                if stage == LAYERS:
                    sp.dma_start(n_st[:, :, :], rounds_of(state, r)).then_inc(st_loaded, 16)
                elif stage > 0:
                    sp.dma_start(n_st[:, :, 0:ROW_L], rounds_of(state, r)[:, :, 0:ROW_L]).then_inc(st_loaded, 16)

            def store_round(stage, r):
                width = ROW if stage == 0 else ROW_L
                sp.wait_ge(n_made, r + (1 + stage * ROUNDS))
                sp.dma_start(rounds_of(xl_tab, r), n_lr[:, :, 0, :]).then_inc(n_stored, 16)
                sp.dma_start(rounds_of(xr_tab, r), n_lr[:, :, 1, :]).then_inc(n_stored, 16)
                sp.dma_start(rounds_of(state, r)[:, :, 0:width], n_new[:, :, 0:width]).then_inc(n_stored, 16)

            def load_item(k, q):
                ch = sp.value_load(tab[0:1, bass.ds(2 * k, 1)], min_val=0, max_val=N_CHUNKS - 1)
                base = sp.value_load(tab[0:1, bass.ds(2 * k + 1, 1)], min_val=0, max_val=EMPTY_BASE)

                def edges(a):
                    return a[bass.ds(ch, 1), :, :].rearrange("a p t -> (a p) t")

                sp.dma_start(idx[:, q, :], edges(src_t)).then_inc(idx_loaded[q], 16)
                sp.dma_start(dst_e[:, q, :], edges(dst_t)).then_inc(item_loaded[q], 16)
                sp.dma_start(dst_next[:, q, :], edges(next_t)).then_inc(item_loaded[q], 16)
                rows = dst[bass.ds(ch, 1), :, :]
                sp.dma_start(dst_b[:, q, :], rows.rearrange("a t e -> a (t e)").to_broadcast([P, CHUNK])).then_inc(item_loaded[q], 16)
                for h in range(HEADS):
                    sp.dma_start(dst_r[h * TILES:(h + 1) * TILES, q, :], rows.rearrange("a t e -> (a t) e")).then_inc(item_loaded[q], 16)
                with nc.allow_non_contiguous_dma(reason="first and last of each tile"):
                    sp.dma_start(tile_ends[:, q, :, :], rows[:, :, 0:P:P - 1]).then_inc(item_loaded[q], 16)
                nodes = node_id[bass.ds(base, P)]
                with nc.allow_non_contiguous_dma(reason="one column of node numbers"):
                    sp.dma_start(node_col[:, q, :], nodes.rearrange("(p a) -> p a", a=1)).then_inc(item_loaded[q], 16)
                sp.dma_start(node_row[:, q, :], nodes.rearrange("(a p) -> a p", a=1).to_broadcast([P, P])).then_inc(item_loaded[q], 16)
                sp.dma_start(xr_w[:, q, :], xr_tab[bass.ds(base, P), :]).then_inc(item_loaded[q], 16)

            def load_attributes(k, q):
                ch = sp.value_load(tab[0:1, bass.ds(2 * k, 1)], min_val=0, max_val=N_CHUNKS - 1)
                sp.dma_start(ea[:, q, :, :].rearrange("p t f -> p (t f)"),
                             edge_attr[bass.ds(ch, 1), :, :].rearrange("a p n -> (a p) n")).then_inc(ea_loaded[q], 16)

            def window(k, width):
                base = sp.value_load(tab[0:1, bass.ds(2 * k + 1, 1)], min_val=0, max_val=EMPTY_BASE)
                return state[bass.ds(base, P), 0:width]

            for stage in range(LAYERS):
                first = stage == 0
                width = ROW if first else ROW_L
                load_round(stage, 0)
                with sp.Fori(0, ROUNDS - 1) as r:
                    store_round(stage, r)
                    load_round(stage, r + 1)
                store_round(stage, ROUNDS - 1)
                sp.wait_ge(n_stored, stored_value * ((stage + 1) * ROUNDS + 1))

                before = pairs * (2 * stage)
                for q in range(2):
                    load_item(q, q)
                    if first:
                        load_attributes(q, q)
                sp.dma_start(st_old[:, 0, 0:width], window(0, width)).then_inc(state_loaded[0], 16)
                with sp.Fori(0, last_pair) as i:
                    for q in range(2):
                        k = 2 * i + q
                        here, ahead = window(k, width), window(k + 1, width)
                        sp.wait_ge(onehot_done[NG - 1], (before + k + 1) * 2)
                        sp.sem_inc(load_go, 1)
                        sp.wait_ge(logit_done[NG - 1], (before + k + 1) * 3)
                        sp.sem_inc(load_go, 1)
                        load_item(k + 2, q)
                        sp.wait_ge(item_done, before + k + 1)
                        sp.dma_start(here, st_new[:, q, 0:width]).then_inc(state_stored, 16)
                        if first:
                            load_attributes(k + 2, q)
                        sp.wait_ge(state_stored, (before + k + 1) * 16)
                        sp.dma_start(st_old[:, 1 - q, 0:width], ahead).then_inc(state_loaded[1 - q], 16)
                for q in range(2):
                    k = 2 * last_pair + q
                    here = window(k, width)
                    if q == 0:
                        ahead = window(k + 1, width)
                    sp.wait_ge(item_done, before + k + 1)
                    sp.dma_start(here, st_new[:, q, 0:width]).then_inc(state_stored, 16)
                    sp.wait_ge(state_stored, (before + k + 1) * 16)
                    if q == 0:
                        sp.dma_start(st_old[:, 1, 0:width], ahead).then_inc(state_loaded[1], 16)
                    else:
                        sp.sem_inc(end_mark, 1)

            load_round(LAYERS, 0)
            with sp.Fori(0, ROUNDS - 1) as r:
                sp.wait_ge(hid_in, r + 1)
                load_round(LAYERS, r + 1)
            with sp.Fori(0, ROUNDS - 1) as r:
                sp.wait_ge(out_made, r + 1)
                sp.dma_start(rounds_of(out, r), n_h[:, :, :]).then_inc(out_stored, 16)
            sp.wait_ge(out_made, ROUNDS)
            sp.dma_start(out[(ROUNDS - 1) * NROWS:N_NODES, :].rearrange("(p j) f -> p j f", j=NB),
                         n_h[0:LAST_P, :, :]).then_inc(out_stored, 16)
            sp.wait_ge(out_stored, 16 * (ROUNDS + 1))

        @block.gpsimd
        def _(pool):
            pool.memset(ident[:, :], 0.0).then_inc(ident_zero, 1)
            pool.iota(k_col[:, :], [[0, 1]], base=0, channel_multiplier=1,
                      allow_small_or_imprecise_dtypes=True).then_inc(rows_made, 1)
            pool.wait_ge(ident_zero, 1)
            pool.affine_select(out=ident[:, :], in_=ident[:, :], compare_op=ALU.not_equal, fill=1.0, base=0,
                               pattern=[[-1, P]], channel_multiplier=1).then_inc(ident_made, 1)
            pool.wait_ge(table_made, 1)
            pairs = pool.value_load(pairs_i[0:1, 1:2], min_val=MIN_PAIRS, max_val=MAX_PAIRS)
            for stage in range(LAYERS):
                with pool.Fori(0, pairs) as i:
                    for q in range(2):
                        pool.wait_ge(idx_loaded[q], (pairs * stage + i + 1) * 16)
                        for g, tiles in enumerate(GROUPS):
                            pool.wait_ge(msg_done[g], pairs * (2 * stage) + 2 * i + (q + 1))
                            pool.sem_inc(gather_go, 1)
                            for t in tiles:
                                pool.indirect_dma_start(xl_g[:, q, t, :], None, xl_tab[:, :],
                                                        bass.IndirectOffsetOnAxis(idx[:, q, t:t + 1], 0))\
                                    .then_inc(gathered[q][g], 16)

        @block.tensor
        def _(pe):
            for g in range(NG):
                pe.sem_inc(msg_done[g], 2)
            pe.wait_ge(ones_made, 1)
            pe.wait_ge(setup, SETUP_ROW_STEPS)
            pe.matmul(flat[:, 0:2 * N_CHUNKS], ones[0:1, :], tab_row[:, :, :].rearrange("a w c -> a (w c)"),
                      start=True, stop=True).then_inc(tab_bc, 1)
            pe.wait_ge(table_made, 1)
            pairs = pe.value_load(pairs_i[0:1, 1:2], min_val=MIN_PAIRS, max_val=MAX_PAIRS)
            last_pair = pe.value_load(pairs_i[0:1, 2:3], min_val=MIN_PAIRS - 1, max_val=MAX_PAIRS - 1)
            pe.wait_ge(ident_made, 1)
            pe.wait_ge(consts_in, 16 * CONST_DMAS)
            for stage in range(LAYERS):
                with pe.Fori(0, ROUNDS) as r:
                    v = r + (1 + stage * ROUNDS)
                    pe.wait_ge(n_ready, v)
                    for j in range(NB):
                        last = pe.transpose(hT_ps[:, j * P:(j + 1) * P], (n_x if stage == 0 else n_h)[:, j, :], ident[:, :])
                    last.then_inc(n_T, 1)
                    pe.wait_ge(n_Tc, v)
                    for j in range(NB):
                        last = pe.matmul(lr_ps[:, j * 2 * F:(j + 1) * 2 * F], n_hT[:, j * P:(j + 1) * P], w_lr[:, stage, :],
                                         start=True, stop=True)
                    last.then_inc(n_prod, 1)

                def pe_step(opens, closes):
                    def expand(g):
                        q, v, use = opens
                        if g == 0:
                            pe.wait_ge(item_loaded[q], use * (16 * ITEM_DMAS))
                        pe.wait_ge(onehotT_done[g], v)
                        if g >= 2:
                            pe.wait_ge(z_done[g - 2], v)
                        for n, t in enumerate(GROUPS[g]):
                            last = pe.matmul(zp[(q + g) % 2][:, n, :], ST[:, t, :], xr_w[:, q, :], start=True, stop=True)
                        last.then_inc(expanded[g], 1)

                    def close(part):
                        q, v, use = closes
                        if part == "rows":
                            pe.wait_ge(logit_done[NG - 1], v * 3)
                            pe.transpose(lt_ps, logit[:, q, :], ident[:, :]).then_inc(logitT_done, 1)
                        if part == "open":
                            pe.wait_ge(runs_done, v)
                            pe.matmul(open_ps[0], run_up[:, P - 1:P], ident[0:LH, 0:LH], start=True, stop=True)
                            pe.matmul(open_ps[1], run_down[:, 0:1], ident[0:LH, 0:LH], start=True, stop=True).then_inc(open_done, 1)
                        if part == "carry":
                            pe.wait_ge(carry_done, v)
                            pe.matmul(carry_ps[:, 0:1], carry[:, 0, :], ones[:, 0:1], start=True, stop=True)
                            pe.matmul(carry_ps[:, 1:2], carry[:, 1, :], ones[:, 0:1], start=True, stop=True).then_inc(carryT_done, 1)
                        if part == "max":
                            pe.wait_ge(segmax_done, v)
                            pe.transpose(mb_ps, seg_max[:, :], ident[0:LH, 0:LH]).then_inc(segmaxT_done, 1)

                    def sums(g):
                        q, v, use = closes
                        pe.wait_ge(onehot_done[g], v * 2)
                        pe.wait_ge(msg_done[g], v + 2)
                        for t in GROUPS[g]:
                            last = pe.matmul(agg_ps, S[:, q, t, :], msg[:, t, :], start=t == 0, stop=t == TILES - 1)
                            if stage == 0:
                                if t == 0:
                                    pe.wait_ge(ea_loaded[q], use * 16)
                                last = pe.matmul(ea_ps, S[:, q, t, :], ea[:, q, t, :], start=t == 0, stop=t == TILES - 1)
                        if g == NG - 1:
                            last.then_inc(agg_done, 1)

                    if closes:
                        close("rows")
                    for g in range(NG):
                        if opens and g == 0:
                            expand(0)
                            expand(1)
                        elif opens and g >= 2:
                            expand(g)
                        if closes and g == 0:
                            close("open")
                        if closes and g == 1:
                            close("carry")
                        if closes and g == 2:
                            close("max")
                        if closes:
                            for m in SUMS_AT.get(g - 1, ()):
                                sums(m)

                pipeline(pe, stage, pairs, last_pair, pe_step)

            for h in range(2):
                last = pe.matmul(PS[:, 4, h:h + 1], w1_u[:, h * P:(h + 1) * P], u_col[:, :], start=True, stop=True)
            last.then_inc(hid_bias, 1)
            pe.wait_ge(hid_b, 1)
            with pe.Fori(0, ROUNDS) as r:
                v = r + 1
                pe.wait_ge(x1_ready, v)
                for j in range(NB):
                    pe.transpose(hT_ps[:, j * P:(j + 1) * P], n_d[:, j, :], ident[:, :])
                for j in range(NB):
                    last = pe.transpose(eT_ps[:, j * P:(j + 1) * P], n_e[:, j, :], ident[:, :])
                last.then_inc(e_T, 1)
                pe.wait_ge(e_Tc, v)
                for h in range(2):
                    for m in range(2):
                        cut = slice(m * (NROWS // 2), (m + 1) * (NROWS // 2))
                        pe.matmul(PS[:, 4 + 2 * h + m, 0:NROWS // 2], w1_x[:, h * P:(h + 1) * P], n_hT[:, cut], start=True, stop=False)
                        last = pe.matmul(PS[:, 4 + 2 * h + m, 0:NROWS // 2], w1_e[:, h * P:(h + 1) * P], n_eT[:, cut], start=False, stop=True)
                last.then_inc(hid_ps, 1)
                pe.wait_ge(hid_done, v)
            with pe.Fori(0, ROUNDS) as r:
                pe.wait_ge(act_done, r + 1)
                for j in range(NB):
                    for h in range(2):
                        last = pe.matmul(out_ps[:, j * F:(j + 1) * F], hid_relu[:, h, j * P:(j + 1) * P], w2_s[:, h, :],
                                         start=h == 0, stop=h == 1)
                last.then_inc(out_mm, 1)
                pe.wait_ge(out_read, r + 1)

        @block.scalar
        def _(act):
            act.wait_ge(table_made, 1)
            pairs = act.value_load(pairs_i[0:1, 1:2], min_val=MIN_PAIRS, max_val=MAX_PAIRS)
            last_pair = act.value_load(pairs_i[0:1, 2:3], min_val=MIN_PAIRS - 1, max_val=MAX_PAIRS - 1)
            for stage in range(LAYERS):
                with act.Fori(0, ROUNDS) as r:
                    v = r + (1 + stage * ROUNDS)
                    if stage > 0:
                        act.wait_ge(n_var, r + (1 + (stage - 1) * ROUNDS))
                        act.activation(n_c[:, 3, :], n_c[:, 2, :], ACT.Sqrt).then_inc(n_std, 1)
                    act.wait_ge(n_T, v)
                    act.copy(n_hT[:, :], hT_ps).then_inc(n_Tc, 1)
                def act_step(opens, closes):
                    def onehot(g):
                        q, v, use = opens
                        n = len(GROUPS[g])
                        if g == 0:
                            act.wait_ge(item_loaded[q], use * (16 * ITEM_DMAS))
                            act.wait_ge(negdst_done, v)
                        for m, t in enumerate(GROUPS[g]):
                            last = act.activation(dist[:, (q + g) % 2, m, :], node_row[:, q, :], ACT.Abs, bias=neg_dst[:, q, t:t + 1])
                        last.then_inc(onehot_done[g], 1)
                        act.wait_ge(onehot_done[g], v * 2 - 1)
                        act.activation(S[:, q, GROUPS[g][0]:GROUPS[g][0] + n, :], dist[:, (q + g) % 2, 0:n, :], ACT.Relu, bias=1.0, scale=-1.0)\
                            .then_inc(onehot_done[g], 1)

                    if opens:
                        onehot(0)
                        onehot(1)
                    if closes:
                        act.wait_ge(shifted_done, closes[1])
                        act.activation(msg[:, :, M_ALPHA:M_ONE], shifted[:, :].rearrange("p (t h) -> p t h", h=HEADS), ACT.Exp)\
                            .then_inc(alpha_done, 1)
                    if opens:
                        for g in range(2, NG):
                            onehot(g)
                    if closes:
                        act.wait_ge(dmax_done, closes[1])
                        act.activation(rescale[:, :, :], dmax[:, :, :], ACT.Exp).then_inc(rescale_done, 1)

                pipeline(act, stage, pairs, last_pair, act_step)
            with act.Fori(0, ROUNDS) as r:
                v = r + 1
                act.wait_ge(n_var, r + (1 + (LAYERS - 1) * ROUNDS))
                act.activation(n_c[:, 3, :], n_c[:, 2, :], ACT.Sqrt).then_inc(n_std, 1)
                act.wait_ge(x1_var, v)
                act.activation(n_c[:, 7, :], n_c[:, 6, :], ACT.Sqrt).then_inc(x1_std, 1)
                act.wait_ge(e_T, v)
                act.copy(n_hT[:, :], hT_ps)
                act.copy(n_eT[:, :], eT_ps).then_inc(e_Tc, 1)
                act.wait_ge(hid_ps, v)
                for h in range(2):
                    for m in range(2):
                        last = act.activation(hid[h][:, bass.ds(r * NROWS + m * (NROWS // 2), NROWS // 2)],
                                              PS[:, 4 + 2 * h + m, 0:NROWS // 2], ACT.Identity, bias=bn[:, 0, h:h + 1])
                last.then_inc(hid_done, 1)
            act.wait_ge(mu_done, 1)
            full = (ROUNDS - 1) * NROWS
            for h in range(2):
                for m in range(3):
                    if h or m:
                        act.wait_ge(sq_done, 3 * h + m)
                    if m < 2:
                        a = act.activation(squares[:, 0:full // 2], hid[h][:, m * (full // 2):(m + 1) * (full // 2)], ACT.Square,
                                           bias=bn[:, 1, h:h + 1], accum_out=bn_sum[:, h, m:m + 1])
                    else:
                        a = act.activation(squares[:, 0:NB * LAST_P].rearrange("p (j e) -> p j e", j=NB),
                                           hid[h][:, full:].rearrange("p (j e) -> p j e", j=NB)[:, :, 0:LAST_P], ACT.Square,
                                           bias=bn[:, 1, h:h + 1], accum_out=bn_sum[:, h, 2:3])
                    a.then_inc(sq_done, 1)
            act.wait_ge(bn_var, 1)
            act.activation(bn[:, 4, :], bn[:, 3, :], ACT.Sqrt).then_inc(bn_std, 1)
            act.wait_ge(bn_done, 1)
            with act.Fori(0, ROUNDS) as r:
                for h in range(2):
                    last = act.activation(hid_relu[:, h, :], hid[h][:, bass.ds(r * NROWS, NROWS)], ACT.Relu, bias=bn[:, 6, h:h + 1], scale=bn[:, 5, h:h + 1])
                last.then_inc(act_done, 1)
                act.wait_ge(out_var, r + 1)
                act.activation(n_c[:, 3, :], n_c[:, 2, :], ACT.Sqrt).then_inc(out_std, 1)

        @block.vector
        def _(dve):
            ch = Chain(dve, setup)
            dve.memset(ones[:, :], 1.0).then_inc(ones_made, 1)
            ch.link(dve.memset(zero_row[:, :], 0.0))
            dve.wait_ge(lohi_in, 48)
            ch.link(dve.tensor_tensor(out=span[:, :], in0=lohi[:, 1, :], in1=lohi[:, 0, :], op=ALU.subtract))
            ch.link(dve.tensor_scalar(span[:, :], span[:, :], 7, None, ALU.arith_shift_right))
            ch.link(dve.tensor_scalar(nwin[:, :], span[:, :], 1.0, None, ALU.add))
            ch.link(dve.tensor_tensor_scan(tab_row[:, 0, :], nwin[:, :], zero_row[:, :], 0.0, ALU.add, ALU.add))
            ch.link(dve.tensor_tensor(out=nwin[:, :], in0=nwin[:, :], in1=tab_row[:, 0, :], op=ALU.subtract))
            ch.link(dve.tensor_copy(lo_f[:, :], lohi[:, 0, :]))
            ch.link(dve.scalar_tensor_tensor(tab_row[:, 1, :], nwin[:, :], float(P), lo_f[:, :], ALU.mult, ALU.add))
            assert ch.n == SETUP_ROW_STEPS, ch.n
            ch.link(dve.tensor_scalar(pairs_i[:, 0:1], tab_row[:, 0, N_CHUNKS - 1:N_CHUNKS], 1.0, None, ALU.add))
            ch.link(dve.tensor_scalar(pairs_i[:, 1:2], pairs_i[:, 0:1], 1, None, ALU.arith_shift_right))
            ch.link(dve.tensor_scalar(pairs_i[:, 2:3], pairs_i[:, 1:2], -1.0, None, ALU.add))
            dve.wait_ge(tab_bc, 1)
            dve.wait_ge(rows_made, 1)
            ch.link(dve.memset(past[:, 0:1], 1.0))
            ch.link(dve.tensor_scalar(past[:, 1:N_CHUNKS + 1], flat[:, 0:N_CHUNKS], k_col[:, 0:1], None, ALU.is_le))
            ch.link(dve.reduce_sum(item_f[:, 0:1], past[:, 1:N_CHUNKS + 1], axis=AX.X))
            ch.link(dve.tensor_tensor(out=own[:, :], in0=past[:, 0:N_CHUNKS], in1=past[:, 1:N_CHUNKS + 1], op=ALU.subtract))
            ch.link(dve.tensor_tensor(out=own[:, :], in0=own[:, :], in1=flat[:, N_CHUNKS:2 * N_CHUNKS], op=ALU.mult))
            ch.link(dve.reduce_sum(item_f[:, 1:2], own[:, :], axis=AX.X))
            ch.link(dve.scalar_tensor_tensor(item_f[:, 1:2], k_col[:, 0:1], float(P), item_f[:, 1:2], ALU.mult, ALU.add))
            ch.link(dve.tensor_scalar(item_f[:, 2:3], past[:, N_CHUNKS:N_CHUNKS + 1], -1.0, 1.0, ALU.mult, ALU.add))
            ch.link(dve.tensor_tensor(out=item_i[:, 0:1], in0=item_f[:, 0:1], in1=item_f[:, 2:3], op=ALU.mult))
            ch.link(dve.tensor_scalar(item_f[:, 3:4], item_f[:, 1:2], -float(EMPTY_BASE), item_f[:, 2:3], ALU.add, ALU.mult))
            ch.link(dve.tensor_scalar(item_i[:, 1:2], item_f[:, 3:4], float(EMPTY_BASE), None, ALU.add))
            dve.memset(row_pen[:, :], 0.0)
            dve.memset(tile_eq[:, :], 0.0)
            dve.memset(open_max[:, :, :], -BIG)
            dve.memset(msg[:, :, M_ONE:M_MAX], 1.0).then_inc(table_made, 1)
            dve.wait_ge(table_made, 1)
            pairs = dve.value_load(pairs_i[0:1, 1:2], min_val=MIN_PAIRS, max_val=MAX_PAIRS)
            last_pair = dve.value_load(pairs_i[0:1, 2:3], min_val=MIN_PAIRS - 1, max_val=MAX_PAIRS - 1)
            dve.wait_ge(ident_made, 1)
            dve.wait_ge(consts_in, 16 * CONST_DMAS)
            dve.tensor_scalar(att_relu[:, :, :], att_b[:, :, :], 1.0 - SLOPE, None, ALU.mult)
            ch.link(dve.tensor_scalar(att_lin[:, :, :], att_b[:, :, :], SLOPE, None, ALU.mult))

            def normalize(n, y, col, var_sem, std_sem, v):
                n.link(dve.reduce_sum(n_c[:, col, :], y, axis=AX.X))
                n.link(dve.tensor_scalar(n_c[:, col + 1, :], n_c[:, col, :], -1.0 / F, None, ALU.mult))
                n.link(dve.tensor_tensor(out=n_d[:, :, :], in0=y, in1=over_features(n_c[:, col + 1, :]), op=ALU.add))
                n.link(dve.tensor_tensor(out=n_t[:, :, :], in0=n_d[:, :, :], in1=n_d[:, :, :], op=ALU.mult))
                n.link(dve.reduce_sum(n_c[:, col, :], n_t[:, :, :], axis=AX.X))
                dve.tensor_scalar(n_c[:, col + 2, :], n_c[:, col, :], 1.0 / F, EPS, ALU.mult, ALU.add).then_inc(var_sem, 1)
                dve.wait_ge(std_sem, v)
                n.link(dve.reciprocal(n_c[:, col + 1, :], n_c[:, col + 3, :]))
                n.link(dve.tensor_tensor(out=n_d[:, :, :], in0=n_d[:, :, :], in1=over_features(n_c[:, col + 1, :]), op=ALU.mult))

            def finish_layer(n, l, v):
                n.link(dve.reciprocal(n_rd[:, :, :], n_st[:, :, C_DEN:C_DEN + HEADS]))
                n.link(dve.tensor_tensor(out=n_h[:, :, :].rearrange("p j (h f) -> p j h f", h=HEADS),
                                         in0=n_st[:, :, C_ACC:C_ACC + F].rearrange("p j (h f) -> p j h f", h=HEADS),
                                         in1=n_rd[:, :, :].unsqueeze(3).to_broadcast([P, NB, HEADS, F // HEADS]), op=ALU.mult))
                n.link(dve.tensor_tensor(out=n_h[:, :, :], in0=n_h[:, :, :], in1=over_blocks(c_b[:, l, :]), op=ALU.add))
                normalize(n, n_h[:, :, :], 0, n_var, n_std, v)
                n.link(dve.tensor_tensor(out=n_d[:, :, :], in0=n_d[:, :, :], in1=over_blocks(g_b[:, l, :]), op=ALU.mult))
                n.link(dve.tensor_tensor(out=n_d[:, :, :], in0=n_d[:, :, :], in1=over_blocks(be_b[:, l, :]), op=ALU.add))

            def transform(n, stage, r):
                v = r + (1 + stage * ROUNDS)
                dve.wait_ge(n_prod, v)
                dve.wait_ge(n_stored, v * stored_value)
                n.link(dve.tensor_tensor(out=n_lr[:, :, :, 0:F], in0=lr_ps.rearrange("p (j s f) -> p j s f", j=NB, s=2),
                                         in1=b_lr[:, stage, :].rearrange("p (s f) -> p s f", s=2).unsqueeze(1).to_broadcast([P, NB, 2, F]),
                                         op=ALU.add))
                dve.tensor_tensor(out=n_t[:, :, :], in0=n_lr[:, :, 0, 0:F], in1=n_lr[:, :, 1, 0:F], op=ALU.add)
                n.link(dve.tensor_tensor(out=n_q[:, :, :, :].rearrange("p j s f -> p (j s) f"),
                                         in0=n_lr[:, :, :, 0:F].rearrange("p j s f -> p (j s) f"),
                                         in1=att_lin[:, stage, :].unsqueeze(1).to_broadcast([P, 2 * NB, F]), op=ALU.mult))
                n.link(dve.scalar_tensor_tensor(n_d[:, :, :], n_t[:, :, :], 0.0, over_blocks(att_relu[:, stage, :]), ALU.max, ALU.mult))
                dve.tensor_copy(n_new[:, :, C_ACC:C_ACC + F], n_lr[:, :, 0, 0:F])
                dve.memset(n_new[:, :, C_DEN:C_DEN + HEADS], 1.0)
                if stage == 0:
                    dve.memset(n_new[:, :, C_CNT:ROW], 0.0)
                lin = n_lr[:, :, :, F:XW]
                if stage < LAYERS - 1:
                    dve.reduce_sum(lin.rearrange("p j s h -> p (j s) h"),
                                   n_q[:, :, :, :].rearrange("p j s (h f) -> p (j s) h f", h=HEADS), axis=AX.X)
                    n.link(dve.reduce_sum(n_rd[:, :, :], n_d[:, :, :].rearrange("p j (h f) -> p j h f", h=HEADS), axis=AX.X))
                    relu_part = n_rd[:, :, :]
                else:
                    dve.reduce_sum(n_l1[:, :], n_q[:, :, :, :].rearrange("p j s f -> p (j s) f"), axis=AX.X)
                    n.link(dve.reduce_sum(n_c[:, 0, :], n_d[:, :, :], axis=AX.X))
                    n.link(dve.tensor_copy(lin.rearrange("p j s h -> p (j s) h"), n_l1[:, :].unsqueeze(2).to_broadcast([P, 2 * NB, HEADS])))
                    relu_part = over_features(n_c[:, 0, :], HEADS)
                n.link(dve.tensor_tensor(out=n_m[:, :, :], in0=relu_part, in1=lin[:, :, 0, :], op=ALU.add))
                dve.tensor_tensor(out=n_new[:, :, 0:HEADS], in0=n_m[:, :, :], in1=lin[:, :, 1, :], op=ALU.add).then_inc(n_made, 1)

            def edge_step(stage, opens, closes):
                def onehotT(g):
                    q, v, use = opens
                    a, n = GROUPS[g][0], len(GROUPS[g])
                    if g == 0:
                        dve.wait_ge(item_loaded[q], use * (16 * ITEM_DMAS))
                        dve.tensor_scalar(neg_dst[:, q, :], dst_e[:, q, :], -1.0, None, ALU.mult).then_inc(negdst_done, 1)
                    dve.tensor_scalar(ST[:, a:a + n, :].rearrange("p t e -> p (t e)"), dst_b[:, q, a * P:(a + n) * P],
                                      node_col[:, q, 0:1], None, ALU.is_equal).then_inc(onehotT_done[g], 1)

                def add_transforms(g):
                    q, v, use = opens
                    a, n = GROUPS[g][0], len(GROUPS[g])
                    dve.wait_ge(expanded[g], v)
                    dve.wait_ge(gathered[q][g], use * (16 * n))
                    dve.tensor_tensor(out=z[:, (q + g) % 2, 0:n, :], in0=zp[(q + g) % 2][:, 0:n, :], in1=xl_g[:, q, a:a + n, :],
                                      op=ALU.add).then_inc(z_done[g], 1)

                def relu_att(g):
                    q, v, use = opens
                    n = len(GROUPS[g])
                    dve.wait_ge(z_done[g], v)
                    dve.scalar_tensor_tensor(am[:, (q + g) % 2, 0:n, :], z[:, (q + g) % 2, 0:n, 0:F], 0.0,
                                             att_relu[:, stage, :].unsqueeze(1).to_broadcast([P, n, F]), ALU.max, ALU.mult)\
                        .then_inc(logit_done[g], 1)

                def sum_heads(g):
                    q, v, use = opens
                    a, n = GROUPS[g][0], len(GROUPS[g])
                    dve.wait_ge(logit_done[g], v * 3 - 2)
                    if stage < LAYERS - 1:
                        s = dve.reduce_sum(relu_logit[:, a * HEADS:(a + n) * HEADS],
                                           am[:, (q + g) % 2, 0:n, :].rearrange("p t (h f) -> p (t h) f", h=HEADS), axis=AX.X)
                    else:
                        s = dve.reduce_sum(relu_logit[:, a:a + n], am[:, (q + g) % 2, 0:n, :], axis=AX.X)
                    s.then_inc(logit_done[g], 1)

                def add_linear(g):
                    q, v, use = opens
                    a, n = GROUPS[g][0], len(GROUPS[g])
                    dve.wait_ge(logit_done[g], v * 3 - 1)
                    if stage < LAYERS - 1:
                        part = relu_logit[:, a * HEADS:(a + n) * HEADS].rearrange("p (t h) -> p t h", h=HEADS)
                    else:
                        part = relu_logit[:, a:a + n].unsqueeze(2).to_broadcast([P, n, HEADS])
                    dve.tensor_tensor(out=by_tile(logit[:, q, :])[:, a:a + n, :], in0=part, in1=z[:, (q + g) % 2, 0:n, F:XW],
                                      op=ALU.add).then_inc(logit_done[g], 1)

                def flags():
                    q, v, use = opens
                    first, last = tile_ends[:, q, :, 0], tile_ends[:, q, :, 1]
                    dve.tensor_tensor(out=row_eq[:, 1:P], in0=dst_r[:, q, 1:P], in1=dst_r[:, q, 0:P - 1], op=ALU.is_equal).then_inc(flag_done[0], 1)
                    dve.tensor_tensor(out=seg_last[:, :], in0=dst_e[:, q, :], in1=dst_next[:, q, :], op=ALU.not_equal).then_inc(flag_done[1], 1)
                    dve.tensor_tensor(out=tile_eq[:, 1:TILES], in0=first[:, 1:TILES], in1=last[:, 0:TILES - 1], op=ALU.is_equal).then_inc(flag_done[2], 1)
                    dve.tensor_tensor(out=tile_one[:, :], in0=first, in1=last, op=ALU.is_equal).then_inc(flag_done[3], 1)
                    dve.wait_ge(flag_done[0], v)
                    dve.tensor_scalar(row_pen[:, 1:P], row_eq[:, 1:P], -1.0, BIG, ALU.add, ALU.mult)
                    dve.wait_ge(flag_done[1], v)
                    dve.tensor_scalar(seg_last[:, TILES - 1:TILES], seg_last[:, TILES - 1:TILES], ident[:, P - 1:P], None, ALU.max).then_inc(flag_done[4], 1)
                    dve.wait_ge(flag_done[3], v)
                    for d in range(2):
                        w = dve.tensor_tensor(out=through[:, d, :], in0=tile_eq[:, d:d + TILES], in1=tile_one[:, :], op=ALU.mult)
                    w.then_inc(flag_done[5], 1)
                    per_head = [1, HEADS, TILES]
                    for d in range(2):
                        dve.tensor_scalar(enter_pen[:, d, :].rearrange("a (h t) -> a h t", h=HEADS),
                                          tile_eq[:, d:d + TILES].unsqueeze(1).to_broadcast(per_head), -1.0, BIG, ALU.add, ALU.mult)
                    dve.wait_ge(flag_done[5], v)
                    for d in range(2):
                        w = dve.tensor_scalar(through_pen[:, d, :].rearrange("a (h t) -> a h t", h=HEADS),
                                              through[:, d, :].unsqueeze(1).to_broadcast(per_head), -1.0, BIG, ALU.add, ALU.mult)
                    w.then_inc(flag_done[6], 1)

                def runs():
                    q, v, use = closes
                    dve.wait_ge(logitT_done, v)
                    dve.wait_ge(flag_done[6], v)
                    dve.tensor_tensor_scan(run_up[:, :], row_pen[:, 0:P], lt_ps, -BIG, ALU.add, ALU.max)
                    dve.tensor_tensor_scan(run_down[:, ::-1], row_pen[:, 1:P + 1][:, ::-1], lt_ps[:, ::-1], -BIG, ALU.add, ALU.max)\
                        .then_inc(runs_done, 1)

                def carries():
                    q, v, use = closes
                    dve.wait_ge(open_done, v)
                    dve.tensor_tensor_scan(open_max[:, 0, 1:LH + 1], through_pen[:, 0, :], open_ps[0], -BIG, ALU.add, ALU.max)
                    dve.tensor_tensor_scan(open_max[:, 1, 1:LH + 1][:, ::-1], through_pen[:, 1, :][:, ::-1], open_ps[1][:, ::-1], -BIG,
                                           ALU.add, ALU.max).then_inc(openmax_done, 1)
                    dve.wait_ge(openmax_done, v)
                    dve.tensor_tensor(out=carry[:, 0, :], in0=open_max[:, 0, 0:LH], in1=enter_pen[:, 0, :], op=ALU.add)
                    dve.tensor_tensor(out=carry[:, 1, :], in0=open_max[:, 1, 2:LH + 2], in1=enter_pen[:, 1, :], op=ALU.add).then_inc(carry_done, 1)

                def maxima():
                    q, v, use = closes
                    dve.wait_ge(carryT_done, v)
                    dve.tensor_copy(carry_col[:, :], carry_ps).then_inc(carrycol_done, 1)
                    dve.wait_ge(carrycol_done, v)
                    dve.tensor_tensor_scan(up[:, :], row_pen[:, 0:P], lt_ps, carry_col[:, 0:1], ALU.add, ALU.max).then_inc(up_done, 1)
                    dve.wait_ge(up_done, v)
                    dve.tensor_tensor_scan(seg_max[:, ::-1], row_pen[:, 1:P + 1][:, ::-1], up[:, ::-1], carry_col[:, 1:2], ALU.add, ALU.max)\
                        .then_inc(segmax_done, 1)

                def shift():
                    q, v, use = closes
                    dve.wait_ge(segmaxT_done, v)
                    dve.tensor_tensor(out=shifted[:, :].rearrange("p (t h) -> p t h", h=HEADS), in0=by_tile(logit[:, q, :]),
                                      in1=by_tile(mb_ps), op=ALU.subtract).then_inc(shifted_done, 1)
                    dve.tensor_tensor(out=msg[:, :, M_MAX:MSG], in0=by_tile(mb_ps),
                                      in1=seg_last[:, :].unsqueeze(2).to_broadcast([P, TILES, HEADS]), op=ALU.mult)

                def message(g):
                    q, v, use = closes
                    a, n = GROUPS[g][0], len(GROUPS[g])
                    if g == 0:
                        dve.wait_ge(alpha_done, v)
                    dve.tensor_tensor(out=msg[:, a:a + n, 0:F].rearrange("p t (h f) -> p t h f", h=HEADS),
                                      in0=xl_g[:, q, a:a + n, 0:F].rearrange("p t (h f) -> p t h f", h=HEADS),
                                      in1=msg[:, a:a + n, M_ALPHA:M_ONE].unsqueeze(3).to_broadcast([P, n, HEADS, F // HEADS]),
                                      op=ALU.mult).then_inc(msg_done[g], 1)

                def new_max():
                    q, v, use = closes
                    dve.wait_ge(agg_done, v)
                    dve.tensor_scalar(some[:, :], agg_ps[:, M_ONE:M_MAX], 1.0, None, ALU.min).then_inc(some_done, 1)
                    dve.wait_ge(some_done, v)
                    dve.tensor_scalar(none_pen[:, :], some[:, :], -1.0, BIG, ALU.add, ALU.mult).then_inc(none_done, 1)
                    dve.wait_ge(none_done, v)
                    dve.tensor_scalar(chunk_max[:, :], agg_ps[:, M_MAX:MSG], none_pen[:, 0:1], None, ALU.add).then_inc(chunkmax_done, 1)
                    dve.wait_ge(chunkmax_done, v)
                    dve.wait_ge(state_loaded[q], use * 16)
                    dve.tensor_tensor(out=st_new[:, q, 0:HEADS], in0=chunk_max[:, :], in1=st_old[:, q, 0:HEADS], op=ALU.max).then_inc(newmax_done, 1)
                    dve.wait_ge(newmax_done, v)
                    dve.tensor_tensor(out=dmax[:, 0, :], in0=st_old[:, q, 0:HEADS], in1=st_new[:, q, 0:HEADS], op=ALU.subtract)
                    dve.tensor_tensor(out=dmax[:, 1, :], in0=chunk_max[:, :], in1=st_new[:, q, 0:HEADS], op=ALU.subtract).then_inc(dmax_done, 1)

                def new_state():
                    q, v, use = closes
                    dve.wait_ge(rescale_done, v)
                    for w, (row, f) in enumerate(((st_old[:, q, C_ACC:C_CNT], rescale[:, 0, :]), (agg_ps[:, 0:F + HEADS], rescale[:, 1, :]))):
                        dve.tensor_tensor(out=scaled[:, w, 0:F].rearrange("p (h f) -> p h f", h=HEADS),
                                          in0=row[:, 0:F].rearrange("p (h f) -> p h f", h=HEADS),
                                          in1=f.unsqueeze(2).to_broadcast([P, HEADS, F // HEADS]), op=ALU.mult)
                        last = dve.tensor_tensor(out=scaled[:, w, F:F + HEADS], in0=row[:, F:F + HEADS], in1=f, op=ALU.mult)
                    last.then_inc(scaled_done, 1)
                    if stage == 0:
                        dve.tensor_tensor(out=st_new[:, q, C_CNT:C_EA], in0=st_old[:, q, C_CNT:C_EA], in1=agg_ps[:, M_ONE:M_MAX], op=ALU.add)
                        dve.tensor_tensor(out=st_new[:, q, C_EA:ROW], in0=st_old[:, q, C_EA:ROW], in1=ea_ps, op=ALU.add)
                    dve.wait_ge(scaled_done, v)
                    dve.tensor_tensor(out=st_new[:, q, C_ACC:C_CNT], in0=scaled[:, 0, :], in1=scaled[:, 1, :], op=ALU.add).then_inc(item_done, 1)

                if opens:
                    onehotT(0)
                    onehotT(1)
                for g in range(NG):
                    if closes and g == 0:
                        runs()
                    if closes and g == 1:
                        carries()
                    if opens:
                        add_transforms(g)
                        if g:
                            add_linear(g - 1)
                    if closes and g == 2:
                        shift()
                    if opens:
                        relu_att(g)
                    if closes and g == 1:
                        maxima()
                    if closes and g == 6:
                        new_max()
                    if opens:
                        if g + 2 < NG:
                            onehotT(g + 2)
                        if g == 4:
                            flags()
                        sum_heads(g)
                    if closes:
                        for m in SUMS_AT.get(g, ()):
                            message(m)
                if opens:
                    add_linear(NG - 1)
                if closes:
                    new_state()

            for stage in range(LAYERS):
                with dve.Fori(0, ROUNDS) as r:
                    n = Chain(dve, n_step[stage], r * NODE_STEPS[stage])
                    if stage == 0:
                        dve.wait_ge(x_loaded, r * 16 + 16)
                        dve.memset(n_c[:, 7, :], 0.0).then_inc(n_ready, 1)
                    else:
                        dve.wait_ge(st_loaded, (r + (1 + (stage - 1) * ROUNDS)) * 16)
                        finish_layer(n, stage - 1, r + (1 + (stage - 1) * ROUNDS))
                        dve.tensor_scalar(n_h[:, :, :], n_d[:, :, :], 0.0, None, ALU.max).then_inc(n_ready, 1)
                    transform(n, stage, r)
                    assert n.n == NODE_STEPS[stage], (stage, n.n)
                pipeline(dve, stage, pairs, last_pair, lambda opens, closes: edge_step(stage, opens, closes))

            dve.wait_ge(hid_bias, 1)
            dve.tensor_tensor(out=bn[:, 0, :], in0=PS[:, 4, 0:2], in1=cols1[:, 0, :], op=ALU.add).then_inc(hid_b, 1)
            with dve.Fori(0, ROUNDS) as r:
                v = r + 1
                n = Chain(dve, n_step[LAYERS], r * NODE_STEPS[LAYERS])
                dve.wait_ge(st_loaded, (r + (1 + (LAYERS - 1) * ROUNDS)) * 16)
                finish_layer(n, LAYERS - 1, r + (1 + (LAYERS - 1) * ROUNDS))
                dve.wait_ge(x_loaded, (r + (1 + ROUNDS)) * 16)
                n.link(dve.scalar_tensor_tensor(n_h[:, :, :], n_d[:, :, :], 0.0, n_x[:, :, :], ALU.max, ALU.add))
                normalize(n, n_h[:, :, :], 4, x1_var, x1_std, v)
                dve.tensor_copy(x1[:, bass.ds(r * NB, NB), :], n_d[:, :, :])
                n.link(dve.tensor_scalar(n_c[:, 0, :], n_st[:, :, C_CNT], 1.0, None, ALU.max))
                n.link(dve.reciprocal(n_c[:, 1, :], n_c[:, 0, :]))
                dve.tensor_tensor(out=n_e[:, :, :], in0=n_st[:, :, C_EA:ROW], in1=over_features(n_c[:, 1, :], D_EDGE), op=ALU.mult)\
                    .then_inc(x1_ready, 1)
                dve.wait_ge(x1_ready, v)
                dve.memset(n_c[:, 2, :], 0.0).then_inc(hid_in, 1)
                dve.wait_ge(hid_done, v)
                assert n.n == NODE_STEPS[LAYERS], n.n

            ch = Chain(dve, o_step[0])
            full = (ROUNDS - 1) * NROWS
            for h in range(2):
                dve.reduce_sum(bn_sum[:, h, 0:1], hid[h][:, 0:full], axis=AX.X)
                ch.link(dve.reduce_sum(bn_sum[:, h, 1:2], hid[h][:, full:].rearrange("p (j e) -> p j e", j=NB)[:, :, 0:LAST_P], axis=AX.XY))
            ch.link(dve.tensor_tensor(out=bn[:, 2, :], in0=bn_sum[:, :, 0], in1=bn_sum[:, :, 1], op=ALU.add))
            dve.tensor_scalar(bn[:, 1, :], bn[:, 2, :], -1.0 / N_NODES, None, ALU.mult).then_inc(mu_done, 1)
            dve.wait_ge(sq_done, 6)
            ch.link(dve.reduce_sum(bn[:, 2, :], bn_sum[:, :, 0:3], axis=AX.X))
            dve.tensor_scalar(bn[:, 3, :], bn[:, 2, :], 1.0 / N_NODES, EPS, ALU.mult, ALU.add).then_inc(bn_var, 1)
            dve.wait_ge(bn_std, 1)
            ch.link(dve.reciprocal(bn[:, 7, :], bn[:, 4, :]))
            ch.link(dve.tensor_tensor(out=bn[:, 5, :], in0=bn[:, 7, :], in1=cols1[:, 1, :], op=ALU.mult))
            ch.link(dve.tensor_tensor(out=bn[:, 2, :], in0=bn[:, 1, :], in1=bn[:, 5, :], op=ALU.mult))
            dve.tensor_tensor(out=bn[:, 6, :], in0=bn[:, 2, :], in1=cols1[:, 2, :], op=ALU.add).then_inc(bn_done, 1)

            with dve.Fori(0, ROUNDS) as r:
                v = r + 1
                n = Chain(dve, o_step[1], r * OUT_STEPS)
                dve.wait_ge(out_mm, v)
                n.link(dve.tensor_tensor(out=n_d[:, :, :], in0=out_ps.rearrange("p (j f) -> p j f", j=NB), in1=over_blocks(b2_b[:, :]), op=ALU.add))
                n.link(dve.tensor_tensor(out=n_x[:, :, :], in0=n_d[:, :, :], in1=x1[:, bass.ds(r * NB, NB), :], op=ALU.add))
                dve.memset(n_c[:, 7, :], 0.0).then_inc(out_read, 1)
                normalize(n, n_x[:, :, :], 0, out_var, out_std, v)
                dve.wait_ge(out_stored, r * 16 + 16)
                dve.tensor_copy(n_h[:, :, :], n_d[:, :, :]).then_inc(out_made, 1)
                dve.wait_ge(out_made, v)
                assert n.n == OUT_STEPS, n.n


_LAYER = {"Wl": "W{}l", "bl": "b{}l", "Wr": "W{}r", "br": "b{}r", "att": "a{}", "c": "c{}", "g": "g{}", "be": "be{}"}
_LAST = ("u", "W1", "b1", "gamma", "beta", "W2", "b2")


def kernel(**inputs):
    import numpy as np
    import concourse.bacc as bacc
    from concourse.bass_utils import run_bass_kernel_spmd

    nc = bacc.Bacc("TRN2", target_bir_lowering=False, num_devices=1)
    arrays = {}

    def given(name, a):
        arrays[name] = np.ascontiguousarray(a)
        return nc.dram_tensor(name, a.shape, mybir.dt.from_np(a.dtype), kind="ExternalInput").ap()

    def padded(a, rows, value):
        a = np.asarray(a)
        return np.concatenate([a, np.full((rows - a.shape[0],) + a.shape[1:], value, a.dtype)])

    def by_partition(flat):
        return flat.reshape((N_CHUNKS, TILES, P) + flat.shape[1:]).swapaxes(1, 2)

    dst = padded(inputs["dst"], E_PAD + 1, NO_NODE)
    args = {
        "x": given("x", padded(inputs["x"], N_PAD, 0)),
        "src_t": given("src_t", by_partition(padded(inputs["src"], E_PAD, 0))),
        "dst_t": given("dst_t", by_partition(dst[0:E_PAD])),
        "next_t": given("next_t", by_partition(dst[1:E_PAD + 1])),
        "dst": given("dst", dst[0:E_PAD].reshape(N_CHUNKS, TILES, P)),
        "edge_attr": given("edge_attr", by_partition(padded(inputs["edge_attr_96"], E_PAD, 0)).reshape(N_CHUNKS, P, TILES * D_EDGE)),
        "node_id": given("node_id", np.arange(N_PAD, dtype=np.float32)),
    }
    for key, name in _LAYER.items():
        args[key] = [given(f"{key}{l}", np.asarray(inputs["L0_gnn_" + name.format(l + 1)])) for l in range(LAYERS)]
    for key in _LAST:
        args[key] = given("last_" + key, np.asarray(inputs["L1_gnn_" + key]))
    args["out"] = nc.dram_tensor("out", (N_NODES, F), F32, kind="ExternalOutput").ap()
    gnn_program(nc, **args)
    r = run_bass_kernel_spmd(nc, [arrays], core_ids=[0])
    return r.results[0]["out"]
```

```python
import concourse.bass as bass
from concourse import mybir
from contextlib import ExitStack

F32 = mybir.dt.float32
I32 = mybir.dt.int32
BF16 = mybir.dt.bfloat16
ALU = mybir.AluOpType
ACT = mybir.ActivationFunctionType
AX = mybir.AxisListType

P = 128
N_NODES = 6250
N_EDGES = 206250
F = 128
HEADS = 4
D_EDGE = 96
D_GRAPH = 64
HIDDEN = 256
N_GRAPHS = 64
LAYERS = 3
EPS = 1e-5
SLOPE = 0.2
BIG = 1e30

TILES = 26
CHUNK = TILES * P
N_CHUNKS = -(-N_EDGES // CHUNK)
E_PAD = N_CHUNKS * CHUNK
LAST_EDGE = N_EDGES - 1 - (N_CHUNKS - 1) * CHUNK
NO_NODE = 100000
GROUPS = [range(a, min(a + 4, TILES)) for a in range(0, TILES, 4)]
NG = len(GROUPS)
SUMS_AT = {2: (0,), 3: (1, 2), 4: (3, 4), 5: (5, 6)}
EA_CUTS = (0, 4, 9, TILES)
LH = TILES * HEADS

NB = 5
NROWS = NB * P
ROUNDS = -(-(N_NODES + P) // NROWS)
N_PAD = ROUNDS * NROWS
EMPTY_BASE = N_PAD - P
LAST_P = (N_NODES - (ROUNDS - 1) * NROWS) // NB
assert LAST_P * NB == N_NODES - (ROUNDS - 1) * NROWS

MAX_ITEMS = N_CHUNKS + N_NODES // P
MAX_ITEMS += MAX_ITEMS % 2
MIN_PAIRS, MAX_PAIRS = N_CHUNKS // 2, MAX_ITEMS // 2
assert N_CHUNKS % 2 == 0

XW = F + HEADS

PARTS = 3

M_ALPHA, M_ONE, M_MAX = F, F + HEADS, F + HEADS + 1
MSG = M_MAX + HEADS

C_ACC, C_DEN, C_CNT, C_EA = HEADS, HEADS + F, 2 * HEADS + F, 2 * HEADS + F + 1
ROW_L = C_CNT
ROW = C_EA + D_EDGE

ITEM_DMAS = 7 + HEADS
SETUP_ROW_STEPS = 8


def gnn_program(nc, x, src_t, dst_t, next_t, dst, edge_attr, node_id, Wl, bl, Wr, br, att, c, g, be,
                u, W1, b1, gamma, beta, W2, b2, out):
    ctx = ExitStack()
    with ctx:
        def sb(name, shape, dt=F32):
            return ctx.enter_context(nc.sbuf_tensor(name, shape, dt))

        def sem(name):
            return ctx.enter_context(nc.semaphore(name))

        def sems(name, n):
            return [sem(f"{name}{i}") for i in range(n)]

        def scratch(name, shape, dt=F32):
            return nc.dram_tensor(name, shape, dt, kind="Internal").ap()

        xl_tab = scratch("xl_tab", (N_PAD, XW))
        xr_tab = scratch("xr_tab", (N_PAD, PARTS * XW), BF16)
        state = scratch("state", (N_PAD, ROW))
        item_tab = scratch("item_tab", (MAX_ITEMS, 2), I32)

        ident = sb("ident", [P, P])
        ones = sb("ones", [1, P])
        ones_h = sb("ones_h", [1, P], BF16)
        w_lr = sb("w_lr", [P, LAYERS, 2, XW])
        b_parts = sb("b_parts", [1, PARTS, LAYERS, 2, XW], BF16)
        att_b = sb("att_b", [P, LAYERS, F])
        att_relu = sb("att_relu", [P, LAYERS, F])
        att_lin = sb("att_lin", [P, LAYERS, F])
        c_b = sb("c_b", [P, LAYERS, F])
        g_col = sb("g_col", [P, LAYERS - 1])
        be_col = sb("be_col", [P, LAYERS - 1])
        g_b = sb("g_b", [P, F])
        be_b = sb("be_b", [P, F])
        w1_x = sb("w1_x", [P, HIDDEN])
        w1_e = sb("w1_e", [D_EDGE, HIDDEN])
        w1_u = sb("w1_u", [D_GRAPH, HIDDEN])
        u_col = sb("u_col", [D_GRAPH, 1])
        w2_s = sb("w2_s", [P, 2, F])
        b2_r = sb("b2_r", [1, F])
        b2_parts = sb("b2_parts", [1, PARTS, F], BF16)
        cols1 = sb("cols1", [P, 3, 2])

        lohi = sb("lohi", [1, 2, N_CHUNKS], I32)
        span = sb("span", [1, N_CHUNKS], I32)
        nwin = sb("nwin", [1, N_CHUNKS])
        zero_row = sb("zero_row", [1, N_CHUNKS])
        tab_row = sb("tab_row", [1, 2, N_CHUNKS])
        lo_f = sb("lo_f", [1, N_CHUNKS])
        pairs_i = sb("pairs_i", [1, 3], I32)
        k_col = sb("k_col", [P, 1])
        past = sb("past", [P, N_CHUNKS + 1])
        own = sb("own", [P, N_CHUNKS])
        item_f = sb("item_f", [P, 4])
        item_i = sb("item_i", [P, 2], I32)
        tab = sb("tab", [1, MAX_ITEMS * 2], I32)

        idx = sb("idx", [P, 2, TILES], I32)
        dst_e = sb("dst_e", [P, 2, TILES], I32)
        dst_next = sb("dst_next", [P, 2, TILES], I32)
        dst_r = sb("dst_r", [LH, 2, P], I32)
        tile_ends = sb("tile_ends", [1, 2, TILES, 2], I32)
        dst_b = sb("dst_b", [P, 2, CHUNK], I32)
        node_col = sb("node_col", [P, 2, 1])
        node_row = sb("node_row", [P, 2, P])
        xr_w = sb("xr_w", [P, 2, PARTS, XW], BF16)
        xl_g = sb("xl_g", [P, 2, TILES, XW])
        ea = sb("ea", [P, 2, TILES, D_EDGE])
        st_old = sb("st_old", [P, 2, ROW])
        st_new = sb("st_new", [P, 2, ROW])
        neg_dst = sb("neg_dst", [P, 2, TILES])
        dist = sb("dist", [P, 2, 4, P])
        S = sb("S", [P, 2, TILES, P])
        ST = sb("ST", [P, TILES, P], BF16)
        z = sb("z", [P, 2, 4, XW])
        am = sb("am", [P, 2, 4, F])
        relu_logit = sb("relu_logit", [P, LH])
        logit = sb("logit", [P, 2, LH])
        seg_last = sb("seg_last", [P, TILES])
        row_eq = sb("row_eq", [LH, P])
        row_pen = sb("row_pen", [LH, P + 1])
        tile_eq = sb("tile_eq", [1, TILES + 1])
        tile_one = sb("tile_one", [1, TILES])
        through = sb("through", [1, 2, TILES])
        through_pen = sb("through_pen", [1, 2, LH])
        enter_pen = sb("enter_pen", [1, 2, LH])
        run_up = sb("run_up", [LH, P])
        run_down = sb("run_down", [LH, P])
        open_max = sb("open_max", [1, 2, LH + 2])
        carry = sb("carry", [1, 2, LH])
        carry_col = sb("carry_col", [LH, 2])
        up = sb("up", [LH, P])
        seg_max = sb("seg_max", [LH, P])
        shifted = sb("shifted", [P, LH])
        msg = sb("msg", [P, TILES, MSG])
        some = sb("some", [P, 1])
        none_pen = sb("none_pen", [P, 1])
        chunk_max = sb("chunk_max", [P, HEADS])
        dmax = sb("dmax", [P, 2, HEADS])
        rescale = sb("rescale", [P, 2, HEADS])
        scaled = sb("scaled", [P, 2, F + HEADS])

        def blocks(flat, at, width=F):
            return flat[:, at:at + NB * width].rearrange("p (j f) -> p j f", j=NB)

        s_flat = S[:, :, :, :].rearrange("p a t n -> p (a t n)")
        xl_flat = xl_g[:, :, :, :].rearrange("p a t f -> p (a t f)")
        ea_flat = ea[:, :, :, :].rearrange("p a t f -> p (a t f)")
        msg_flat = msg[:, :, :].rearrange("p t n -> p (t n)")
        am_flat = am[:, :, :, :].rearrange("p a t f -> p (a t f)")
        z_flat = z[:, :, :, :].rearrange("p a t f -> p (a t f)")
        after_st = 2 * NB * ROW
        n_st = [blocks(ea_flat, q * NB * ROW, ROW) for q in range(2)]
        n_in = [blocks(ea_flat, after_st + q * NROWS) for q in range(2)]
        n_y = blocks(ea_flat, after_st + 2 * NROWS)
        n_sum = blocks(ea_flat, after_st + 3 * NROWS)
        n_junk = blocks(z_flat, 0)
        n_relu = blocks(am_flat, 0)
        n_lr = [xl_flat[:, q * NB * 2 * XW:(q + 1) * NB * 2 * XW].rearrange("p (j s f) -> p j s f", j=NB, s=2) for q in range(2)]
        n_rest = blocks(xl_flat, 2 * NB * 2 * XW, XW)
        n_xr = [s_flat[:, :].bitcast(BF16)[:, q * NB * PARTS * XW:(q + 1) * NB * PARTS * XW].rearrange("p (j s f) -> p j s f", j=NB, s=PARTS)
                for q in range(2)]
        n_new = sb("n_new", [P, 2, NB, ROW])
        n_hT = sb("n_hT", [P, NROWS])
        n_rd = sb("n_rd", [P, NB, HEADS])
        n_rs = sb("n_rs", [P, NB, HEADS])
        n_m = sb("n_m", [P, NB, HEADS])
        n_c = sb("n_c", [P, 6, NB])
        n_x = [blocks(msg_flat, q * NROWS) for q in range(2)]
        n_h = n_sum
        n_eT = sb("n_eT", [D_EDGE, NROWS])
        n_e = sb("n_e", [P, NB, D_EDGE])
        n_cnt = sb("n_cnt", [P, 2, NB])
        h_c = sb("h_c", [P, 6, NB])
        o_c = sb("o_c", [P, 2, 6, NB])
        x1 = s_flat[:, 0:ROUNDS * NB * F].rearrange("p (j f) -> p j f", f=F)
        hid = [xl_flat[:, 0:N_PAD],
               dst_b[:, :, :].rearrange("p a e -> p (a e)")[:, 0:N_PAD].bitcast(F32)]
        hid_relu = [ea_flat[:, q * 2 * NROWS:(q + 1) * 2 * NROWS].rearrange("p (h e) -> p h e", h=2) for q in range(2)]
        squares = msg_flat
        o_y = [blocks(msg_flat, q * NROWS) for q in range(2)]
        o_out = [blocks(msg_flat, (2 + q) * NROWS) for q in range(2)]
        b_lr = s_flat[0:1, F:F + LAYERS * 2 * XW].rearrange("a (l s f) -> a l s f", l=LAYERS, s=2)
        b_rest = s_flat[0:1, F + LAYERS * 2 * XW:F + 2 * LAYERS * 2 * XW]
        bn = sb("bn", [P, 8, 2])
        bn_sum = sb("bn_sum", [P, 2, 4])

        PS = ctx.enter_context(nc.psum_tensor("PS", [P, 8, 512], F32))
        flat = PS[:, :, :].rearrange("p b n -> p (b n)")
        zp = [flat[:, b * 1024:(b + 1) * 1024].rearrange("p (t f) -> p t f", t=4)[:, :, 0:XW] for b in range(2)]
        lt_ps = PS[0:LH, 4, 0:P]
        mb_ps = PS[:, 4, 128:128 + LH]
        open_ps = [PS[0:1, 4, 232 + d * LH:232 + (d + 1) * LH] for d in range(2)]
        carry_ps = PS[0:LH, 4, 440:442]
        agg_ps = PS[:, 5, 0:MSG]
        ea_ps = PS[:, 6, 0:D_EDGE]
        hT_ps = flat[:, 0:NROWS]
        eT_ps = flat[0:D_EDGE, 1024:1024 + NROWS]
        lr_ps = PS[:, 3:3 + NB, 0:2 * XW]
        out_ps = [flat[:, q * 1024:q * 1024 + NROWS] for q in range(2)]

        consts_in = sem("consts_in")
        ident_zero = sem("ident_zero")
        ident_made = sem("ident_made")
        ones_made = sem("ones_made")
        lohi_in = sem("lohi_in")
        tab_bc = sem("tab_bc")
        table_made = sem("table_made")
        table_out = sem("table_out")
        table_in = sem("table_in")
        setup = sem("setup")
        rows_made = sem("rows_made")

        idx_loaded = sems("idx_loaded", 2)
        item_loaded = sems("item_loaded", 2)
        ea_loaded = sems("ea_loaded", 2)
        state_loaded = sems("state_loaded", 2)
        state_stored = sem("state_stored")
        gathered = [sems(f"gathered{q}_", NG) for q in range(2)]
        gather_go = sem("gather_go")
        load_go = sem("load_go")
        negdst_done = sem("negdst_done")
        flag_done = sems("flag_done", 7)
        onehotT_done = sems("onehotT_done", NG)
        onehot_done = sems("onehot_done", NG)
        expanded = sems("expanded", NG)
        z_done = sems("z_done", NG)
        logit_done = sems("logit_done", NG)
        logitT_done = sem("logitT_done")
        runs_done = sem("runs_done")
        open_done = sem("open_done")
        openmax_done = sem("openmax_done")
        carry_done = sem("carry_done")
        carryT_done = sem("carryT_done")
        carrycol_done = sem("carrycol_done")
        up_done = sem("up_done")
        segmax_done = sem("segmax_done")
        segmaxT_done = sem("segmaxT_done")
        shifted_done = sem("shifted_done")
        alpha_done = sem("alpha_done")
        msg_done = sems("msg_done", NG)
        agg_done = sem("agg_done")
        merge_step = sem("merge_step")
        dmax_done = sem("dmax_done")
        rescale_done = sem("rescale_done")
        scaled_done = sem("scaled_done")
        item_done = sem("item_done")

        consts_made = sem("consts_made")
        x_loaded = sems("x_loaded", 2)
        st_loaded = sems("st_loaded", 2)
        n_stored = sems("n_stored", 2)
        ln_step = sem("ln_step")
        n_mean = sem("n_mean")
        n_sq = sem("n_sq")
        n_var = sem("n_var")
        n_std = sem("n_std")
        n_norm = sem("n_norm")
        n_T = sem("n_T")
        n_Tc = sem("n_Tc")
        n_prod = sem("n_prod")
        n_copied = sem("n_copied")
        logit_step = sem("logit_step")
        n_made = sem("n_made")
        split_step = sem("split_step")
        fx_loaded = sems("fx_loaded", 2)
        h_step = sem("h_step")
        h_mean = sem("h_mean")
        h_sq = sem("h_sq")
        h_var = sem("h_var")
        h_std = sem("h_std")
        x1_step = sem("x1_step")
        x1_ready = sem("x1_ready")
        bn_step = sem("bn_step")
        e_T = sem("e_T")
        e_Tc = sem("e_Tc")
        hid_ps = sem("hid_ps")
        hid_bias = sem("hid_bias")
        hid_done = sem("hid_done")
        hid_b = sem("hid_b")
        mu_done = sem("mu_done")
        sq_done = sem("sq_done")
        bn_var = sem("bn_var")
        bn_std = sem("bn_std")
        bn_done = sem("bn_done")
        act_done = sem("act_done")
        out_mm = sem("out_mm")
        o_step = sem("o_step")
        o_mean = sem("o_mean")
        o_sq = sem("o_sq")
        o_var = sem("o_var")
        o_std = sem("o_std")
        o_norm = sem("o_norm")
        out_made = sem("out_made")
        out_stored = sems("out_stored", 2)

        block = ctx.enter_context(nc.Block())

        NODE_STORES = 3
        CONST_DMAS = 6 * LAYERS + 2 * (LAYERS - 1) + 11
        LN_STEPS, LOGIT_STEPS, H_STEPS, X1_STEPS, O_STEPS, SPLIT_STEPS = 5, 4, 4, 3, 2, 3
        stored_value = 16 * NODE_STORES

        def rounds_of(ap, r):
            return ap[bass.ds(r * NROWS, NROWS), :].rearrange("(p j) f -> p j f", j=NB)

        def over_blocks(ap):
            return ap.unsqueeze(1).to_broadcast([P, NB, ap.shape[1]])

        def over_features(ap, n=F):
            return ap.unsqueeze(2).to_broadcast([P, NB, n])

        def by_tile(ap):
            return ap.rearrange("p (h t) -> p t h", h=HEADS)

        class Chain:

            def __init__(self, eng, step_sem, base=0):
                self.eng, self.sem, self.base, self.n = eng, step_sem, base, 0

            def did(self, instruction):
                instruction.then_inc(self.sem, 1)
                self.n += 1
                return self.n

            def link(self, instruction):
                n = self.did(instruction)
                self.eng.wait_ge(self.sem, self.base + n)

        def rounds(eng, lags, step):
            lag = max(lags)

            def steps(i, n):
                step(*[(2 * i + n - a, (n - a) % 2, i + ((n - a) // 2 + 1)) if n >= a and (lag <= n < lag + 2 or n - a < ROUNDS) else None
                       for a in lags])

            pairs = (ROUNDS - lag) // 2
            for n in range(lag):
                steps(0, n)
            with eng.Fori(0, pairs) as i:
                for n in range(lag, lag + 2):
                    steps(i, n)
            for n in range(lag + 2 * pairs, ROUNDS + lag):
                steps(0, n)

        def pipeline(eng, stage, pairs, last_pair, step):
            def item(i, q):
                return q, pairs * (2 * stage) + 2 * i + (q + 1), pairs * stage + i + 1

            step(item(0, 0), None)
            with eng.Fori(0, last_pair) as i:
                step(item(i, 1), item(i, 0))
                step(item(i + 1, 0), item(i, 1))
            step(item(last_pair, 1), item(last_pair, 0))
            step(None, item(last_pair, 1))

        @block.sync
        def _(sp):
            for q in range(2):
                sp.sem_inc(n_stored[q], stored_value)
                sp.sem_inc(out_stored[q], 16)
            with nc.allow_non_contiguous_dma(reason="a few numbers"):
                sp.dma_start(lohi[:, 0, :], dst.rearrange("(a c) t e -> a c (t e)", a=1)[:, :, 0]).then_inc(lohi_in, 16)
                sp.dma_start(lohi[:, 1, 0:N_CHUNKS - 1], dst[0:N_CHUNKS - 1].rearrange("(a c) t e -> a c (t e)", a=1)[:, :, CHUNK - 1]).then_inc(lohi_in, 16)
            sp.dma_start(lohi[:, 1, N_CHUNKS - 1:N_CHUNKS], dst[N_CHUNKS - 1].rearrange("(a t) e -> a (t e)", a=1)[:, LAST_EDGE:LAST_EDGE + 1]).then_inc(lohi_in, 16)
            for l in range(LAYERS):
                for s, (w, b) in enumerate(((Wl, bl), (Wr, br))):
                    sp.dma_start(w_lr[:, l, s, 0:F], w[l]).then_inc(consts_in, 16)
                    sp.dma_start(b_lr[:, l, s, 0:F], b[l].rearrange("(a f) -> a f", a=1)).then_inc(consts_in, 16)
                sp.dma_start(att_b[:, l, :], att[l].rearrange("h f -> (h f)").partition_broadcast(P)).then_inc(consts_in, 16)
                sp.dma_start(c_b[:, l, :], c[l].partition_broadcast(P)).then_inc(consts_in, 16)
                for row, col, v in ((g_b, g_col, g), (be_b, be_col, be)):
                    if l == LAYERS - 1:
                        sp.dma_start(row[:, :], v[l].partition_broadcast(P)).then_inc(consts_in, 16)
                    else:
                        with nc.allow_non_contiguous_dma(reason="a column"):
                            sp.dma_start(col[:, l:l + 1], v[l].rearrange("(p a) -> p a", a=1)).then_inc(consts_in, 16)
            sp.dma_start(w1_x[:, :], W1[0:F, :]).then_inc(consts_in, 16)
            sp.dma_start(w1_e[:, :], W1[F:F + D_EDGE, :]).then_inc(consts_in, 16)
            sp.dma_start(w1_u[:, :], W1[F + D_EDGE:F + D_EDGE + D_GRAPH, :]).then_inc(consts_in, 16)
            with nc.allow_non_contiguous_dma(reason="a few columns"):
                sp.dma_start(u_col[:, :], u[0:1, :].rearrange("a d -> d a")).then_inc(consts_in, 16)
                for i, v in enumerate((b1, gamma, beta)):
                    sp.dma_start(cols1[:, i, :], v.rearrange("(h p) -> p h", p=P)).then_inc(consts_in, 16)
            sp.dma_start(w2_s[:, :, :], W2.rearrange("(h p) f -> p h f", p=P)).then_inc(consts_in, 16)
            sp.dma_start(b2_r[:, :], b2.rearrange("(a f) -> a f", a=1)).then_inc(consts_in, 16)

            sp.wait_ge(table_made, 1)
            sp.dma_start(item_tab, item_i[0:MAX_ITEMS, :]).then_inc(table_out, 16)
            sp.wait_ge(table_out, 16)
            sp.dma_start(tab[:, :], item_tab.rearrange("(a k) w -> a (k w)", a=1)).then_inc(table_in, 16)
            sp.wait_ge(table_in, 16)
            pairs = sp.value_load(pairs_i[0:1, 1:2], min_val=MIN_PAIRS, max_val=MAX_PAIRS)

            last_pair = sp.value_load(pairs_i[0:1, 2:3], min_val=MIN_PAIRS - 1, max_val=MAX_PAIRS - 1)

            def load_round(stage, at):
                r, q, use = at
                if stage == 0:
                    sp.dma_start(n_in[q], rounds_of(x, r)).then_inc(x_loaded[q], 16)
                elif stage < LAYERS:
                    sp.dma_start(n_st[q][:, :, 0:ROW_L], rounds_of(state, r)[:, :, 0:ROW_L]).then_inc(st_loaded[q], 16)
                else:
                    sp.dma_start(n_x[q], rounds_of(x, r)).then_inc(fx_loaded[q], 16)
                    sp.dma_start(n_st[q], rounds_of(state, r)).then_inc(st_loaded[q], 16)

            def node_step(stage):
                width = ROW if stage == 0 else ROW_L

                def step(ahead, behind):
                    if ahead:
                        if behind:
                            if stage == 0:
                                sp.wait_ge(n_T, behind[0] + 1)
                            else:
                                sp.wait_ge(n_mean, behind[0] + (1 + (stage - 1) * ROUNDS))
                        load_round(stage, ahead)
                    if behind:
                        r, q, use = behind
                        sp.wait_ge(n_made, r + (1 + stage * ROUNDS))
                        sp.dma_start(rounds_of(xl_tab, r), n_lr[q][:, :, 0, :]).then_inc(n_stored[q], 16)
                        sp.wait_ge(split_step, (r + stage * ROUNDS) * SPLIT_STEPS + SPLIT_STEPS)
                        sp.dma_start(rounds_of(xr_tab, r), n_xr[q].rearrange("p j s f -> p j (s f)")).then_inc(n_stored[q], 16)
                        sp.dma_start(rounds_of(state, r)[:, :, 0:width], n_new[:, q, :, 0:width]).then_inc(n_stored[q], 16)
                return step

            def load_item(k, q):
                ch = sp.value_load(tab[0:1, bass.ds(2 * k, 1)], min_val=0, max_val=N_CHUNKS - 1)
                base = sp.value_load(tab[0:1, bass.ds(2 * k + 1, 1)], min_val=0, max_val=EMPTY_BASE)

                def edges(a):
                    return a[bass.ds(ch, 1), :, :].rearrange("a p t -> (a p) t")

                sp.dma_start(idx[:, q, :], edges(src_t)).then_inc(idx_loaded[q], 16)
                sp.dma_start(dst_e[:, q, :], edges(dst_t)).then_inc(item_loaded[q], 16)
                sp.dma_start(dst_next[:, q, :], edges(next_t)).then_inc(item_loaded[q], 16)
                rows = dst[bass.ds(ch, 1), :, :]
                sp.dma_start(dst_b[:, q, :], rows.rearrange("a t e -> a (t e)").to_broadcast([P, CHUNK])).then_inc(item_loaded[q], 16)
                for h in range(HEADS):
                    sp.dma_start(dst_r[h * TILES:(h + 1) * TILES, q, :], rows.rearrange("a t e -> (a t) e")).then_inc(item_loaded[q], 16)
                with nc.allow_non_contiguous_dma(reason="first and last of each tile"):
                    sp.dma_start(tile_ends[:, q, :, :], rows[:, :, 0:P:P - 1]).then_inc(item_loaded[q], 16)
                nodes = node_id[bass.ds(base, P)]
                with nc.allow_non_contiguous_dma(reason="one column of node numbers"):
                    sp.dma_start(node_col[:, q, :], nodes.rearrange("(p a) -> p a", a=1)).then_inc(item_loaded[q], 16)
                sp.dma_start(node_row[:, q, :], nodes.rearrange("(a p) -> a p", a=1).to_broadcast([P, P])).then_inc(item_loaded[q], 16)
                sp.dma_start(xr_w[:, q, :, :].rearrange("p s f -> p (s f)"), xr_tab[bass.ds(base, P), :]).then_inc(item_loaded[q], 16)

            def load_attributes(k, q):
                ch = sp.value_load(tab[0:1, bass.ds(2 * k, 1)], min_val=0, max_val=N_CHUNKS - 1)
                sp.dma_start(ea[:, q, :, :].rearrange("p t f -> p (t f)"),
                             edge_attr[bass.ds(ch, 1), :, :].rearrange("a p n -> (a p) n")).then_inc(ea_loaded[q], 16)

            def window(k, width):
                base = sp.value_load(tab[0:1, bass.ds(2 * k + 1, 1)], min_val=0, max_val=EMPTY_BASE)
                return state[bass.ds(base, P), 0:width]

            for stage in range(LAYERS):
                first = stage == 0
                width = ROW if first else ROW_L
                rounds(sp, (0, 2), node_step(stage))
                for q in range(2):
                    sp.wait_ge(n_stored[q], stored_value * ((stage + 1) * (ROUNDS // 2) + 1))

                before = pairs * (2 * stage)
                for q in range(2):
                    load_item(q, q)
                    if first:
                        load_attributes(q, q)
                sp.dma_start(st_old[:, 0, 0:width], window(0, width)).then_inc(state_loaded[0], 16)
                with sp.Fori(0, last_pair) as i:
                    for q in range(2):
                        k = 2 * i + q
                        here, ahead = window(k, width), window(k + 1, width)
                        sp.wait_ge(onehot_done[NG - 1], (before + k + 1) * 2)
                        sp.sem_inc(load_go, 1)
                        sp.wait_ge(logit_done[NG - 1], (before + k + 1) * 3)
                        sp.sem_inc(load_go, 1)
                        load_item(k + 2, q)
                        sp.wait_ge(item_done, before + k + 1)
                        sp.dma_start(here, st_new[:, q, 0:width]).then_inc(state_stored, 16)
                        if first:
                            load_attributes(k + 2, q)
                        sp.wait_ge(state_stored, (before + k + 1) * 16)
                        sp.dma_start(st_old[:, 1 - q, 0:width], ahead).then_inc(state_loaded[1 - q], 16)
                for q in range(2):
                    k = 2 * last_pair + q
                    here = window(k, width)
                    if q == 0:
                        ahead = window(k + 1, width)
                    sp.wait_ge(item_done, before + k + 1)
                    sp.dma_start(here, st_new[:, q, 0:width]).then_inc(state_stored, 16)
                    sp.wait_ge(state_stored, (before + k + 1) * 16)
                    if q == 0:
                        sp.dma_start(st_old[:, 1, 0:width], ahead).then_inc(state_loaded[1], 16)

            def last_step(ahead, behind):
                if ahead:
                    if behind:
                        sp.wait_ge(x1_ready, behind[0] + 1)
                    load_round(LAYERS, ahead)

            rounds(sp, (0, 2), last_step)

            def out_step(at):
                r, q, use = at
                sp.wait_ge(out_made, r + 1)
                sp.dma_start(rounds_of(out, r), o_out[q]).then_inc(out_stored[q], 16)

            with sp.Fori(0, ROUNDS // 2 - 1) as i:
                for q in range(2):
                    out_step((2 * i + q, q, i + 1))
            out_step((ROUNDS - 2, 0, ROUNDS // 2))
            sp.wait_ge(out_made, ROUNDS)
            sp.dma_start(out[(ROUNDS - 1) * NROWS:N_NODES, :].rearrange("(p j) f -> p j f", j=NB),
                         o_out[1][0:LAST_P, :, :]).then_inc(out_stored[1], 16)
            for q in range(2):
                sp.wait_ge(out_stored[q], 16 * (ROUNDS // 2 + 1))

        @block.gpsimd
        def _(pool):
            pool.memset(ident[:, :], 0.0).then_inc(ident_zero, 1)
            pool.iota(k_col[:, :], [[0, 1]], base=0, channel_multiplier=1,
                      allow_small_or_imprecise_dtypes=True).then_inc(rows_made, 1)
            pool.wait_ge(ident_zero, 1)
            pool.affine_select(out=ident[:, :], in_=ident[:, :], compare_op=ALU.not_equal, fill=1.0, base=0,
                               pattern=[[-1, P]], channel_multiplier=1).then_inc(ident_made, 1)
            pool.wait_ge(table_made, 1)
            pairs = pool.value_load(pairs_i[0:1, 1:2], min_val=MIN_PAIRS, max_val=MAX_PAIRS)

            def split(stage):
                def step(at):
                    r, q, use = at
                    n = Chain(pool, split_step, (r + stage * ROUNDS) * SPLIT_STEPS)
                    pool.wait_ge(n_copied, r + (1 + stage * ROUNDS))
                    pool.sem_inc(gather_go, 1)
                    whole, high, middle, low = n_lr[q][:, :, 1, :], *[n_xr[q][:, :, w, :] for w in range(PARTS)]
                    n.did(pool.tensor_tensor(out=middle, in0=whole, in1=high, op=ALU.subtract))
                    n.link(pool.tensor_tensor(out=n_rest, in0=whole, in1=high, op=ALU.subtract))
                    pool.sem_inc(gather_go, 1)
                    n.link(pool.tensor_tensor(out=low, in0=n_rest, in1=middle, op=ALU.subtract))
                    pool.sem_inc(gather_go, 1)
                    assert n.n == SPLIT_STEPS, n.n
                return step

            for stage in range(LAYERS):
                rounds(pool, (0,), split(stage))
                with pool.Fori(0, pairs) as i:
                    for q in range(2):
                        pool.wait_ge(idx_loaded[q], (pairs * stage + i + 1) * 16)
                        for g, tiles in enumerate(GROUPS):
                            pool.wait_ge(msg_done[g], pairs * (2 * stage) + 2 * i + (q + 1))
                            pool.sem_inc(gather_go, 1)
                            for t in tiles:
                                pool.indirect_dma_start(xl_g[:, q, t, :], None, xl_tab[:, :],
                                                        bass.IndirectOffsetOnAxis(idx[:, q, t:t + 1], 0))\
                                    .then_inc(gathered[q][g], 16)

        @block.tensor
        def _(pe):
            for g in range(NG):
                pe.sem_inc(msg_done[g], 2)
            pe.wait_ge(ones_made, 1)
            pe.wait_ge(setup, SETUP_ROW_STEPS)
            pe.matmul(flat[:, 0:2 * N_CHUNKS], ones[0:1, :], tab_row[:, :, :].rearrange("a w c -> a (w c)"),
                      start=True, stop=True).then_inc(tab_bc, 1)
            pe.wait_ge(table_made, 1)
            pairs = pe.value_load(pairs_i[0:1, 1:2], min_val=MIN_PAIRS, max_val=MAX_PAIRS)
            last_pair = pe.value_load(pairs_i[0:1, 2:3], min_val=MIN_PAIRS - 1, max_val=MAX_PAIRS - 1)
            pe.wait_ge(ident_made, 1)
            pe.wait_ge(consts_in, 16 * CONST_DMAS)
            pe.wait_ge(consts_made, 1)

            def transform(stage):
                def step(at):
                    r, q, use = at
                    v = r + (1 + stage * ROUNDS)
                    if stage == 0:
                        pe.wait_ge(x_loaded[q], use * 16)
                    else:
                        pe.wait_ge(n_norm, r + (1 + (stage - 1) * ROUNDS))
                    for j in range(NB):
                        last = pe.transpose(hT_ps[:, j * P:(j + 1) * P], n_in[q][:, j, :], ident[:, :])
                    last.then_inc(n_T, 1)
                    pe.wait_ge(n_Tc, v)
                    for j in range(NB):
                        for w in range(PARTS):
                            pe.matmul(lr_ps[:, j, :], ones_h[0:1, :], b_parts[:, w, stage, :, :].rearrange("a s f -> a (s f)"), start=w == 0, stop=False)
                        last = pe.matmul(lr_ps[:, j, :], n_hT[:, j * P:(j + 1) * P], w_lr[:, stage, :, :].rearrange("p s f -> p (s f)"),
                                         start=False, stop=True)
                    last.then_inc(n_prod, 1)
                return step

            for stage in range(LAYERS):
                rounds(pe, (0,), transform(stage))

                def pe_step(opens, closes):
                    def expand(g):
                        q, v, use = opens
                        if g == 0:
                            pe.wait_ge(item_loaded[q], use * (16 * ITEM_DMAS))
                        pe.wait_ge(onehotT_done[g], v)
                        if g >= 2:
                            pe.wait_ge(z_done[g - 2], v)
                        for n, t in enumerate(GROUPS[g]):
                            for w in range(PARTS):
                                last = pe.matmul(zp[(q + g) % 2][:, n, :], ST[:, t, :], xr_w[:, q, w, :], start=w == 0, stop=w == PARTS - 1)
                        last.then_inc(expanded[g], 1)

                    def close(part):
                        q, v, use = closes
                        if part == "rows":
                            pe.wait_ge(logit_done[NG - 1], v * 3)
                            pe.transpose(lt_ps, logit[:, q, :], ident[:, :]).then_inc(logitT_done, 1)
                        if part == "open":
                            pe.wait_ge(runs_done, v)
                            pe.matmul(open_ps[0], run_up[:, P - 1:P], ident[0:LH, 0:LH], start=True, stop=True)
                            pe.matmul(open_ps[1], run_down[:, 0:1], ident[0:LH, 0:LH], start=True, stop=True).then_inc(open_done, 1)
                        if part == "carry":
                            pe.wait_ge(carry_done, v)
                            pe.matmul(carry_ps[:, 0:1], carry[:, 0, :], ones[:, 0:1], start=True, stop=True)
                            pe.matmul(carry_ps[:, 1:2], carry[:, 1, :], ones[:, 0:1], start=True, stop=True).then_inc(carryT_done, 1)
                        if part == "max":
                            pe.wait_ge(segmax_done, v)
                            pe.transpose(mb_ps, seg_max[:, :], ident[0:LH, 0:LH]).then_inc(segmaxT_done, 1)

                    def attribute_sums(tiles):
                        q, v, use = closes
                        if tiles[0] == 0:
                            pe.wait_ge(ea_loaded[q], use * 16)
                            pe.wait_ge(onehot_done[NG - 1], v * 2)
                        for t in tiles:
                            pe.matmul(ea_ps, S[:, q, t, :], ea[:, q, t, :], start=t == 0, stop=t == TILES - 1)

                    def sums(g):
                        q, v, use = closes
                        pe.wait_ge(onehot_done[g], v * 2)
                        pe.wait_ge(msg_done[g], v + 2)
                        for t in GROUPS[g]:
                            last = pe.matmul(agg_ps, S[:, q, t, :], msg[:, t, :], start=t == 0, stop=t == TILES - 1)
                        if g == NG - 1:
                            last.then_inc(agg_done, 1)

                    if closes:
                        close("rows")
                    for g in range(NG):
                        if opens and g == 0:
                            expand(0)
                            expand(1)
                        elif opens and g >= 2:
                            expand(g)
                        if closes and g == 0:
                            close("open")
                        if closes and g == 1:
                            close("carry")
                        if closes and g == 2:
                            close("max")
                        if closes and stage == 0 and g < 3:
                            attribute_sums(range(*EA_CUTS[g:g + 2]))
                        if closes:
                            for m in SUMS_AT.get(g - 1, ()):
                                sums(m)

                pipeline(pe, stage, pairs, last_pair, pe_step)

            for h in range(2):
                last = pe.matmul(PS[:, 4, h:h + 1], w1_u[:, h * P:(h + 1) * P], u_col[:, :], start=True, stop=True)
            last.then_inc(hid_bias, 1)
            pe.wait_ge(hid_b, 1)

            def hidden_products(at):
                r, q, use = at
                v = r + 1
                pe.wait_ge(x1_ready, v)
                for j in range(NB):
                    pe.transpose(hT_ps[:, j * P:(j + 1) * P], n_in[q][:, j, :], ident[:, :])
                for j in range(NB):
                    last = pe.transpose(eT_ps[:, j * P:(j + 1) * P], n_e[:, j, :], ident[:, :])
                last.then_inc(e_T, 1)
                pe.wait_ge(e_Tc, v)
                for h in range(2):
                    for m in range(2):
                        cut = slice(m * (NROWS // 2), (m + 1) * (NROWS // 2))
                        pe.matmul(PS[:, 4 + 2 * h + m, 0:NROWS // 2], w1_x[:, h * P:(h + 1) * P], n_hT[:, cut], start=True, stop=False)
                        last = pe.matmul(PS[:, 4 + 2 * h + m, 0:NROWS // 2], w1_e[:, h * P:(h + 1) * P], n_eT[:, cut], start=False, stop=True)
                last.then_inc(hid_ps, 1)

            rounds(pe, (0,), hidden_products)

            def out_products(at):
                r, q, use = at
                pe.wait_ge(act_done, r + 1)
                for j in range(NB):
                    for w in range(PARTS):
                        pe.matmul(out_ps[q][:, j * F:(j + 1) * F], ones_h[0:1, :], b2_parts[:, w, :], start=w == 0, stop=False)
                    for h in range(2):
                        last = pe.matmul(out_ps[q][:, j * F:(j + 1) * F], hid_relu[q][:, h, j * P:(j + 1) * P], w2_s[:, h, :],
                                         start=False, stop=h == 1)
                last.then_inc(out_mm, 1)

            rounds(pe, (0,), out_products)

        @block.scalar
        def _(act):
            act.wait_ge(table_made, 1)
            pairs = act.value_load(pairs_i[0:1, 1:2], min_val=MIN_PAIRS, max_val=MAX_PAIRS)
            last_pair = act.value_load(pairs_i[0:1, 2:3], min_val=MIN_PAIRS - 1, max_val=MAX_PAIRS - 1)

            def squares_of(y, c):
                for j in range(NB):
                    last = act.activation(n_junk[:, j, :], y[:, j, :], ACT.Square, bias=c[:, 1, j:j + 1], accum_out=c[:, 2, j:j + 1])
                return last

            def node_step(stage):
                def step(ahead, behind):
                    if ahead and stage > 0:
                        v = ahead[0] + (1 + (stage - 1) * ROUNDS)
                        act.wait_ge(n_mean, v)
                        squares_of(n_y, n_c).then_inc(n_sq, 1)
                        act.wait_ge(n_var, v)
                        act.activation(n_c[:, 4, :], n_c[:, 3, :], ACT.Sqrt).then_inc(n_std, 1)
                    if behind:
                        r, q, use = behind
                        act.wait_ge(n_prod, r + (1 + stage * ROUNDS))
                        act.wait_ge(n_stored[q], (use + stage * (ROUNDS // 2)) * stored_value)
                        act.copy(n_lr[q].rearrange("p j s f -> p j (s f)"), lr_ps)
                        act.copy(n_xr[q][:, :, 0, :], lr_ps[:, :, XW:2 * XW])
                        act.copy(n_new[:, q, :, C_ACC:C_ACC + F], lr_ps[:, :, 0:F]).then_inc(n_copied, 1)
                    if ahead:
                        act.wait_ge(n_T, ahead[0] + (1 + stage * ROUNDS))
                        if stage == 0:
                            act.copy(n_hT[:, :], hT_ps).then_inc(n_Tc, 1)
                        else:
                            act.activation(n_hT[:, :], hT_ps, ACT.Relu, bias=be_col[:, stage - 1:stage], scale=g_col[:, stage - 1:stage])\
                                .then_inc(n_Tc, 1)
                return step

            for stage in range(LAYERS):
                rounds(act, (0, 1), node_step(stage))

                def act_step(opens, closes):
                    def onehot(g):
                        q, v, use = opens
                        n = len(GROUPS[g])
                        if g == 0:
                            act.wait_ge(item_loaded[q], use * (16 * ITEM_DMAS))
                            act.wait_ge(negdst_done, v)
                        for m, t in enumerate(GROUPS[g]):
                            last = act.activation(dist[:, (q + g) % 2, m, :], node_row[:, q, :], ACT.Abs, bias=neg_dst[:, q, t:t + 1])
                        last.then_inc(onehot_done[g], 1)
                        act.wait_ge(onehot_done[g], v * 2 - 1)
                        act.activation(S[:, q, GROUPS[g][0]:GROUPS[g][0] + n, :], dist[:, (q + g) % 2, 0:n, :], ACT.Relu, bias=1.0, scale=-1.0)\
                            .then_inc(onehot_done[g], 1)

                    if opens:
                        onehot(0)
                        onehot(1)
                    if closes:
                        act.wait_ge(shifted_done, closes[1])
                        act.activation(msg[:, :, M_ALPHA:M_ONE], shifted[:, :].rearrange("p (t h) -> p t h", h=HEADS), ACT.Exp)\
                            .then_inc(alpha_done, 1)
                    if opens:
                        for g in range(2, NG):
                            onehot(g)
                    if closes:
                        act.wait_ge(dmax_done, closes[1])
                        act.activation(rescale[:, :, :], dmax[:, :, :], ACT.Exp).then_inc(rescale_done, 1)

                pipeline(act, stage, pairs, last_pair, act_step)

            def last_step(ahead, behind, before):
                if behind:
                    act.wait_ge(h_var, behind[0] + 1)
                    act.activation(h_c[:, 4, :], h_c[:, 3, :], ACT.Sqrt).then_inc(h_std, 1)
                if ahead:
                    v = ahead[0] + (1 + (LAYERS - 1) * ROUNDS)
                    act.wait_ge(n_mean, v)
                    squares_of(n_y, n_c).then_inc(n_sq, 1)
                    act.wait_ge(n_var, v)
                    act.activation(n_c[:, 4, :], n_c[:, 3, :], ACT.Sqrt).then_inc(n_std, 1)
                if before:
                    r = before[0]
                    act.wait_ge(hid_ps, r + 1)
                    for h in range(2):
                        for m in range(2):
                            last = act.activation(hid[h][:, bass.ds(r * NROWS + m * (NROWS // 2), NROWS // 2)],
                                                  PS[:, 4 + 2 * h + m, 0:NROWS // 2], ACT.Identity, bias=bn[:, 0, h:h + 1])
                    last.then_inc(hid_done, 1)
                if behind:
                    act.wait_ge(e_T, behind[0] + 1)
                    act.copy(n_hT[:, :], hT_ps)
                    act.copy(n_eT[:, :], eT_ps).then_inc(e_Tc, 1)
                    act.copy(x1[:, bass.ds(behind[0] * NB, NB), :], n_in[behind[1]])
                if ahead:
                    act.wait_ge(h_mean, ahead[0] + 1)
                    squares_of(n_h, h_c).then_inc(h_sq, 1)

            rounds(act, (0, 1, 2), last_step)
            act.wait_ge(mu_done, 1)
            full = (ROUNDS - 1) * NROWS
            for h in range(2):
                for m in range(3):
                    if h or m:
                        act.wait_ge(sq_done, 3 * h + m)
                    if m < 2:
                        a = act.activation(squares[:, 0:full // 2], hid[h][:, m * (full // 2):(m + 1) * (full // 2)], ACT.Square,
                                           bias=bn[:, 1, h:h + 1], accum_out=bn_sum[:, h, m:m + 1])
                    else:
                        a = act.activation(squares[:, 0:NB * LAST_P].rearrange("p (j e) -> p j e", j=NB),
                                           hid[h][:, full:].rearrange("p (j e) -> p j e", j=NB)[:, :, 0:LAST_P], ACT.Square,
                                           bias=bn[:, 1, h:h + 1], accum_out=bn_sum[:, h, 2:3])
                    a.then_inc(sq_done, 1)
            act.wait_ge(bn_var, 1)
            act.activation(bn[:, 4, :], bn[:, 3, :], ACT.Sqrt).then_inc(bn_std, 1)
            act.wait_ge(bn_done, 1)

            def out_step(ahead, behind):
                if ahead:
                    r, q, use = ahead
                    for h in range(2):
                        last = act.activation(hid_relu[q][:, h, :], hid[h][:, bass.ds(r * NROWS, NROWS)], ACT.Relu,
                                              bias=bn[:, 6, h:h + 1], scale=bn[:, 5, h:h + 1])
                    last.then_inc(act_done, 1)
                if behind:
                    r, q, use = behind
                    act.wait_ge(o_mean, r + 1)
                    squares_of(o_y[q], o_c[:, q, :, :]).then_inc(o_sq, 1)
                    act.wait_ge(o_var, r + 1)
                    act.activation(o_c[:, q, 4, :], o_c[:, q, 3, :], ACT.Sqrt).then_inc(o_std, 1)

            rounds(act, (0, 1), out_step)

        @block.vector
        def _(dve):
            ch = Chain(dve, setup)
            dve.memset(ones[:, :], 1.0).then_inc(ones_made, 1)
            ch.link(dve.memset(zero_row[:, :], 0.0))
            dve.wait_ge(lohi_in, 48)
            ch.link(dve.tensor_tensor(out=span[:, :], in0=lohi[:, 1, :], in1=lohi[:, 0, :], op=ALU.subtract))
            ch.link(dve.tensor_scalar(span[:, :], span[:, :], 7, None, ALU.arith_shift_right))
            ch.link(dve.tensor_scalar(nwin[:, :], span[:, :], 1.0, None, ALU.add))
            ch.link(dve.tensor_tensor_scan(tab_row[:, 0, :], nwin[:, :], zero_row[:, :], 0.0, ALU.add, ALU.add))
            ch.link(dve.tensor_tensor(out=nwin[:, :], in0=nwin[:, :], in1=tab_row[:, 0, :], op=ALU.subtract))
            ch.link(dve.tensor_copy(lo_f[:, :], lohi[:, 0, :]))
            ch.link(dve.scalar_tensor_tensor(tab_row[:, 1, :], nwin[:, :], float(P), lo_f[:, :], ALU.mult, ALU.add))
            assert ch.n == SETUP_ROW_STEPS, ch.n
            ch.link(dve.tensor_scalar(pairs_i[:, 0:1], tab_row[:, 0, N_CHUNKS - 1:N_CHUNKS], 1.0, None, ALU.add))
            ch.link(dve.tensor_scalar(pairs_i[:, 1:2], pairs_i[:, 0:1], 1, None, ALU.arith_shift_right))
            ch.link(dve.tensor_scalar(pairs_i[:, 2:3], pairs_i[:, 1:2], -1.0, None, ALU.add))
            dve.wait_ge(tab_bc, 1)
            dve.wait_ge(rows_made, 1)
            ch.link(dve.memset(past[:, 0:1], 1.0))
            ch.link(dve.tensor_scalar(past[:, 1:N_CHUNKS + 1], flat[:, 0:N_CHUNKS], k_col[:, 0:1], None, ALU.is_le))
            ch.link(dve.reduce_sum(item_f[:, 0:1], past[:, 1:N_CHUNKS + 1], axis=AX.X))
            ch.link(dve.tensor_tensor(out=own[:, :], in0=past[:, 0:N_CHUNKS], in1=past[:, 1:N_CHUNKS + 1], op=ALU.subtract))
            ch.link(dve.tensor_tensor(out=own[:, :], in0=own[:, :], in1=flat[:, N_CHUNKS:2 * N_CHUNKS], op=ALU.mult))
            ch.link(dve.reduce_sum(item_f[:, 1:2], own[:, :], axis=AX.X))
            ch.link(dve.scalar_tensor_tensor(item_f[:, 1:2], k_col[:, 0:1], float(P), item_f[:, 1:2], ALU.mult, ALU.add))
            ch.link(dve.tensor_scalar(item_f[:, 2:3], past[:, N_CHUNKS:N_CHUNKS + 1], -1.0, 1.0, ALU.mult, ALU.add))
            ch.link(dve.tensor_tensor(out=item_i[:, 0:1], in0=item_f[:, 0:1], in1=item_f[:, 2:3], op=ALU.mult))
            ch.link(dve.tensor_scalar(item_f[:, 3:4], item_f[:, 1:2], -float(EMPTY_BASE), item_f[:, 2:3], ALU.add, ALU.mult))
            ch.link(dve.tensor_scalar(item_i[:, 1:2], item_f[:, 3:4], float(EMPTY_BASE), None, ALU.add))
            dve.memset(row_pen[:, :], 0.0)
            dve.memset(tile_eq[:, :], 0.0)
            dve.memset(open_max[:, :, :], -BIG)
            dve.memset(msg[:, :, M_ONE:M_MAX], 1.0).then_inc(table_made, 1)
            dve.wait_ge(table_made, 1)
            pairs = dve.value_load(pairs_i[0:1, 1:2], min_val=MIN_PAIRS, max_val=MAX_PAIRS)
            last_pair = dve.value_load(pairs_i[0:1, 2:3], min_val=MIN_PAIRS - 1, max_val=MAX_PAIRS - 1)
            dve.wait_ge(ident_made, 1)
            dve.wait_ge(consts_in, 16 * CONST_DMAS)
            dve.tensor_scalar(att_relu[:, :, :], att_b[:, :, :], 1.0 - SLOPE, None, ALU.mult)
            ch.link(dve.tensor_scalar(att_lin[:, :, :], att_b[:, :, :], SLOPE, None, ALU.mult))
            for l in range(LAYERS):
                for s in range(2):
                    for parts, w in ((P, w_lr[:, :, :, :]), (1, b_lr)):
                        heads = HEADS if l < LAYERS - 1 else 1
                        part = s_flat[0:parts, 0:F]
                        ch.link(dve.tensor_tensor(out=part, in0=w[:, l, s, 0:F], in1=att_lin[0:parts, l, :], op=ALU.mult))
                        sums = n_c[0:parts, 0, 0:heads]
                        ch.link(dve.reduce_sum(sums, part.rearrange("p (h f) -> p h f", h=heads), axis=AX.X))
                        ch.link(dve.tensor_copy(w[:, l, s, F:XW], sums if heads == HEADS else sums.to_broadcast([parts, HEADS])))
            dve.memset(ones_h[:, :], 1.0)
            for whole, parts in ((b_lr.rearrange("a l s f -> a (l s f)"), b_parts[:, :, :, :, :].rearrange("a w l s f -> a w (l s f)")),
                                 (b2_r[:, :], b2_parts[:, :, :])):
                rest, left = whole, b_rest[:, 0:whole.shape[1]]
                for w in range(PARTS):
                    ch.link(dve.tensor_copy(parts[:, w, :], rest))
                    if w < PARTS - 1:
                        ch.link(dve.tensor_tensor(out=left, in0=rest, in1=parts[:, w, :], op=ALU.subtract))
                        rest = left
            dve.memset(n_new[:, :, :, C_CNT:ROW], 0.0)
            dve.memset(n_new[:, :, :, C_DEN:C_DEN + HEADS], 1.0).then_inc(consts_made, 1)

            def mean_of(n, y, c, mean_sem):
                n.link(dve.reduce_sum(c[:, 0, :], y, axis=AX.X))
                dve.tensor_scalar(c[:, 1, :], c[:, 0, :], -1.0 / F, None, ALU.mult).then_inc(mean_sem, 1)

            def variance_of(c, sq_sem, v, var_sem):
                dve.wait_ge(sq_sem, v)
                dve.tensor_scalar(c[:, 3, :], c[:, 2, :], 1.0 / F, EPS, ALU.mult, ALU.add).then_inc(var_sem, 1)

            def normalized(n, to, y, c, std_sem, v):
                dve.wait_ge(std_sem, v)
                n.link(dve.reciprocal(c[:, 5, :], c[:, 4, :]))
                for j in range(NB):
                    last = dve.tensor_scalar(to(j), y[:, j, :], c[:, 1, j:j + 1], c[:, 5, j:j + 1], ALU.add, ALU.mult)
                return last

            def layer_mean(l, at):
                r, q, use = at
                n = Chain(dve, ln_step, (r + l * ROUNDS) * LN_STEPS)
                dve.wait_ge(st_loaded[q], (use + l * (ROUNDS // 2)) * 16)
                n.link(dve.reciprocal(n_rd[:, :, :], n_st[q][:, :, C_DEN:C_DEN + HEADS]))
                n.link(dve.tensor_tensor(out=n_y.rearrange("p j (h f) -> p j h f", h=HEADS),
                                         in0=n_st[q][:, :, C_ACC:C_ACC + F].rearrange("p j (h f) -> p j h f", h=HEADS),
                                         in1=n_rd[:, :, :].unsqueeze(3).to_broadcast([P, NB, HEADS, F // HEADS]), op=ALU.mult))
                n.link(dve.tensor_tensor(out=n_y, in0=n_y, in1=over_blocks(c_b[:, l, :]), op=ALU.add))
                mean_of(n, n_y, n_c, n_mean)
                return n

            def layer_norm(n, l, at):
                r, q, use = at
                v = r + (1 + l * ROUNDS)
                variance_of(n_c, n_sq, v, n_var)
                normalized(n, lambda j: n_in[q][:, j, :], n_y, n_c, n_std, v).then_inc(n_norm, 1)
                assert n.n == LN_STEPS, n.n

            def loop_logits(stage, at):
                r, q, use = at
                v = r + (1 + stage * ROUNDS)
                n = Chain(dve, logit_step, (r + stage * ROUNDS) * LOGIT_STEPS)
                dve.wait_ge(n_copied, v)
                lr = n_lr[q]
                n.link(dve.tensor_tensor(out=n_sum, in0=lr[:, :, 0, 0:F], in1=lr[:, :, 1, 0:F], op=ALU.add))
                n.link(dve.scalar_tensor_tensor(n_relu, n_sum, 0.0, over_blocks(att_relu[:, stage, :]), ALU.max, ALU.mult))
                if stage < LAYERS - 1:
                    n.link(dve.reduce_sum(n_rs[:, :, :], n_relu.rearrange("p j (h f) -> p j h f", h=HEADS), axis=AX.X))
                    relu_part = n_rs[:, :, :]
                else:
                    n.link(dve.reduce_sum(n_rs[:, :, 0], n_relu, axis=AX.X))
                    relu_part = over_features(n_rs[:, :, 0], HEADS)
                n.link(dve.tensor_tensor(out=n_m[:, :, :], in0=relu_part, in1=lr[:, :, 0, F:XW], op=ALU.add))
                dve.tensor_tensor(out=n_new[:, q, :, 0:HEADS], in0=n_m[:, :, :], in1=lr[:, :, 1, F:XW], op=ALU.add).then_inc(n_made, 1)
                assert n.n == LOGIT_STEPS, n.n

            def node_step(stage):
                def step(ahead, behind):
                    if ahead:
                        n = layer_mean(stage - 1, ahead)
                    if behind:
                        loop_logits(stage, behind)
                    if ahead:
                        layer_norm(n, stage - 1, ahead)
                return step

            def edge_step(stage, opens, closes):
                def onehotT(g):
                    q, v, use = opens
                    a, n = GROUPS[g][0], len(GROUPS[g])
                    if g == 0:
                        dve.wait_ge(item_loaded[q], use * (16 * ITEM_DMAS))
                        dve.tensor_scalar(neg_dst[:, q, :], dst_e[:, q, :], -1.0, None, ALU.mult).then_inc(negdst_done, 1)
                    dve.tensor_scalar(ST[:, a:a + n, :].rearrange("p t e -> p (t e)"), dst_b[:, q, a * P:(a + n) * P],
                                      node_col[:, q, 0:1], None, ALU.is_equal).then_inc(onehotT_done[g], 1)

                def add_transforms(g):
                    q, v, use = opens
                    a, n = GROUPS[g][0], len(GROUPS[g])
                    dve.wait_ge(expanded[g], v)
                    dve.wait_ge(gathered[q][g], use * (16 * n))
                    dve.tensor_tensor(out=z[:, (q + g) % 2, 0:n, :], in0=zp[(q + g) % 2][:, 0:n, :], in1=xl_g[:, q, a:a + n, :],
                                      op=ALU.add).then_inc(z_done[g], 1)

                def relu_att(g):
                    q, v, use = opens
                    n = len(GROUPS[g])
                    dve.wait_ge(z_done[g], v)
                    dve.scalar_tensor_tensor(am[:, (q + g) % 2, 0:n, :], z[:, (q + g) % 2, 0:n, 0:F], 0.0,
                                             att_relu[:, stage, :].unsqueeze(1).to_broadcast([P, n, F]), ALU.max, ALU.mult)\
                        .then_inc(logit_done[g], 1)

                def sum_heads(g):
                    q, v, use = opens
                    a, n = GROUPS[g][0], len(GROUPS[g])
                    dve.wait_ge(logit_done[g], v * 3 - 2)
                    if stage < LAYERS - 1:
                        s = dve.reduce_sum(relu_logit[:, a * HEADS:(a + n) * HEADS],
                                           am[:, (q + g) % 2, 0:n, :].rearrange("p t (h f) -> p (t h) f", h=HEADS), axis=AX.X)
                    else:
                        s = dve.reduce_sum(relu_logit[:, a:a + n], am[:, (q + g) % 2, 0:n, :], axis=AX.X)
                    s.then_inc(logit_done[g], 1)

                def add_linear(g):
                    q, v, use = opens
                    a, n = GROUPS[g][0], len(GROUPS[g])
                    dve.wait_ge(logit_done[g], v * 3 - 1)
                    if stage < LAYERS - 1:
                        part = relu_logit[:, a * HEADS:(a + n) * HEADS].rearrange("p (t h) -> p t h", h=HEADS)
                    else:
                        part = relu_logit[:, a:a + n].unsqueeze(2).to_broadcast([P, n, HEADS])
                    dve.tensor_tensor(out=by_tile(logit[:, q, :])[:, a:a + n, :], in0=part, in1=z[:, (q + g) % 2, 0:n, F:XW],
                                      op=ALU.add).then_inc(logit_done[g], 1)

                def flags():
                    q, v, use = opens
                    first, last = tile_ends[:, q, :, 0], tile_ends[:, q, :, 1]
                    dve.tensor_tensor(out=row_eq[:, 1:P], in0=dst_r[:, q, 1:P], in1=dst_r[:, q, 0:P - 1], op=ALU.is_equal).then_inc(flag_done[0], 1)
                    dve.tensor_tensor(out=seg_last[:, :], in0=dst_e[:, q, :], in1=dst_next[:, q, :], op=ALU.not_equal).then_inc(flag_done[1], 1)
                    dve.tensor_tensor(out=tile_eq[:, 1:TILES], in0=first[:, 1:TILES], in1=last[:, 0:TILES - 1], op=ALU.is_equal).then_inc(flag_done[2], 1)
                    dve.tensor_tensor(out=tile_one[:, :], in0=first, in1=last, op=ALU.is_equal).then_inc(flag_done[3], 1)
                    dve.wait_ge(flag_done[0], v)
                    dve.tensor_scalar(row_pen[:, 1:P], row_eq[:, 1:P], -1.0, BIG, ALU.add, ALU.mult)
                    dve.wait_ge(flag_done[1], v)
                    dve.tensor_scalar(seg_last[:, TILES - 1:TILES], seg_last[:, TILES - 1:TILES], ident[:, P - 1:P], None, ALU.max).then_inc(flag_done[4], 1)
                    dve.wait_ge(flag_done[3], v)
                    for d in range(2):
                        w = dve.tensor_tensor(out=through[:, d, :], in0=tile_eq[:, d:d + TILES], in1=tile_one[:, :], op=ALU.mult)
                    w.then_inc(flag_done[5], 1)
                    per_head = [1, HEADS, TILES]
                    for d in range(2):
                        dve.tensor_scalar(enter_pen[:, d, :].rearrange("a (h t) -> a h t", h=HEADS),
                                          tile_eq[:, d:d + TILES].unsqueeze(1).to_broadcast(per_head), -1.0, BIG, ALU.add, ALU.mult)
                    dve.wait_ge(flag_done[5], v)
                    for d in range(2):
                        w = dve.tensor_scalar(through_pen[:, d, :].rearrange("a (h t) -> a h t", h=HEADS),
                                              through[:, d, :].unsqueeze(1).to_broadcast(per_head), -1.0, BIG, ALU.add, ALU.mult)
                    w.then_inc(flag_done[6], 1)

                def runs():
                    q, v, use = closes
                    dve.wait_ge(logitT_done, v)
                    dve.wait_ge(flag_done[6], v)
                    dve.tensor_tensor_scan(run_up[:, :], row_pen[:, 0:P], lt_ps, -BIG, ALU.add, ALU.max)
                    dve.tensor_tensor_scan(run_down[:, ::-1], row_pen[:, 1:P + 1][:, ::-1], lt_ps[:, ::-1], -BIG, ALU.add, ALU.max)\
                        .then_inc(runs_done, 1)

                def carries():
                    q, v, use = closes
                    dve.wait_ge(open_done, v)
                    dve.tensor_tensor_scan(open_max[:, 0, 1:LH + 1], through_pen[:, 0, :], open_ps[0], -BIG, ALU.add, ALU.max)
                    dve.tensor_tensor_scan(open_max[:, 1, 1:LH + 1][:, ::-1], through_pen[:, 1, :][:, ::-1], open_ps[1][:, ::-1], -BIG,
                                           ALU.add, ALU.max).then_inc(openmax_done, 1)
                    dve.wait_ge(openmax_done, v)
                    dve.tensor_tensor(out=carry[:, 0, :], in0=open_max[:, 0, 0:LH], in1=enter_pen[:, 0, :], op=ALU.add)
                    dve.tensor_tensor(out=carry[:, 1, :], in0=open_max[:, 1, 2:LH + 2], in1=enter_pen[:, 1, :], op=ALU.add).then_inc(carry_done, 1)

                def maxima():
                    q, v, use = closes
                    dve.wait_ge(carryT_done, v)
                    dve.tensor_copy(carry_col[:, :], carry_ps).then_inc(carrycol_done, 1)
                    dve.wait_ge(carrycol_done, v)
                    dve.tensor_tensor_scan(up[:, :], row_pen[:, 0:P], lt_ps, carry_col[:, 0:1], ALU.add, ALU.max).then_inc(up_done, 1)
                    dve.wait_ge(up_done, v)
                    dve.tensor_tensor_scan(seg_max[:, ::-1], row_pen[:, 1:P + 1][:, ::-1], up[:, ::-1], carry_col[:, 1:2], ALU.add, ALU.max)\
                        .then_inc(segmax_done, 1)

                def shift():
                    q, v, use = closes
                    dve.wait_ge(segmaxT_done, v)
                    dve.tensor_tensor(out=shifted[:, :].rearrange("p (t h) -> p t h", h=HEADS), in0=by_tile(logit[:, q, :]),
                                      in1=by_tile(mb_ps), op=ALU.subtract).then_inc(shifted_done, 1)
                    dve.tensor_tensor(out=msg[:, :, M_MAX:MSG], in0=by_tile(mb_ps),
                                      in1=seg_last[:, :].unsqueeze(2).to_broadcast([P, TILES, HEADS]), op=ALU.mult)

                def message(g):
                    q, v, use = closes
                    a, n = GROUPS[g][0], len(GROUPS[g])
                    if g == 0:
                        dve.wait_ge(alpha_done, v)
                    dve.tensor_tensor(out=msg[:, a:a + n, 0:F].rearrange("p t (h f) -> p t h f", h=HEADS),
                                      in0=xl_g[:, q, a:a + n, 0:F].rearrange("p t (h f) -> p t h f", h=HEADS),
                                      in1=msg[:, a:a + n, M_ALPHA:M_ONE].unsqueeze(3).to_broadcast([P, n, HEADS, F // HEADS]),
                                      op=ALU.mult).then_inc(msg_done[g], 1)

                def new_max():
                    q, v, use = closes
                    dve.wait_ge(agg_done, v)
                    dve.tensor_scalar(some[:, :], agg_ps[:, M_ONE:M_MAX], 1.0, None, ALU.min).then_inc(merge_step, 1)
                    dve.wait_ge(merge_step, v * 4 - 3)
                    dve.tensor_scalar(none_pen[:, :], some[:, :], -1.0, BIG, ALU.add, ALU.mult).then_inc(merge_step, 1)
                    dve.wait_ge(merge_step, v * 4 - 2)
                    dve.tensor_scalar(chunk_max[:, :], agg_ps[:, M_MAX:MSG], none_pen[:, 0:1], None, ALU.add).then_inc(merge_step, 1)
                    dve.wait_ge(merge_step, v * 4 - 1)
                    dve.wait_ge(state_loaded[q], use * 16)
                    dve.tensor_tensor(out=st_new[:, q, 0:HEADS], in0=chunk_max[:, :], in1=st_old[:, q, 0:HEADS], op=ALU.max).then_inc(merge_step, 1)
                    dve.wait_ge(merge_step, v * 4)
                    dve.tensor_tensor(out=dmax[:, 0, :], in0=st_old[:, q, 0:HEADS], in1=st_new[:, q, 0:HEADS], op=ALU.subtract)
                    dve.tensor_tensor(out=dmax[:, 1, :], in0=chunk_max[:, :], in1=st_new[:, q, 0:HEADS], op=ALU.subtract).then_inc(dmax_done, 1)

                def new_state():
                    q, v, use = closes
                    dve.wait_ge(rescale_done, v)
                    for w, (row, f) in enumerate(((st_old[:, q, C_ACC:C_CNT], rescale[:, 0, :]), (agg_ps[:, 0:F + HEADS], rescale[:, 1, :]))):
                        dve.tensor_tensor(out=scaled[:, w, 0:F].rearrange("p (h f) -> p h f", h=HEADS),
                                          in0=row[:, 0:F].rearrange("p (h f) -> p h f", h=HEADS),
                                          in1=f.unsqueeze(2).to_broadcast([P, HEADS, F // HEADS]), op=ALU.mult)
                        last = dve.tensor_tensor(out=scaled[:, w, F:F + HEADS], in0=row[:, F:F + HEADS], in1=f, op=ALU.mult)
                    last.then_inc(scaled_done, 1)
                    if stage == 0:
                        dve.tensor_tensor(out=st_new[:, q, C_CNT:C_EA], in0=st_old[:, q, C_CNT:C_EA], in1=agg_ps[:, M_ONE:M_MAX], op=ALU.add)
                        dve.tensor_tensor(out=st_new[:, q, C_EA:ROW], in0=st_old[:, q, C_EA:ROW], in1=ea_ps, op=ALU.add)
                    dve.wait_ge(scaled_done, v)
                    dve.tensor_tensor(out=st_new[:, q, C_ACC:C_CNT], in0=scaled[:, 0, :], in1=scaled[:, 1, :], op=ALU.add).then_inc(item_done, 1)

                if opens:
                    onehotT(0)
                    onehotT(1)
                for g in range(NG):
                    if closes and g == 0:
                        runs()
                    if closes and g == 1:
                        carries()
                    if opens:
                        add_transforms(g)
                        if g:
                            add_linear(g - 1)
                    if closes and g == 2:
                        shift()
                    if opens:
                        relu_att(g)
                    if closes and g == 1:
                        maxima()
                    if closes and g == 6:
                        new_max()
                    if opens:
                        if g + 2 < NG:
                            onehotT(g + 2)
                        if g == 4:
                            flags()
                        sum_heads(g)
                    if closes:
                        for m in SUMS_AT.get(g, ()):
                            message(m)
                if opens:
                    add_linear(NG - 1)
                if closes:
                    new_state()

            for stage in range(LAYERS):
                if stage == 0:
                    rounds(dve, (0,), lambda at: loop_logits(0, at))
                else:
                    rounds(dve, (0, 2), node_step(stage))
                pipeline(dve, stage, pairs, last_pair, lambda opens, closes: edge_step(stage, opens, closes))

            dve.wait_ge(hid_bias, 1)
            dve.tensor_tensor(out=bn[:, 0, :], in0=PS[:, 4, 0:2], in1=cols1[:, 0, :], op=ALU.add).then_inc(hid_b, 1)

            def hidden_mean(at):
                r, q, use = at
                n = Chain(dve, h_step, r * H_STEPS)
                dve.wait_ge(n_norm, r + (1 + (LAYERS - 1) * ROUNDS))
                n.link(dve.tensor_tensor(out=n_in[q], in0=n_in[q], in1=over_blocks(g_b[:, :]), op=ALU.mult))
                n.link(dve.tensor_tensor(out=n_in[q], in0=n_in[q], in1=over_blocks(be_b[:, :]), op=ALU.add))
                dve.wait_ge(fx_loaded[q], use * 16)
                n.link(dve.scalar_tensor_tensor(n_h, n_in[q], 0.0, n_x[q], ALU.max, ALU.add))
                mean_of(n, n_h, h_c, h_mean)
                assert n.n == H_STEPS, n.n

            def x1_and_attributes(at):
                r, q, use = at
                n = Chain(dve, x1_step, r * X1_STEPS)
                variance_of(h_c, h_sq, r + 1, h_var)
                n.link(dve.tensor_scalar(n_cnt[:, 0, :], n_st[q][:, :, C_CNT], 1.0, None, ALU.max))
                n.link(dve.reciprocal(n_cnt[:, 1, :], n_cnt[:, 0, :]))
                dve.tensor_tensor(out=n_e[:, :, :], in0=n_st[q][:, :, C_EA:ROW], in1=over_features(n_cnt[:, 1, :], D_EDGE), op=ALU.mult)
                normalized(n, lambda j: n_in[q][:, j, :], n_h, h_c, h_std, r + 1)\
                    .then_inc(x1_ready, 1)
                assert n.n == X1_STEPS, n.n

            def last_step(ahead, behind):
                if ahead:
                    n = layer_mean(LAYERS - 1, ahead)
                if behind:
                    x1_and_attributes(behind)
                if ahead:
                    layer_norm(n, LAYERS - 1, ahead)
                    hidden_mean(ahead)

            rounds(dve, (0, 1), last_step)

            ch = Chain(dve, bn_step)
            dve.wait_ge(hid_done, ROUNDS)
            full = (ROUNDS - 1) * NROWS
            for h in range(2):
                dve.reduce_sum(bn_sum[:, h, 0:1], hid[h][:, 0:full], axis=AX.X)
                ch.link(dve.reduce_sum(bn_sum[:, h, 1:2], hid[h][:, full:].rearrange("p (j e) -> p j e", j=NB)[:, :, 0:LAST_P], axis=AX.XY))
            ch.link(dve.tensor_tensor(out=bn[:, 2, :], in0=bn_sum[:, :, 0], in1=bn_sum[:, :, 1], op=ALU.add))
            dve.tensor_scalar(bn[:, 1, :], bn[:, 2, :], -1.0 / N_NODES, None, ALU.mult).then_inc(mu_done, 1)
            dve.wait_ge(sq_done, 6)
            ch.link(dve.reduce_sum(bn[:, 2, :], bn_sum[:, :, 0:3], axis=AX.X))
            dve.tensor_scalar(bn[:, 3, :], bn[:, 2, :], 1.0 / N_NODES, EPS, ALU.mult, ALU.add).then_inc(bn_var, 1)
            dve.wait_ge(bn_std, 1)
            ch.link(dve.reciprocal(bn[:, 7, :], bn[:, 4, :]))
            ch.link(dve.tensor_tensor(out=bn[:, 5, :], in0=bn[:, 7, :], in1=cols1[:, 1, :], op=ALU.mult))
            ch.link(dve.tensor_tensor(out=bn[:, 2, :], in0=bn[:, 1, :], in1=bn[:, 5, :], op=ALU.mult))
            dve.tensor_tensor(out=bn[:, 6, :], in0=bn[:, 2, :], in1=cols1[:, 2, :], op=ALU.add).then_inc(bn_done, 1)

            def out_step(ahead, behind):
                if behind:
                    r, q, use = behind
                    n = Chain(dve, o_norm, r)
                    variance_of(o_c[:, q, :, :], o_sq, r + 1, o_var)
                    dve.wait_ge(out_stored[q], use * 16)
                    normalized(n, lambda j: o_out[q][:, j, :], o_y[q], o_c[:, q, :, :], o_std, r + 1).then_inc(out_made, 1)
                    dve.wait_ge(out_made, r + 1)
                if ahead:
                    r, q, use = ahead
                    n = Chain(dve, o_step, r * O_STEPS)
                    dve.wait_ge(out_mm, r + 1)
                    n.link(dve.tensor_tensor(out=o_y[q], in0=out_ps[q].rearrange("p (j f) -> p j f", j=NB),
                                             in1=x1[:, bass.ds(r * NB, NB), :], op=ALU.add))
                    mean_of(n, o_y[q], o_c[:, q, :, :], o_mean)
                    assert n.n == O_STEPS, n.n

            rounds(dve, (0, 1), out_step)


_LAYER = {"Wl": "W{}l", "bl": "b{}l", "Wr": "W{}r", "br": "b{}r", "att": "a{}", "c": "c{}", "g": "g{}", "be": "be{}"}
_LAST = ("u", "W1", "b1", "gamma", "beta", "W2", "b2")


def kernel(**inputs):
    import numpy as np
    import concourse.bacc as bacc
    from concourse.bass_utils import run_bass_kernel_spmd

    nc = bacc.Bacc("TRN2", target_bir_lowering=False, num_devices=1)
    arrays = {}

    def given(name, a):
        arrays[name] = np.ascontiguousarray(a)
        return nc.dram_tensor(name, a.shape, mybir.dt.from_np(a.dtype), kind="ExternalInput").ap()

    def padded(a, rows, value):
        a = np.asarray(a)
        return np.concatenate([a, np.full((rows - a.shape[0],) + a.shape[1:], value, a.dtype)])

    def by_partition(flat):
        return flat.reshape((N_CHUNKS, TILES, P) + flat.shape[1:]).swapaxes(1, 2)

    dst = padded(inputs["dst"], E_PAD + 1, NO_NODE)
    args = {
        "x": given("x", padded(inputs["x"], N_PAD, 0)),
        "src_t": given("src_t", by_partition(padded(inputs["src"], E_PAD, 0))),
        "dst_t": given("dst_t", by_partition(dst[0:E_PAD])),
        "next_t": given("next_t", by_partition(dst[1:E_PAD + 1])),
        "dst": given("dst", dst[0:E_PAD].reshape(N_CHUNKS, TILES, P)),
        "edge_attr": given("edge_attr", by_partition(padded(inputs["edge_attr_96"], E_PAD, 0)).reshape(N_CHUNKS, P, TILES * D_EDGE)),
        "node_id": given("node_id", np.arange(N_PAD, dtype=np.float32)),
    }
    for key, name in _LAYER.items():
        args[key] = [given(f"{key}{l}", np.asarray(inputs["L0_gnn_" + name.format(l + 1)])) for l in range(LAYERS)]
    for key in _LAST:
        args[key] = given("last_" + key, np.asarray(inputs["L1_gnn_" + key]))
    args["out"] = nc.dram_tensor("out", (N_NODES, F), F32, kind="ExternalOutput").ap()
    gnn_program(nc, **args)
    r = run_bass_kernel_spmd(nc, [arrays], core_ids=[0])
    return r.results[0]["out"]
```
